# Optimizing a Trainium2 kernel written in Bass

```python
import numpy as np
import jax
import jax.numpy as jnp

def _softmax(x, axis=-1):
    return jax.nn.softmax(x, axis=axis)

def _gelu(x):
    return jax.nn.gelu(x, approximate=True)

def _silu(x):
    return jax.nn.silu(x)

def _sigmoid(x):
    return jax.nn.sigmoid(x)

def _layernorm(x, axis=-1, eps=1e-05):
    m = jnp.mean(x, axis=axis, keepdims=True)
    v = jnp.var(x, axis=axis, keepdims=True)
    return (x - m) / jnp.sqrt(v + eps)

def _scatter_add(tgt, idx, src, axis=0):
    return tgt.at[idx].add(src)

def _segment_sum(src, seg, n):
    return jax.ops.segment_sum(src, seg, n)
kernel_name = 'mk_cond_seq_d4_seqx_r4_b51625'

def setup_inputs(seed: int=0):
    np.random.seed(seed)
    _w = jnp.asarray

    def _rec_inputs():
        import jax
        import jax.numpy as jnp
        _rk = jax.random.key(seed)
        x = -0.0002928 + 1 * jax.random.normal(jax.random.fold_in(_rk, 1), (32, 256, 256), jnp.float32)
        _lenS = 256 - jax.random.randint(jax.random.fold_in(_rk, 7), (32,), 0, max(1, 256 // 4) + 1, jnp.int32)
        _lenS2 = 256 - jax.random.randint(jax.random.fold_in(_rk, 8), (32,), 0, max(1, 256 // 4) + 1, jnp.int32)
        cond_2048 = 0.00782532 + 1.00527 * jax.random.normal(jax.random.fold_in(_rk, 11), (32, 512), jnp.float32)
        itok_S_0_1023 = jax.random.randint(jax.random.fold_in(_rk, 12), (256,), 0, 256, jnp.int32)
        _validS = jnp.arange(256)[None, :] < _lenS[:, None]
        _validS2 = jnp.arange(256)[None, :] < _lenS2[:, None]
        _causal = jnp.tril(jnp.ones((256, 256), dtype=bool))
        mask_BxS_ff1 = jnp.where(jnp.ones((32, 256), dtype=bool), 1.0, 0.0).astype(jnp.float32)
        mask_BxS_ik0 = jnp.where(jnp.broadcast_to(_validS[:, :], (32, 256)), 0, 1).astype(jnp.int32)
        return (x, cond_2048, itok_S_0_1023, mask_BxS_ff1, mask_BxS_ik0)
    x, cond_2048, itok_S_0_1023, mask_BxS_ff1, mask_BxS_ik0 = _rec_inputs()

    def _L0_cond_setup():
        import jax, jax.numpy as jnp
        import numpy as np
        B_SZ, S, D = (4, 256, 256)
        DI, DS, DTR, DC = (512, 16, 64, 4)
        EPS = 1e-05

        def _layernorm(x, g, b):
            m = jnp.mean(x, axis=-1, keepdims=True)
            v = jnp.var(x, axis=-1, keepdims=True)
            return (x - m) * jax.lax.rsqrt(v + EPS) * g + b

        def _mamba(h, W_in, conv_w, conv_b, W_xp, W_dt, b_dt, A_log, D_param, W_out):
            bsz = h.shape[0]
            xz = h @ W_in
            xm, z = jnp.split(xz, 2, axis=-1)
            xc = jnp.transpose(xm, (0, 2, 1))
            xc = jax.lax.conv_general_dilated(xc, conv_w, (1,), [(DC - 1, 0)], feature_group_count=DI, dimension_numbers=('NCH', 'OIH', 'NCH'))
            xc = xc + conv_b[None, :, None]
            xm = jax.nn.silu(jnp.transpose(xc, (0, 2, 1)))
            xdbl = xm @ W_xp
            dtr, Bm, Cm = jnp.split(xdbl, [DTR, DTR + DS], axis=-1)
            dt = jax.nn.softplus(dtr @ W_dt + b_dt)
            A = -jnp.exp(A_log)

            def step(hst, inp):
                dt_t, B_t, C_t, x_t = inp
                dA = jnp.exp(dt_t[:, :, None] * A)
                hst = hst * dA + (dt_t * x_t)[:, :, None] * B_t[:, None, :]
                y = jnp.einsum('bds,bs->bd', hst, C_t)
                return (hst, y)
            inputs = (jnp.transpose(dt, (1, 0, 2)), jnp.transpose(Bm, (1, 0, 2)), jnp.transpose(Cm, (1, 0, 2)), jnp.transpose(xm, (1, 0, 2)))
            h0 = jnp.zeros((bsz, DI, DS), dt.dtype)
            _, ys = jax.lax.scan(step, h0, inputs)
            y = jnp.transpose(ys, (1, 0, 2)) + xm * D_param
            y = y * jax.nn.silu(z)
            return y @ W_out
        key = jax.random.key(seed)
        ks = jax.random.split(key, 12)

        def w(k, shape, scale=0.02):
            return jax.random.normal(k, shape, jnp.float32) * scale
        x = jax.random.normal(ks[0], (B_SZ, S, D), jnp.float32)
        c = jax.random.normal(ks[1], (B_SZ, 2 * D), jnp.float32)
        W_ada = w(ks[2], (2 * D, 3 * D))
        b_ada = jnp.zeros((3 * D,), jnp.float32)
        gamma = jnp.ones((D,), jnp.float32)
        beta = jnp.zeros((D,), jnp.float32)
        W_in = w(ks[3], (D, 2 * DI))
        conv_w = w(ks[4], (DI, 1, DC), 0.1)
        conv_b = jnp.zeros((DI,), jnp.float32)
        W_xp = w(ks[5], (DI, DTR + 2 * DS))
        W_dt = w(ks[6], (DTR, DI))
        b_dt = jnp.full((DI,), jnp.log(jnp.expm1(jnp.float32(0.01))), jnp.float32)
        A_log = jnp.log(jnp.broadcast_to(jnp.arange(1, DS + 1, dtype=jnp.float32), (DI, DS)))
        D_param = jnp.ones((DI,), jnp.float32)
        W_out = w(ks[7], (DI, D))
        perm = jax.random.permutation(ks[8], S)
        inv_perm = jnp.argsort(perm)
        return dict(x=x, c=c, W_ada=W_ada, b_ada=b_ada, gamma=gamma, beta=beta, W_in=W_in, conv_w=conv_w, conv_b=conv_b, W_xp=W_xp, W_dt=W_dt, b_dt=b_dt, A_log=A_log, D_param=D_param, W_out=W_out, perm=perm, inv_perm=inv_perm)
    _L0_cond_all = _L0_cond_setup()
    _L0_cond_in = {k: v for k, v in _L0_cond_all.items() if k in ('W_ada', 'b_ada', 'gamma', 'beta', 'W_in', 'conv_w', 'conv_b', 'W_xp', 'W_dt', 'b_dt', 'A_log', 'D_param', 'W_out')}
    del _L0_cond_all

    def _L1_cond_setup():
        import jax, jax.numpy as jnp
        import numpy as np
        B, T, D, H, TE = (8, 256, 256, 16, 512)
        LN_EPS = 1e-05

        def layer_norm(x, w, b):
            m = jnp.mean(x, axis=-1, keepdims=True)
            v = jnp.var(x, axis=-1, keepdims=True)
            return (x - m) / jnp.sqrt(v + LN_EPS) * w + b
        key = jax.random.key(seed)
        ks = jax.random.split(key, 8)
        s = lambda k, sh: jax.random.normal(k, sh, jnp.float32) * 0.02
        return dict(x=jax.random.normal(ks[0], (B, T, D), jnp.float32), emb=jax.random.normal(ks[1], (B, TE), jnp.float32), src_mask=jnp.ones((B, T), jnp.float32), norm_w=jnp.ones((D,), jnp.float32), norm_b=jnp.zeros((D,), jnp.float32), q_w=s(ks[2], (D, D)), q_b=jnp.zeros((D,), jnp.float32), k_w=s(ks[3], (D, D)), k_b=jnp.zeros((D,), jnp.float32), v_w=s(ks[4], (D, D)), v_b=jnp.zeros((D,), jnp.float32), emb_w=s(ks[5], (TE, 2 * D)), emb_b=jnp.zeros((2 * D,), jnp.float32), sb_norm_w=jnp.ones((D,), jnp.float32), sb_norm_b=jnp.zeros((D,), jnp.float32), out_w=s(ks[6], (D, D)), out_b=jnp.zeros((D,), jnp.float32))
    _L1_cond_all = _L1_cond_setup()
    _L1_cond_in = {k: v for k, v in _L1_cond_all.items() if k in ('norm_w', 'norm_b', 'q_w', 'q_b', 'k_w', 'k_b', 'v_w', 'v_b', 'emb_w', 'emb_b', 'sb_norm_w', 'sb_norm_b', 'out_w', 'out_b')}
    del _L1_cond_all

    def _L2_cond_setup():
        import jax, jax.numpy as jnp
        import numpy as np
        D = 256
        DI = 512
        N = 16
        DT_RANK = 64
        D_CONV = 4
        EPS = 1e-05

        def _layernorm(x, g, b):
            mu = jnp.mean(x, axis=-1, keepdims=True)
            var = jnp.mean((x - mu) ** 2, axis=-1, keepdims=True)
            return (x - mu) * jax.lax.rsqrt(var + EPS) * g + b

        def _mamba(xn, in_proj_w, conv_w, conv_b, x_proj_w, dt_proj_w, dt_proj_b, A_log, D_param, out_proj_w):
            b, sl, _ = xn.shape
            xz = jnp.einsum('bsd,ed->bse', xn, in_proj_w)
            x_in, z = jnp.split(xz, 2, axis=-1)
            xt = jnp.transpose(x_in, (0, 2, 1))
            u = jax.lax.conv_general_dilated(xt, conv_w[:, None, :], (1,), [(D_CONV - 1, 0)], feature_group_count=DI, dimension_numbers=('NCH', 'OIH', 'NCH')) + conv_b[None, :, None]
            u = jax.nn.silu(jnp.transpose(u, (0, 2, 1)))
            x_dbl = jnp.einsum('bsd,ed->bse', u, x_proj_w)
            dt_r, B, C = jnp.split(x_dbl, [DT_RANK, DT_RANK + N], axis=-1)
            dt = jax.nn.softplus(jnp.einsum('bsr,dr->bsd', dt_r, dt_proj_w) + dt_proj_b)
            A = -jnp.exp(A_log)

            def step(h, inp):
                dt_t, B_t, C_t, u_t = inp
                dA = jnp.exp(dt_t[:, :, None] * A)
                h = h * dA + (dt_t * u_t)[:, :, None] * B_t[:, None, :]
                y = jnp.einsum('bdn,bn->bd', h, C_t)
                return (h, y)
            seq = (jnp.transpose(dt, (1, 0, 2)), jnp.transpose(B, (1, 0, 2)), jnp.transpose(C, (1, 0, 2)), jnp.transpose(u, (1, 0, 2)))
            h0 = jnp.zeros((b, DI, N), xn.dtype)
            _, ys = jax.lax.scan(step, h0, seq)
            y = jnp.transpose(ys, (1, 0, 2)) + u * D_param
            y = y * jax.nn.silu(z)
            return jnp.einsum('bsd,ed->bse', y, out_proj_w)
        key = jax.random.key(seed)
        ks = jax.random.split(key, 16)
        s = lambda fan: 1.0 / np.sqrt(fan)
        inp = {'x': jax.random.normal(ks[0], (2, 512, D), jnp.float32), 'c': jax.random.normal(ks[1], (2, 2 * D), jnp.float32), 'ln_g': jnp.ones((D,), jnp.float32), 'ln_b': jnp.zeros((D,), jnp.float32), 'ada_w': jax.random.normal(ks[2], (3 * D, 2 * D), jnp.float32) * s(2 * D), 'ada_b': jnp.zeros((3 * D,), jnp.float32), 'in_proj_w': jax.random.normal(ks[3], (2 * DI, D), jnp.float32) * s(D), 'conv_w': jax.random.normal(ks[4], (DI, D_CONV), jnp.float32) * s(D_CONV), 'conv_b': jnp.zeros((DI,), jnp.float32), 'x_proj_w': jax.random.normal(ks[5], (DT_RANK + 2 * N, DI), jnp.float32) * s(DI), 'dt_proj_w': jax.random.normal(ks[6], (DI, DT_RANK), jnp.float32) * s(DT_RANK), 'dt_proj_b': jax.random.uniform(ks[7], (DI,), jnp.float32, -4.0, -2.0), 'A_log': jnp.tile(jnp.log(jnp.arange(1, N + 1, dtype=jnp.float32)), (DI, 1)), 'D_param': jnp.ones((DI,), jnp.float32), 'out_proj_w': jax.random.normal(ks[8], (D, DI), jnp.float32) * s(DI)}
        return inp
    _L2_cond_all = _L2_cond_setup()
    _L2_cond_in = {k: v for k, v in _L2_cond_all.items() if k in ('ln_g', 'ln_b', 'ada_w', 'ada_b', 'in_proj_w', 'conv_w', 'conv_b', 'x_proj_w', 'dt_proj_w', 'dt_proj_b', 'A_log', 'D_param', 'out_proj_w')}
    del _L2_cond_all

    def _L3_cond_setup():
        import jax, jax.numpy as jnp
        import numpy as np
        H = 16
        LN_EPS = 1e-05

        def _layernorm(x, scale, bias):
            mu = jnp.mean(x, axis=-1, keepdims=True)
            var = jnp.var(x, axis=-1, keepdims=True)
            return (x - mu) * jax.lax.rsqrt(var + LN_EPS) * scale + bias
        key = jax.random.key(seed)
        ks = jax.random.split(key, 8)
        B, T, D, E = (4, 1024, 256, 512)
        s = 0.02
        return {'x': jax.random.normal(ks[0], (B, T, D), jnp.float32), 'emb': jax.random.normal(ks[1], (B, E), jnp.float32), 'src_mask': jax.random.randint(ks[2], (B, T), 0, 2).astype(jnp.int32), 'norm_scale': jnp.ones((D,), jnp.float32), 'norm_bias': jnp.zeros((D,), jnp.float32), 'Wq': jax.random.normal(ks[3], (D, D), jnp.float32) * s, 'bq': jnp.zeros((D,), jnp.float32), 'Wk': jax.random.normal(ks[4], (D, D), jnp.float32) * s, 'bk': jnp.zeros((D,), jnp.float32), 'Wv': jax.random.normal(ks[5], (D, D), jnp.float32) * s, 'bv': jnp.zeros((D,), jnp.float32), 'film_emb_W': jax.random.normal(ks[6], (E, 2 * D), jnp.float32) * s, 'film_emb_b': jnp.zeros((2 * D,), jnp.float32), 'film_norm_scale': jnp.ones((D,), jnp.float32), 'film_norm_bias': jnp.zeros((D,), jnp.float32), 'film_out_W': jax.random.normal(ks[7], (D, D), jnp.float32) * s, 'film_out_b': jnp.zeros((D,), jnp.float32)}
    _L3_cond_all = _L3_cond_setup()
    _L3_cond_in = {k: v for k, v in _L3_cond_all.items() if k in ('norm_scale', 'norm_bias', 'Wq', 'bq', 'Wk', 'bk', 'Wv', 'bv', 'film_emb_W', 'film_emb_b', 'film_norm_scale', 'film_norm_bias', 'film_out_W', 'film_out_b')}
    del _L3_cond_all
    return {'x': x, 'cond_2048': cond_2048, 'itok_S_0_1023': itok_S_0_1023, 'mask_BxS_ff1': mask_BxS_ff1, 'mask_BxS_ik0': mask_BxS_ik0, 'L0_cond_W_ada': _L0_cond_in['W_ada'], 'L0_cond_b_ada': _L0_cond_in['b_ada'], 'L0_cond_gamma': _L0_cond_in['gamma'], 'L0_cond_beta': _L0_cond_in['beta'], 'L0_cond_W_in': _L0_cond_in['W_in'], 'L0_cond_conv_w': _L0_cond_in['conv_w'], 'L0_cond_conv_b': _L0_cond_in['conv_b'], 'L0_cond_W_xp': _L0_cond_in['W_xp'], 'L0_cond_W_dt': _L0_cond_in['W_dt'], 'L0_cond_b_dt': _L0_cond_in['b_dt'], 'L0_cond_A_log': _L0_cond_in['A_log'], 'L0_cond_D_param': _L0_cond_in['D_param'], 'L0_cond_W_out': _L0_cond_in['W_out'], 'L1_cond_norm_w': _L1_cond_in['norm_w'], 'L1_cond_norm_b': _L1_cond_in['norm_b'], 'L1_cond_q_w': _L1_cond_in['q_w'], 'L1_cond_q_b': _L1_cond_in['q_b'], 'L1_cond_k_w': _L1_cond_in['k_w'], 'L1_cond_k_b': _L1_cond_in['k_b'], 'L1_cond_v_w': _L1_cond_in['v_w'], 'L1_cond_v_b': _L1_cond_in['v_b'], 'L1_cond_emb_w': _L1_cond_in['emb_w'], 'L1_cond_emb_b': _L1_cond_in['emb_b'], 'L1_cond_sb_norm_w': _L1_cond_in['sb_norm_w'], 'L1_cond_sb_norm_b': _L1_cond_in['sb_norm_b'], 'L1_cond_out_w': _L1_cond_in['out_w'], 'L1_cond_out_b': _L1_cond_in['out_b'], 'L2_cond_ln_g': _L2_cond_in['ln_g'], 'L2_cond_ln_b': _L2_cond_in['ln_b'], 'L2_cond_ada_w': _L2_cond_in['ada_w'], 'L2_cond_ada_b': _L2_cond_in['ada_b'], 'L2_cond_in_proj_w': _L2_cond_in['in_proj_w'], 'L2_cond_conv_w': _L2_cond_in['conv_w'], 'L2_cond_conv_b': _L2_cond_in['conv_b'], 'L2_cond_x_proj_w': _L2_cond_in['x_proj_w'], 'L2_cond_dt_proj_w': _L2_cond_in['dt_proj_w'], 'L2_cond_dt_proj_b': _L2_cond_in['dt_proj_b'], 'L2_cond_A_log': _L2_cond_in['A_log'], 'L2_cond_D_param': _L2_cond_in['D_param'], 'L2_cond_out_proj_w': _L2_cond_in['out_proj_w'], 'L3_cond_norm_scale': _L3_cond_in['norm_scale'], 'L3_cond_norm_bias': _L3_cond_in['norm_bias'], 'L3_cond_Wq': _L3_cond_in['Wq'], 'L3_cond_bq': _L3_cond_in['bq'], 'L3_cond_Wk': _L3_cond_in['Wk'], 'L3_cond_bk': _L3_cond_in['bk'], 'L3_cond_Wv': _L3_cond_in['Wv'], 'L3_cond_bv': _L3_cond_in['bv'], 'L3_cond_film_emb_W': _L3_cond_in['film_emb_W'], 'L3_cond_film_emb_b': _L3_cond_in['film_emb_b'], 'L3_cond_film_norm_scale': _L3_cond_in['film_norm_scale'], 'L3_cond_film_norm_bias': _L3_cond_in['film_norm_bias'], 'L3_cond_film_out_W': _L3_cond_in['film_out_W'], 'L3_cond_film_out_b': _L3_cond_in['film_out_b']}

def reference(x, cond_2048, itok_S_0_1023, mask_BxS_ff1, mask_BxS_ik0, L0_cond_W_ada, L0_cond_b_ada, L0_cond_gamma, L0_cond_beta, L0_cond_W_in, L0_cond_conv_w, L0_cond_conv_b, L0_cond_W_xp, L0_cond_W_dt, L0_cond_b_dt, L0_cond_A_log, L0_cond_D_param, L0_cond_W_out, L1_cond_norm_w, L1_cond_norm_b, L1_cond_q_w, L1_cond_q_b, L1_cond_k_w, L1_cond_k_b, L1_cond_v_w, L1_cond_v_b, L1_cond_emb_w, L1_cond_emb_b, L1_cond_sb_norm_w, L1_cond_sb_norm_b, L1_cond_out_w, L1_cond_out_b, L2_cond_ln_g, L2_cond_ln_b, L2_cond_ada_w, L2_cond_ada_b, L2_cond_in_proj_w, L2_cond_conv_w, L2_cond_conv_b, L2_cond_x_proj_w, L2_cond_dt_proj_w, L2_cond_dt_proj_b, L2_cond_A_log, L2_cond_D_param, L2_cond_out_proj_w, L3_cond_norm_scale, L3_cond_norm_bias, L3_cond_Wq, L3_cond_bq, L3_cond_Wk, L3_cond_bk, L3_cond_Wv, L3_cond_bv, L3_cond_film_emb_W, L3_cond_film_emb_b, L3_cond_film_norm_scale, L3_cond_film_norm_bias, L3_cond_film_out_W, L3_cond_film_out_b):
    import jax
    import jax.numpy as jnp

    def _L0_cond_ref(x, c, W_ada, b_ada, gamma, beta, W_in, conv_w, conv_b, W_xp, W_dt, b_dt, A_log, D_param, W_out, perm, inv_perm):
        import jax, jax.numpy as jnp
        import numpy as np
        B_SZ, S, D = (4, 256, 256)
        DI, DS, DTR, DC = (512, 16, 64, 4)
        EPS = 1e-05

        def _layernorm(x, g, b):
            m = jnp.mean(x, axis=-1, keepdims=True)
            v = jnp.var(x, axis=-1, keepdims=True)
            return (x - m) * jax.lax.rsqrt(v + EPS) * g + b

        def _mamba(h, W_in, conv_w, conv_b, W_xp, W_dt, b_dt, A_log, D_param, W_out):
            bsz = h.shape[0]
            xz = h @ W_in
            xm, z = jnp.split(xz, 2, axis=-1)
            xc = jnp.transpose(xm, (0, 2, 1))
            xc = jax.lax.conv_general_dilated(xc, conv_w, (1,), [(DC - 1, 0)], feature_group_count=DI, dimension_numbers=('NCH', 'OIH', 'NCH'))
            xc = xc + conv_b[None, :, None]
            xm = jax.nn.silu(jnp.transpose(xc, (0, 2, 1)))
            xdbl = xm @ W_xp
            dtr, Bm, Cm = jnp.split(xdbl, [DTR, DTR + DS], axis=-1)
            dt = jax.nn.softplus(dtr @ W_dt + b_dt)
            A = -jnp.exp(A_log)

            def step(hst, inp):
                dt_t, B_t, C_t, x_t = inp
                dA = jnp.exp(dt_t[:, :, None] * A)
                hst = hst * dA + (dt_t * x_t)[:, :, None] * B_t[:, None, :]
                y = jnp.einsum('bds,bs->bd', hst, C_t)
                return (hst, y)
            inputs = (jnp.transpose(dt, (1, 0, 2)), jnp.transpose(Bm, (1, 0, 2)), jnp.transpose(Cm, (1, 0, 2)), jnp.transpose(xm, (1, 0, 2)))
            h0 = jnp.zeros((bsz, DI, DS), dt.dtype)
            _, ys = jax.lax.scan(step, h0, inputs)
            y = jnp.transpose(ys, (1, 0, 2)) + xm * D_param
            y = y * jax.nn.silu(z)
            return y @ W_out
        mod = jax.nn.silu(c) @ W_ada + b_ada
        shift, scale, gate = jnp.split(mod, 3, axis=1)
        h = _layernorm(x, gamma, beta)
        h = h * (1.0 + scale[:, None, :]) + shift[:, None, :]
        h = h[:, perm]
        y = _mamba(h, W_in, conv_w, conv_b, W_xp, W_dt, b_dt, A_log, D_param, W_out)
        y = y[:, inv_perm]
        return x + gate[:, None, :] * y

    def _L1_cond_ref(x, emb, src_mask, norm_w, norm_b, q_w, q_b, k_w, k_b, v_w, v_b, emb_w, emb_b, sb_norm_w, sb_norm_b, out_w, out_b):
        import jax, jax.numpy as jnp
        import numpy as np
        B, T, D, H, TE = (8, 256, 256, 16, 512)
        LN_EPS = 1e-05

        def layer_norm(x, w, b):
            m = jnp.mean(x, axis=-1, keepdims=True)
            v = jnp.var(x, axis=-1, keepdims=True)
            return (x - m) / jnp.sqrt(v + LN_EPS) * w + b
        Bx, Tx, Dx = x.shape
        xn = layer_norm(x, norm_w, norm_b)
        q = (xn @ q_w + q_b).reshape(Bx, Tx, H, -1)
        k = (xn @ k_w + k_b).reshape(Bx, Tx, H, -1)
        att = jnp.einsum('bnhl,bmhl->bnmh', q, k)
        mask = src_mask.reshape(Bx, 1, Tx, 1)
        att = att + (1.0 - mask) * -1000000.0
        att = jax.nn.softmax(att, axis=2)
        v = ((xn @ v_w + v_b) * src_mask[:, :, None]).reshape(Bx, Tx, H, -1)
        y = jnp.einsum('bnmh,bmhl->bnhl', att, v).reshape(Bx, Tx, Dx)
        e = jax.nn.silu(emb) @ emb_w + emb_b
        scale, shift = jnp.split(e[:, None, :], 2, axis=2)
        h = layer_norm(y, sb_norm_w, sb_norm_b) * (1.0 + scale) + shift
        h = jax.nn.silu(h) @ out_w + out_b
        return x + h

    def _L2_cond_ref(x, c, ln_g, ln_b, ada_w, ada_b, in_proj_w, conv_w, conv_b, x_proj_w, dt_proj_w, dt_proj_b, A_log, D_param, out_proj_w):
        import jax, jax.numpy as jnp
        import numpy as np
        D = 256
        DI = 512
        N = 16
        DT_RANK = 64
        D_CONV = 4
        EPS = 1e-05

        def _layernorm(x, g, b):
            mu = jnp.mean(x, axis=-1, keepdims=True)
            var = jnp.mean((x - mu) ** 2, axis=-1, keepdims=True)
            return (x - mu) * jax.lax.rsqrt(var + EPS) * g + b

        def _mamba(xn, in_proj_w, conv_w, conv_b, x_proj_w, dt_proj_w, dt_proj_b, A_log, D_param, out_proj_w):
            b, sl, _ = xn.shape
            xz = jnp.einsum('bsd,ed->bse', xn, in_proj_w)
            x_in, z = jnp.split(xz, 2, axis=-1)
            xt = jnp.transpose(x_in, (0, 2, 1))
            u = jax.lax.conv_general_dilated(xt, conv_w[:, None, :], (1,), [(D_CONV - 1, 0)], feature_group_count=DI, dimension_numbers=('NCH', 'OIH', 'NCH')) + conv_b[None, :, None]
            u = jax.nn.silu(jnp.transpose(u, (0, 2, 1)))
            x_dbl = jnp.einsum('bsd,ed->bse', u, x_proj_w)
            dt_r, B, C = jnp.split(x_dbl, [DT_RANK, DT_RANK + N], axis=-1)
            dt = jax.nn.softplus(jnp.einsum('bsr,dr->bsd', dt_r, dt_proj_w) + dt_proj_b)
            A = -jnp.exp(A_log)

            def step(h, inp):
                dt_t, B_t, C_t, u_t = inp
                dA = jnp.exp(dt_t[:, :, None] * A)
                h = h * dA + (dt_t * u_t)[:, :, None] * B_t[:, None, :]
                y = jnp.einsum('bdn,bn->bd', h, C_t)
                return (h, y)
            seq = (jnp.transpose(dt, (1, 0, 2)), jnp.transpose(B, (1, 0, 2)), jnp.transpose(C, (1, 0, 2)), jnp.transpose(u, (1, 0, 2)))
            h0 = jnp.zeros((b, DI, N), xn.dtype)
            _, ys = jax.lax.scan(step, h0, seq)
            y = jnp.transpose(ys, (1, 0, 2)) + u * D_param
            y = y * jax.nn.silu(z)
            return jnp.einsum('bsd,ed->bse', y, out_proj_w)
        ada = jnp.einsum('bc,ec->be', jax.nn.silu(c), ada_w) + ada_b
        shift, scale, gate = jnp.split(ada, 3, axis=1)
        xn = _layernorm(x, ln_g, ln_b)
        xn = xn * (1.0 + scale[:, None, :]) + shift[:, None, :]
        x_ssm = _mamba(xn, in_proj_w, conv_w, conv_b, x_proj_w, dt_proj_w, dt_proj_b, A_log, D_param, out_proj_w)
        return x + gate[:, None, :] * x_ssm

    def _L3_cond_ref(x, emb, src_mask, norm_scale, norm_bias, Wq, bq, Wk, bk, Wv, bv, film_emb_W, film_emb_b, film_norm_scale, film_norm_bias, film_out_W, film_out_b):
        import jax, jax.numpy as jnp
        import numpy as np
        H = 16
        LN_EPS = 1e-05

        def _layernorm(x, scale, bias):
            mu = jnp.mean(x, axis=-1, keepdims=True)
            var = jnp.var(x, axis=-1, keepdims=True)
            return (x - mu) * jax.lax.rsqrt(var + LN_EPS) * scale + bias
        B, T, D = x.shape
        dh = D // H
        xn = _layernorm(x, norm_scale, norm_bias)
        q = xn @ Wq + bq
        k = xn @ Wk + bk
        v = xn @ Wv + bv
        mask = (src_mask == 1)[:, :, None]
        k = jnp.where(mask, -jnp.inf, k)
        v = jnp.where(mask, 0.0, v)
        q = q.reshape(B, T, H, dh).transpose(0, 2, 1, 3)
        k = k.reshape(B, T, H, dh).transpose(0, 2, 1, 3)
        v = v.reshape(B, T, H, dh).transpose(0, 2, 1, 3)
        q = jax.nn.softmax(q, axis=-1)
        k = jax.nn.softmax(k, axis=2)
        attn = jnp.einsum('bhse,bhsd->bhed', k, v)
        y = jnp.einsum('bhtd,bhed->bhte', q, attn)
        y = y.transpose(0, 2, 1, 3).reshape(B, T, D)
        emb_out = jax.nn.silu(emb) @ film_emb_W + film_emb_b
        scale, shift = jnp.split(emb_out, 2, axis=-1)
        h = _layernorm(y, film_norm_scale, film_norm_bias) * (1.0 + scale[:, None, :]) + shift[:, None, :]
        h = jax.nn.silu(h) @ film_out_W + film_out_b
        return x + h
    x = _L0_cond_ref(x, cond_2048, L0_cond_W_ada, L0_cond_b_ada, L0_cond_gamma, L0_cond_beta, L0_cond_W_in, L0_cond_conv_w, L0_cond_conv_b, L0_cond_W_xp, L0_cond_W_dt, L0_cond_b_dt, L0_cond_A_log, L0_cond_D_param, L0_cond_W_out, itok_S_0_1023, itok_S_0_1023)
    x = _L1_cond_ref(x, cond_2048, mask_BxS_ff1, L1_cond_norm_w, L1_cond_norm_b, L1_cond_q_w, L1_cond_q_b, L1_cond_k_w, L1_cond_k_b, L1_cond_v_w, L1_cond_v_b, L1_cond_emb_w, L1_cond_emb_b, L1_cond_sb_norm_w, L1_cond_sb_norm_b, L1_cond_out_w, L1_cond_out_b)
    x = _L2_cond_ref(x, cond_2048, L2_cond_ln_g, L2_cond_ln_b, L2_cond_ada_w, L2_cond_ada_b, L2_cond_in_proj_w, L2_cond_conv_w, L2_cond_conv_b, L2_cond_x_proj_w, L2_cond_dt_proj_w, L2_cond_dt_proj_b, L2_cond_A_log, L2_cond_D_param, L2_cond_out_proj_w)
    x = _L3_cond_ref(x, cond_2048, mask_BxS_ik0, L3_cond_norm_scale, L3_cond_norm_bias, L3_cond_Wq, L3_cond_bq, L3_cond_Wk, L3_cond_bk, L3_cond_Wv, L3_cond_bv, L3_cond_film_emb_W, L3_cond_film_emb_b, L3_cond_film_norm_scale, L3_cond_film_norm_bias, L3_cond_film_out_W, L3_cond_film_out_b)
    return x

_drawn_inputs = setup_inputs


def setup_inputs(seed=0):
    import zlib

    import numpy as np

    out = dict(_drawn_inputs(seed))
    spreads = {'L0_cond_b_ada': (0.0, 0.1),
     'L0_cond_gamma': (1.0, 0.2),
     'L0_cond_beta': (0.0, 0.1),
     'L0_cond_conv_b': (0.0, 0.1),
     'L0_cond_b_dt': (-4.600166320800781, 0.2),
     'L0_cond_D_param': (1.0, 0.2),
     'L1_cond_norm_w': (1.0, 0.2),
     'L1_cond_norm_b': (0.0, 0.1),
     'L1_cond_q_b': (0.0, 0.1),
     'L1_cond_k_b': (0.0, 0.1),
     'L1_cond_v_b': (0.0, 0.1),
     'L1_cond_emb_b': (0.0, 0.1),
     'L1_cond_sb_norm_w': (1.0, 0.2),
     'L1_cond_sb_norm_b': (0.0, 0.1),
     'L1_cond_out_b': (0.0, 0.1),
     'L2_cond_ln_g': (1.0, 0.2),
     'L2_cond_ln_b': (0.0, 0.1),
     'L2_cond_ada_b': (0.0, 0.1),
     'L2_cond_conv_b': (0.0, 0.1),
     'L2_cond_D_param': (1.0, 0.2),
     'L3_cond_norm_scale': (1.0, 0.2),
     'L3_cond_norm_bias': (0.0, 0.1),
     'L3_cond_bq': (0.0, 0.1),
     'L3_cond_bk': (0.0, 0.1),
     'L3_cond_bv': (0.0, 0.1),
     'L3_cond_film_emb_b': (0.0, 0.1),
     'L3_cond_film_norm_scale': (1.0, 0.2),
     'L3_cond_film_norm_bias': (0.0, 0.1),
     'L3_cond_film_out_b': (0.0, 0.1)}
    factors = {}
    for name, (base, spread) in spreads.items():
        noise = np.random.default_rng([zlib.crc32(name.encode()), seed]).standard_normal(out[name].shape)
        drawn = base * np.exp(spread * noise) if base else spread * noise
        out[name] = jnp.asarray(drawn.astype(out[name].dtype))
    for name, factor in factors.items():
        out[name] = (out[name] * factor).astype(out[name].dtype)
    return out
```

```python
from contextlib import ExitStack

import numpy as np
import concourse.bass as bass
from concourse import mybir

F32 = mybir.dt.float32
F32R = mybir.dt.float32r
I32 = mybir.dt.int32
ALU = mybir.AluOpType
ACT = mybir.ActivationFunctionType
X = mybir.AxisListType.X

P = 128
B, S, D = 32, 256, 256
GB = 2
NG = B // GB
T = GB * S
R = T // P
RB = S // P
DC = D // P
DI = 512
IC = DI // P
NS = 16
TAPS = 4
DTR = 64
H, DH = 16, 16
EPS = 1e-5
STEPS = 2 * NS
RING = 4
AHEAD = 2
BC_RING = 3
PAIRS = H // 2
HP = PAIRS // 2
EXP_CAP = 1e18

COLS = {}


def _col(name, n):
    COLS[name] = (sum(w for _, w in COLS.values()), n)


for _l in ("m0", "m1"):
    for _n, _w in (("conv_w", IC * TAPS), ("conv_b", IC), ("b_dt", IC), ("D", IC), ("A_log", IC * NS),
                   ("ln_g", DC), ("ln_b", DC)):
        _col(f"{_l}_{_n}", _w)
for _n in ("a_norm_w", "a_norm_b", "a_q_b", "a_k_b", "a_sb_w", "a_sb_b",
           "l_norm_w", "l_norm_b", "l_k_b", "l_sb_w", "l_sb_b"):
    _col(_n, DC)
NCOL = sum(w for _, w in COLS.values())
ROWS = ["a_v_b", "a_out_b", "l_q_b", "l_v_b", "l_out_b"]
SITES = ["m0", "a", "m1", "l"]
MODW = 2560
SCALE_AT = {"m0": 256, "a": 768, "m1": 1280 + 256, "l": 2048}
SHIFT_AT = {"m0": 0, "a": 1024, "m1": 1280, "l": 2304}
GATE_AT = {"m0": 512, "m1": 1280 + 512}


class Piece:

    def __init__(self, sem, name, events, banks=()):
        self.name = name
        self.events = {e: list(v) for e, v in events.items() if v}
        self.sem = {e: sem(f"{name}_{e}") for e in self.events}
        self.where = {n: (e, k + 1) for e, v in self.events.items() for k, n in enumerate(v)}
        self.bank = dict(banks)
        self.made = {e: 0 for e in self.events}

    def of(self, name):
        return self.sem[self.where[name][0]]

    def upto(self, g, name):
        e, k = self.where[name]
        return g * len(self.events[e]) + k

    def next(self, name):
        e, _ = self.where[name]
        assert self.events[e][self.made[e] % len(self.events[e])] == name, (self.name, e, name)
        self.made[e] += 1
        return self.sem[e]


def front_piece(sem, name):
    pe = ["h0", "h1"] + [f"m{m}" for m in range(2 * IC)] + ["xp"] + [f"d{m}" for m in range(IC)]
    act = ["xc"] * (name == "front1") + ["hc0", "hc1"]
    for m in range(IC):
        act.append(f"tap{m}")
        if m:
            act.append(f"u{m - 1}")
    act += [f"u{IC - 1}"] + [f"z{m}" for m in range(IC)] + ["dtr", "bchi"]
    act += ["e0", "e1", "e2", "l0", "l1", "l2", "e3", "l3"]
    dve = ["st", "cur", "mv", "xh"] + [f"cv{m}_{s}" for m in range(IC) for s in (1, 2, 3)] + ["bclo"]
    dve += ["mn0", "mn1", "mn2", "dt0", "dt1", "dt2", "mn3", "dt3"]
    pool = ["var", "rstd"] + [f"dtx{m}" for m in range(IC)]
    uses = [("h0", 0), ("h1", 1)]
    uses += [(f"m{m}", (2 + m) % 3) for m in range(2 * IC)]
    uses += [("xp", 1)] + [(f"d{m}", (2 + m) % 3) for m in range(IC)]
    return Piece(sem, name, {"pe": pe, "act": act, "dve": dve, "pool": pool}, uses)


def back_piece(sem, name, gather):
    if gather:
        ev = {"pe": ["y0", "y1", "g0", "g1"], "act": ["yo0", "yo1"]}
        uses = [("y0", 0), ("y1", 1), ("g0", 2), ("g1", 0)]
    else:
        ev = {"pe": ["g0", "g1"]}
        uses = [("g0", 0), ("g1", 1)]
    return Piece(sem, name, ev | {"dve": ["mul0", "mul1", "x0", "x1"]}, uses)


def attn_piece(sem):
    pe, pool = ["h", "q", "k", "v"], ["var", "rstd", "var2", "rstd2"]
    act = ["hc", "qhi", "khi", "v_"]
    dve = ["st", "cur", "mcur", "mv", "mbias", "xh", "mval", "mhi", "mlo", "qlo", "klo"]
    uses = [("h", 0), ("q", 1), ("k", 2), ("v", 0)]
    for z in range(2):
        ps = range(z * HP, (z + 1) * HP)
        pe += [f"r{p}" for p in ps] + [f"s{p}{t}" for p in ps for t in range(2)] + [f"nm{z}"]
        act += [f"rc{p}" for p in ps if p % 2 == 0] + [f"nmhi{z}"]
        dve += [f"rc{p}" for p in ps if p % 2] + [f"mx{p}{t}" for p in ps for t in range(2)] + [f"nmlo{z}"]
        uses += [(f"r{p}", p % 3) for p in ps]
        uses += [(f"s{p}{t}", (2 * p + t) % 3) for p in ps for t in range(2)] + [(f"nm{z}", 0)]
        for p in range(z * HP, (z + 1) * HP + 1):
            if p < (z + 1) * HP:
                pe += [f"t{p}0", f"t{p}1"]
                act += [f"x{p}0", f"x{p}1"]
                uses += [(f"t{p}0", 0), (f"t{p}1", 1)]
                if p % 2:
                    uses += [(f"Y{p // 2}", 2)]
            if p > z * HP:
                pe.append(f"pv{p - 1}")
                if p % 2 == 0:
                    (act if p % 4 == 0 else dve).append(f"ye{p // 2 - 1}")
    pe += ["o0", "o1", "h2", "out"]
    dve += ["rec0", "yn0", "rec1", "yn1", "st2", "mv2", "xh2", "xo"]
    act += ["hc2"]
    uses += [("o0", 0), ("o1", 1), ("h2", 2), ("out", 0)]
    return Piece(sem, "attn", {"pe": pe, "act": act, "dve": dve, "pool": pool}, uses)


def linattn_piece(sem):
    pe = ["h", "q", "k", "v", "qt", "kt", "at", "y", "h2", "out"]
    act = ["hc", "qe", "v_", "ke0", "ke1", "qtc", "ktc", "hc2"]
    dve = ["st", "cur", "kcur", "mv", "kmask", "masked", "nmask", "xh", "qm", "qs", "kb0", "kb1", "km", "qsum", "qrec", "qn", "krec", "kn0", "kn1",
           "atm", "st2", "mv2", "xh2", "xo"]
    pool = ["var", "rstd", "var2", "rstd2"]
    uses = [("h", 0), ("q", 1), ("k", 2), ("v", 0), ("qt", 1),
            ("kt", 2), ("at", 0), ("y", 1), ("h2", 2), ("out", 0)]
    return Piece(sem, "linattn", {"pe": pe, "act": act, "dve": dve, "pool": pool}, uses)


def scan_piece(sem, name):
    pe, act, dve = ["bc0", "bc1", "bc2", "du0"], [f"exp{q}" for q in range(AHEAD)], []
    for s in range(STEPS):
        dve += [f"dbx{s}", f"scan{s}", f"hc{s}"]
        if s == NS + 1:
            dve += ["yg0", "yg1"]
        if s:
            pe += [f"bc{k}" for k in (2 * s + 1, 2 * s + 2) if k < 2 * STEPS]
            pe += ["du1"] * (s == NS + 3) + [f"red{(s - 3) // 2}"] * (s % 2 and s >= 3)
        if s + AHEAD < STEPS:
            act.append(f"exp{s + AHEAD}")
    return Piece(sem, name, {"pe": pe + [f"red{STEPS // 2 - 1}"], "act": act, "dve": dve + ["yg2", "yg3"],
                             "pool": [f"add{q}" for q in range(STEPS // 2)]})


FRONT_PH, BACK_PH, ATTN_PH, LIN_PH = 12, 2, 28, 9
WEIGHT = {"front0": [1] * FRONT_PH, "front1": [1] * FRONT_PH, "back0": [1] * BACK_PH, "back1": [1] * BACK_PH,
          "attn_a": [1] * ATTN_PH, "attn_b": [1] * ATTN_PH, "lin_a": [1] * LIN_PH, "lin_b": [1] * LIN_PH}
AT = {"spread_c": -0.6, "spread_b": 0.05, "reduce": 0.5, "last": 0, "decay": -0.3, "scan": 0.33,
      "times_c": 0.67, "gated": 0.5, "add": 1.0}
LAG = {"pe": 0.5, "act": 0.7, "dve": 0.9, "pool": 0.9}

R_FREE = ["v_", "qlo", "klo", "rc0", "x31", "ye1", "x30", "rc4"]
SIDE = [("back1", -2, 0), ("lin_a", -2, 0), ("attn_b", -1, 0), ("lin_b", -2, 0), ("front1", -1, 0),
        ("back0", 0, 1), ("attn_a", 0, 1), ("front0", 1, 1)]
SCAN = [("scan0", 0), ("scan1", -1)]
FIRST_IT, LAST_IT, LOOP_FROM, LOOP_TO = -1, NG + 1, 3, NG - 1


def alive(i, off):
    return not isinstance(i, int) or 0 <= i + off < NG


def before_side(i, at):
    while True:
        at -= 1
        if at < 0:
            at, i = len(SIDE) - 1, i - 1
        if isinstance(i, int) and i < FIRST_IT:
            return None
        if alive(i, SIDE[at][1]):
            return SIDE[at][0], i + SIDE[at][1]


def before_scan(i, at):
    while True:
        at -= 1
        if at < 0:
            at, i = 1, i - 1
        if isinstance(i, int) and i < FIRST_IT:
            return None
        if alive(i, SCAN[at][1]):
            return SCAN[at][0], i + SCAN[at][1]


def build(nc, a, out):
    ctx = ExitStack()
    with ctx:
        def sb(name, shape, dt=F32):
            return ctx.enter_context(nc.sbuf_tensor(name, shape, dt))

        def sem(name):
            return ctx.enter_context(nc.semaphore(name))

        w_in = [sb(f"w_in{l}", [P, DC, 2 * DI]) for l in range(2)]
        w_xp = [sb(f"w_xp{l}", [P, IC, DTR + 2 * NS]) for l in range(2)]
        w_dt = sb("w_dt", [2 * DTR, DI])
        w_out = [sb(f"w_out{l}", [P, IC, D]) for l in range(2)]
        w_att = {n: sb(f"w_{n}", [P, DC, D]) for n in ("a_q", "a_k", "a_v", "a_out", "l_q", "l_k", "l_v", "l_out")}
        cols = sb("cols", [P, NCOL])
        rows = sb("rows", [97, 2, D])
        ident = sb("ident", [P, P])
        pick = sb("pick", [P, 2 * NS], F32R)
        onehot = sb("onehot", [P, RB, S])
        stack = sb("stack", [P, 4, 4, P], F32R)
        blocks = sb("blocks", [P, P])
        diag_d = sb("diag_d", [P, 2, IC, P])
        a_neg = sb("a_neg", [P, 2, IC * NS])
        coef = sb("coef", [P, len(SITES) * 2 * DC, B])
        amask = sb("amask", [P, B, RB])
        kmask_col = sb("kmask_col", [P, B, RB], I32)
        ones = sb("ones", [P, P])
        one_col = sb("one_col", [P, 1])
        nhalf = sb("nhalf", [P, R])
        eps = sb("eps", [P, R])
        u = sb("u", [P, IC, T])
        dt_ = [sb(f"dt{l}", [P, IC, T]) for l in range(2)]
        dtx = [sb(f"dtx{l}", [P, IC, T]) for l in range(2)]
        sz = [sb(f"sz{l}", [P, IC, T]) for l in range(2)]
        bcr = [sb(f"bcr{l}", [P, T], F32R) for l in range(2)]
        da = [sb(f"da{k}", [P, 2, GB, S]) for k in range(AHEAD + 1)]
        hw = [sb(f"hw{k}", [P, 2, T]) for k in range(RING)]
        x_b = sb("x_b", [P, R, D])
        x_c = sb("x_c", [P, R, D])
        gate = sb("gate", [P, GB, D])
        xhat = sb("xhat", [P, R, D])
        hT = sb("hT", [P, DC, T])
        stats = sb("stats", [P, R, 6])
        mv = sb("mv", [P, R, 2])
        rstd = sb("rstd", [P, R])
        cur = sb("cur", [P, 2, DC, GB])
        xd = sb("xd", [2 * DTR, T])
        qhl = sb("qhl", [P, 2, DC, S], F32R)
        khl = sb("khl", [P, 2, DC, S], F32R)
        qk = sb("qk", [P, HP, 2, S], F32R)
        va = sb("va", [P, RB, H, 32])
        mx = sb("mx", [P, RB, H])
        nm = sb("nm", [P, S], F32R)
        mb = sb("mb", [P, S], F32R)
        mrow = sb("mrow", [1, S])
        mcur = sb("mcur", [P, 2, RB])
        pt2 = sb("pt2", [P, 2, T])
        pt = [(u if k < 2 else pt2)[:, k % 2, :].rearrange("p (h s) -> p h s", h=2) for k in range(4)]
        yT = sb("yT", [P, H // 4, S])
        rec = sb("rec", [P, 2, RB, H])
        kmrow = sb("kmrow", [P, S], I32)
        kT = yT[:, 0:2, :]
        kmb = yT[:, 2, :]
        qrow = pt[0]
        krow = pt[1]
        vrow = pt[2]
        qT = pt[3]
        attnT = hT[:, :, S:S + P]
        small = sb("small", [P, 8])
        qmx = rec[:, 0, :, :]
        qrs = rec[:, 1, :, :]

        ps = ctx.enter_context(nc.psum_tensor("ps", [P, 8, T], F32))
        yps = ps[:, 0:2, :]
        bc = [ps[:, 2 + k, :] for k in range(BC_RING)]
        side = [ps[:, 2 + BC_RING + k, :] for k in range(3)]

        gates_dram = nc.dram_tensor("gates_scratch", (2, B, D), F32, kind="Internal").ap()

        loaded = sem("loaded")
        gates_out = sem("gates_out")
        xin = sem("xin")
        xb_in = sem("residual_in")
        gin = [sem("gate0_in"), sem("gate1_in")]
        min_ = sem("mask_row_in")
        kmin = sem("key_mask_in")
        stored = sem("stored")
        p_pool, p_act, p_pe, p_dve = (sem(f"prologue_{e}") for e in ("pool", "act", "pe", "dve"))
        fr = [front_piece(sem, "front0"), front_piece(sem, "front1")]
        bk = [back_piece(sem, "back0", True), back_piece(sem, "back1", False)]
        at = attn_piece(sem)
        li = linattn_piece(sem)
        sc = [scan_piece(sem, "scan0"), scan_piece(sem, "scan1")]

        def flat(t, n):
            return t[:].rearrange("p a b -> p (a b)")[:, 0:n]

        w_mod = [dt_[0], dt_[1], dtx[0], dtx[1], sz[0]]
        mod_rows = hw[0]
        mod_rows2 = hw[1]
        mod_rows3 = hw[2]
        c_raw = x_b[:].rearrange("p a b -> p (a b)")[:, 0:4 * B].rearrange("p (k b) -> p k b", b=B)
        c_act = x_c[:].rearrange("p a b -> p (a b)")[:, 0:4 * B].rearrange("p (k b) -> p k b", b=B)
        mod_bias = [da[0][:].rearrange("p a b c -> p a (b c)"), da[1][:].rearrange("p a b c -> p a (b c)"),
                    da[2][:].rearrange("p a b c -> p a (b c)")]
        modT = sz[1][:].rearrange("p a b -> p (a b)")[:, 0:16 * B].rearrange("p (k b) -> p k b", b=B)
        idx_i = kmrow
        idx_f = yT[:, 0, :]
        iot_i = sb("iot_i", [P, RB], I32)
        iot_f = sb("iot_f", [P, RB])
        stack_f = xhat[:].rearrange("p a b -> p (a b)")
        stack_g = hT[:].rearrange("p a b -> p (a b)")
        pick_f = yT[:, 3, 0:2 * NS]

        def col(name, k=0, n=1):
            at0, _ = COLS[name]
            return cols[:, at0 + k:at0 + k + n]

        def rowb(name):
            r = ROWS.index(name)
            return ones[32 * (r % 4):32 * (r % 4) + 1, :], rows[32 * (r % 4):32 * (r % 4) + 1, r // 4, :]

        xv = a["x"].rearrange("b (k p) d -> p (b k) d", p=P)
        ov = out.rearrange("b (k p) d -> p (b k) d", p=P)
        x_src, x_res = [xhat, x_b], [x_b, x_c]
        busy = {}

        def number(name, g):
            return {"front0": (fr[0], g), "front1": (fr[1], g), "back0": (bk[0], g), "back1": (bk[1], g),
                    "attn_a": (at, 2 * g), "attn_b": (at, 2 * g + 1), "lin_a": (li, 2 * g),
                    "lin_b": (li, 2 * g + 1), "scan0": (sc[0], g), "scan1": (sc[1], g)}[name]

        def after(eng, prev, half_of_u=None):
            if prev is not None:
                kind, n = number(*prev)
                for e, v in kind.events.items():
                    eng.wait_ge(kind.sem[e], (n + 1) * len(v))
            if half_of_u is not None and busy["scan"] is not None:
                kind, n = number(*busy["scan"])
                eng.wait_ge(kind.of(f"du{half_of_u}"), kind.upto(n, f"du{half_of_u}"))

        def loads_of_piece(act, kind, v, g, prev):
            if prev is not None and prev[0] in ("lin_a", "lin_b"):
                store_result(act, prev[1], 0 if prev[0] == "lin_a" else 1)
            if kind == "front" and v == 0:
                act.dma_start(xhat[:, :, :], xv[:, bass.ds(g * R, R), :]).then_inc(xin, 16)
            if kind == "back":
                for b in range(GB):
                    act.dma_start(gate[:, b, :], gates_dram[v, bass.ds(g * GB + b, 1), :].broadcast_to([P, D]))\
                       .then_inc(gin[v], 16)
                if v == 0:
                    act.dma_start(x_b[:, :, :], xv[:, bass.ds(g * R, R), :]).then_inc(xb_in, 16)
            if kind == "attn":
                act.dma_start(mrow[:, :], a["amask_row"][bass.ds(2 * g + v, 1), :]).then_inc(min_, 16)
            if kind == "lin":
                act.dma_start(kmrow[:, :], a["kmask_row"][bass.ds(2 * g + v, 1), :].broadcast_to([P, S]))\
                   .then_inc(kmin, 16)

        def store_result(act, g, b):
            act.dma_start(ov[:, bass.ds((GB * g + b) * RB, RB), :], x_c[:, RB * b:RB * (b + 1), :])\
               .then_inc(stored, 16)

        def ln_stats(dve, pc, n, src, tiles, tag="", also=None):
            for r in range(tiles):
                ins = nc.vector.bn_stats(stats[:, r, :], src(r))
            ins.then_inc(pc.next("st" + tag), 1)
            if also is not None:
                also()
            dve.wait_ge(pc.of("st" + tag), pc.upto(n, "st" + tag))
            nc.vector.tensor_copy(small[:, 7:8], one_col[:, 0:1])
            for r in range(tiles):
                ins = nc.vector.bn_aggr(mv[:, r, :], stats[:, r, :])
            ins.then_inc(pc.next("mv" + tag), 1)

        def ln_rstd(pool, pc, n, tiles, tag=""):
            pool.wait_ge(pc.of("mv" + tag), pc.upto(n, "mv" + tag))
            nc.gpsimd.tensor_tensor(rstd[:, 0:tiles], mv[:, 0:tiles, 1], eps[:, 0:tiles], ALU.add).then_inc(pc.next("var" + tag), 1)
            pool.wait_ge(pc.of("var" + tag), pc.upto(n, "var" + tag))
            nc.gpsimd.tensor_tensor(rstd[:, 0:tiles], rstd[:, 0:tiles], nhalf[:, 0:tiles], ALU.pow).then_inc(pc.next("rstd" + tag), 1)

        def ln_apply(dve, pc, n, src, tiles, tag=""):
            dve.wait_ge(pc.of("rstd" + tag), pc.upto(n, "rstd" + tag))
            for r in range(tiles):
                ins = nc.vector.tensor_scalar(xhat[:, r, :], src(r), mv[:, r, 0:1], rstd[:, r:r + 1],
                                              ALU.subtract, ALU.mult)
            ins.then_inc(pc.next("xh" + tag), 1)

        def front_tensor(pe, l, g, prev):
            pc = fr[l]
            lr = slice(l * DTR, (l + 1) * DTR)
            after(pe, prev)
            yield
            yield
            pe.wait_ge(pc.of("xh"), pc.upto(g, "xh"))
            for c in range(DC):
                for b in range(GB):
                    for k in range(RB):
                        if l == 0:
                            ins = nc.tensor.matmul(side[pc.bank[f"h{c}"]][:, b * S:(b + 1) * S],
                                                   xhat[:, RB * b + k, c * P:(c + 1) * P], onehot[:, k, :],
                                                   start=(k == 0), stop=(k == RB - 1))
                        else:
                            ins = nc.tensor.transpose(
                                side[pc.bank[f"h{c}"]][:, b * S + k * P:b * S + (k + 1) * P],
                                xhat[:, RB * b + k, c * P:(c + 1) * P], ident[:, :])
                ins.then_inc(pc.next(f"h{c}"), 1)
            yield
            pe.wait_ge(pc.of("hc1"), pc.upto(g, "hc1"))
            for m in range(2 * IC):
                if m >= 3:
                    free = f"cv{m - 3}_3" if m - 3 < IC else f"z{m - 3 - IC}"
                    pe.wait_ge(pc.of(free), pc.upto(g, free))
                for k in range(DC):
                    ins = nc.tensor.matmul(side[pc.bank[f"m{m}"]], w_in[l][:, k, m * P:(m + 1) * P],
                                           hT[:, k, :], start=(k == 0), stop=(k == DC - 1))
                ins.then_inc(pc.next(f"m{m}"), 1)
                if m % 2:
                    yield
            yield
            pe.wait_ge(pc.of("z1"), pc.upto(g, "z1"))
            for c in range(IC):
                ins = nc.tensor.matmul(side[pc.bank["xp"]][0:DTR + 2 * NS, :], w_xp[l][:, c, :], u[:, c, :],
                                       start=(c == 0), stop=(c == IC - 1))
            ins.then_inc(pc.next("xp"), 1)
            yield
            for m in range(IC):
                if m == 0:
                    pe.wait_ge(pc.of("dtr"), pc.upto(g, "dtr"))
                if m == 2:
                    pe.wait_ge(pc.of("bclo"), pc.upto(g, "bclo"))
                if m == 3:
                    pe.wait_ge(pc.of("dt0"), pc.upto(g, "dt0"))
                nc.tensor.matmul(side[pc.bank[f"d{m}"]], w_dt[lr, m * P:(m + 1) * P], xd[lr, :],
                                           start=True, stop=True).then_inc(pc.next(f"d{m}"), 1)
                if m == 1 or m == 2:
                    yield
            yield

        def front_scalar(act, l, g, prev):
            pc = fr[l]
            after(act, prev, half_of_u=1)
            loads_of_piece(act, "front", l, g, prev)
            if l == 1:
                if not (isinstance(g, int) and g == 0):
                    act.wait_ge(stored, 16 * GB * g)
                nc.scalar.activation(x_c[:, :, :].rearrange("p r d -> p (r d)"),
                                               x_b[:, :, :].rearrange("p r d -> p (r d)"), ACT.Copy).then_inc(pc.next("xc"), 1)
            yield
            yield
            for c in range(DC):
                act.wait_ge(pc.of(f"h{c}"), pc.upto(g, f"h{c}"))
                if c == 0:
                    act.wait_ge(pc.of("cur"), pc.upto(g, "cur"))
                for b in range(GB):
                    ins = nc.scalar.activation(hT[:, c, b * S:(b + 1) * S],
                                               side[pc.bank[f"h{c}"]][:, b * S:(b + 1) * S], ACT.Identity,
                                               bias=cur[:, 1, c, b:b + 1], scale=cur[:, 0, c, b:b + 1])
                ins.then_inc(pc.next(f"hc{c}"), 1)
            yield

            def silu_u(m):
                act.wait_ge(pc.of(f"cv{m}_3"), pc.upto(g, f"cv{m}_3"))
                nc.scalar.activation(u[:, m, :], u[:, m, :], ACT.Silu).then_inc(pc.next(f"u{m}"), 1)

            for m in range(IC):
                act.wait_ge(pc.of(f"m{m}"), pc.upto(g, f"m{m}"))
                nc.scalar.activation(u[:, m, :], side[pc.bank[f"m{m}"]], ACT.Identity,
                                               bias=col(f"m{l}_conv_b", m),
                                               scale=col(f"m{l}_conv_w", m * TAPS + TAPS - 1)).then_inc(pc.next(f"tap{m}"), 1)
                if m:
                    silu_u(m - 1)
                if m % 2:
                    yield
            silu_u(IC - 1)
            for m in range(IC):
                act.wait_ge(pc.of(f"m{IC + m}"), pc.upto(g, f"m{IC + m}"))
                nc.scalar.activation(sz[l][:, m, :], side[pc.bank[f"m{IC + m}"]], ACT.Silu).then_inc(pc.next(f"z{m}"), 1)
                if m % 2:
                    yield
            yield
            act.wait_ge(pc.of("xp"), pc.upto(g, "xp"))
            nc.scalar.activation(xd[l * DTR:(l + 1) * DTR, :], side[pc.bank["xp"]][0:DTR, :], ACT.Copy).then_inc(pc.next("dtr"), 1)
            nc.scalar.activation(bcr[l][0:32, :], side[pc.bank["xp"]][DTR:DTR + 32, :], ACT.Copy).then_inc(pc.next("bchi"), 1)
            yield

            def exp_dt(m):
                act.wait_ge(pc.of(f"d{m}"), pc.upto(g, f"d{m}"))
                nc.scalar.activation(dt_[l][:, m, :], side[pc.bank[f"d{m}"]], ACT.Exp,
                                               bias=col(f"m{l}_b_dt", m)).then_inc(pc.next(f"e{m}"), 1)

            def ln_dt(m):
                act.wait_ge(pc.of(f"mn{m}"), pc.upto(g, f"mn{m}"))
                nc.scalar.activation(dt_[l][:, m, :], dt_[l][:, m, :], ACT.Ln, bias=one_col[:, 0:1]).then_inc(pc.next(f"l{m}"), 1)

            exp_dt(0)
            exp_dt(1)
            yield
            exp_dt(2)
            for m in range(IC - 1):
                ln_dt(m)
            yield
            exp_dt(3)
            ln_dt(3)
            yield

        def front_vector(dve, l, g, prev):
            pc = fr[l]
            after(dve, prev, half_of_u=1)
            src = lambda r: x_src[l][:, r, :]
            if l == 0:
                dve.wait_ge(xin, 16 * g + 16)
            ln_stats(dve, pc, g, src, R, also=lambda: copy_coef(pc, "m0" if l == 0 else "m1", g))
            yield
            ln_apply(dve, pc, g, src, R)
            yield
            yield
            for m in range(IC):
                bank = side[pc.bank[f"m{m}"]].rearrange("p (b s) -> p b s", b=GB)
                um = u[:, m, :].rearrange("p (b s) -> p b s", b=GB)
                for s in range(1, TAPS):
                    dve.wait_ge(pc.of(f"cv{m}_{s - 1}" if s > 1 else f"tap{m}"), pc.upto(g, f"cv{m}_{s - 1}" if s > 1 else f"tap{m}"))
                    nc.vector.scalar_tensor_tensor(
                        out=um[:, :, s:], in0=bank[:, :, 0:S - s], scalar=col(f"m{l}_conv_w", m * TAPS + TAPS - 1 - s),
                        in1=um[:, :, s:], op0=ALU.mult, op1=ALU.add).then_inc(pc.next(f"cv{m}_{s}"), 1)
                if m % 2:
                    yield
            yield
            yield
            yield
            dve.wait_ge(pc.of("bchi"), pc.upto(g, "bchi"))
            nc.vector.tensor_tensor(bcr[l][32:64, :], side[pc.bank["xp"]][DTR:DTR + 32, :],
                                              bcr[l][0:32, :], ALU.subtract).then_inc(pc.next("bclo"), 1)
            yield

            def cap(m):
                dve.wait_ge(pc.of(f"e{m}"), pc.upto(g, f"e{m}"))
                nc.vector.tensor_scalar(dt_[l][:, m, :], dt_[l][:, m, :], EXP_CAP, None, ALU.min).then_inc(pc.next(f"mn{m}"), 1)

            def step_size(m):
                dve.wait_ge(pc.of(f"l{m}"), pc.upto(g, f"l{m}"))
                nc.vector.scalar_tensor_tensor(
                    out=dt_[l][:, m, :], in0=side[pc.bank[f"d{m}"]], scalar=col(f"m{l}_b_dt", m),
                    in1=dt_[l][:, m, :], op0=ALU.add, op1=ALU.max).then_inc(pc.next(f"dt{m}"), 1)

            cap(0)
            cap(1)
            yield
            cap(2)
            for m in range(IC - 1):
                step_size(m)
            yield
            cap(3)
            step_size(3)
            yield

        def front_pool(pool, l, g, prev):
            pc = fr[l]
            after(pool, prev)
            yield
            ln_rstd(pool, pc, g, R)
            for _ in range(FRONT_PH - 3):
                yield
            for m in range(IC):
                pool.wait_ge(pc.of(f"dt{m}"), pc.upto(g, f"dt{m}"))
                nc.gpsimd.tensor_tensor(dtx[l][:, m, :], dt_[l][:, m, :], u[:, m, :], ALU.mult).then_inc(pc.next(f"dtx{m}"), 1)
                if m == 2:
                    yield
            yield

        def copy_coef(pc, site, g):
            c0 = SITES.index(site) * 2 * DC
            nc.vector.tensor_copy(cur[:, :, :, :].rearrange("p a c b -> p (a c) b"),
                                            coef[:, c0:c0 + 2 * DC, bass.ds(g * GB, GB)]).then_inc(pc.next("cur"), 1)

        def scan_tensor(pe, l, g, prev):
            pc = sc[l]

            def spread(k):
                if k >= BC_RING:
                    used = (f"hc{(k - BC_RING) // 2}" if (k - BC_RING) % 2 else f"dbx{(k - BC_RING) // 2}")
                    pe.wait_ge(pc.of(used), pc.upto(g, used))
                row = k // 2 % NS + NS * (k % 2)
                nc.tensor.matmul(bc[k % BC_RING], pick[:, row:row + 1].broadcast_to([P, P]), bcr[l][:, :],
                                 start=True, stop=True).then_inc(pc.next(f"bc{k}"), 1)

            def skip_term(half):
                for cc in range(2):
                    c = 2 * half + cc
                    ins = nc.tensor.matmul(yps[:, cc, :], diag_d[:, l, c, :], u[:, c, :], start=True, stop=False)
                ins.then_inc(pc.next(f"du{half}"), 1)

            def reduce(q):
                pe.wait_ge(pc.of(f"add{q}"), pc.upto(g, f"add{q}"))
                for cc in range(2):
                    ins = nc.tensor.matmul(yps[:, cc, :], ident[:, :], hw[(2 * q + 1) % RING][:, cc, :],
                                           start=False, stop=(2 * q % NS == NS - 2))
                ins.then_inc(pc.next(f"red{q}"), 1)

            yield 0
            for e, v in fr[l].events.items():
                pe.wait_ge(fr[l].sem[e], (g + 1) * len(v))
            if prev is not None:
                kind, n = number(*prev)
                pe.wait_ge(kind.of(f"hc{STEPS - 1}"), kind.upto(n, f"hc{STEPS - 1}"))
            for k in range(BC_RING):
                spread(k)
            if prev is not None:
                pe.wait_ge(kind.of("yg3"), kind.upto(n, "yg3"))
            skip_term(0)
            for s in range(1, STEPS):
                yield s + AT["spread_c"]
                spread(2 * s + 1)
                if s + 1 < STEPS:
                    yield s + AT["spread_b"]
                    spread(2 * s + 2)
                if s == NS + 3:
                    pe.wait_ge(pc.of("yg1"), pc.upto(g, "yg1"))
                    skip_term(1)
                if s % 2 and s >= 3:
                    yield s + AT["reduce"]
                    reduce((s - 3) // 2)
            yield STEPS + AT["last"]
            reduce(STEPS // 2 - 1)

        def scan_scalar(act, l, g, prev):
            pc = sc[l]

            def decay(q):
                if q > AHEAD:
                    act.wait_ge(pc.of(f"scan{q - AHEAD - 1}"), pc.upto(g, f"scan{q - AHEAD - 1}"))
                for cc in range(2):
                    c = 2 * (q // NS) + cc
                    ins = nc.scalar.activation(
                        da[q % (AHEAD + 1)][:, cc, :, 1:S],
                        dt_[l][:, c, :].rearrange("p (b s) -> p b s", b=GB)[:, :, 1:S],
                        ACT.Exp, scale=a_neg[:, l, c * NS + q % NS:c * NS + q % NS + 1])
                ins.then_inc(pc.next(f"exp{q}"), 1)

            yield 0
            for e, v in fr[l].events.items():
                act.wait_ge(fr[l].sem[e], (g + 1) * len(v))
            if prev is not None:
                kind, n = number(*prev)
                act.wait_ge(kind.of(f"scan{STEPS - 1}"), kind.upto(n, f"scan{STEPS - 1}"))
            for q in range(AHEAD):
                decay(q)
            for s in range(STEPS - AHEAD):
                yield s + AT["decay"]
                decay(s + AHEAD)

        def gated(dve, l, g, half):
            pc = sc[l]
            last = f"red{NS // 2 * (half + 1) - 1}"
            dve.wait_ge(pc.of(last), pc.upto(g, last))
            for cc in range(2):
                c = 2 * half + cc
                nc.vector.tensor_tensor(dtx[l][:, c, :], yps[:, cc, :], sz[l][:, c, :], ALU.mult)\
                  .then_inc(pc.next(f"yg{c}"), 1)

        def scan_vector(dve, l, g, prev):
            pc = sc[l]
            yield 0
            for e, v in fr[l].events.items():
                dve.wait_ge(fr[l].sem[e], (g + 1) * len(v))
            if prev is not None:
                kind, k = number(*prev)
                dve.wait_ge(kind.of(f"red{STEPS // 2 - 1}"), kind.upto(k, f"red{STEPS // 2 - 1}"))
            for s in range(STEPS):
                half, tile = s // NS, hw[s % RING]
                b_n = bc[2 * s % BC_RING].unsqueeze(1).broadcast_to([P, 2, T])
                c_n = bc[(2 * s + 1) % BC_RING].unsqueeze(1).broadcast_to([P, 2, T])
                yield s
                dve.wait_ge(pc.of(f"bc{2 * s}"), pc.upto(g, f"bc{2 * s}"))
                if s >= RING:
                    used = (f"red{(s - RING) // 2}" if s % 2 else f"add{(s - RING) // 2}")
                    dve.wait_ge(pc.of(used), pc.upto(g, used))
                nc.vector.tensor_tensor(tile[:, :, :], dtx[l][:, 2 * half:2 * half + 2, :], b_n, ALU.mult)\
                  .then_inc(pc.next(f"dbx{s}"), 1)
                yield s + AT["scan"]
                dve.wait_ge(pc.of(f"exp{s}"), pc.upto(g, f"exp{s}"))
                dve.wait_ge(pc.of(f"dbx{s}"), pc.upto(g, f"dbx{s}"))
                ht = tile[:, :, :].rearrange("p c t -> p (c t)")
                nc.vector.tensor_tensor_scan(
                    ht, da[s % (AHEAD + 1)][:, :, :, :].rearrange("p c b s -> p (c b s)"), ht, 0.0, ALU.mult, ALU.add)\
                  .then_inc(pc.next(f"scan{s}"), 1)
                yield s + AT["times_c"]
                dve.wait_ge(pc.of(f"bc{2 * s + 1}"), pc.upto(g, f"bc{2 * s + 1}"))
                dve.wait_ge(pc.of(f"scan{s}"), pc.upto(g, f"scan{s}"))
                nc.vector.tensor_tensor(tile[:, :, :], tile[:, :, :], c_n, ALU.mult).then_inc(pc.next(f"hc{s}"), 1)
                if s == NS + 1:
                    gated(dve, l, g, 0)
            yield STEPS + AT["gated"]
            gated(dve, l, g, 1)

        def scan_pool(pool, l, g, prev):
            pc = sc[l]
            for s in range(1, STEPS, 2):
                yield s + AT["add"]
                pool.wait_ge(pc.of(f"hc{s}"), pc.upto(g, f"hc{s}"))
                nc.gpsimd.tensor_tensor(hw[s % RING][:, :, :], hw[(s - 1) % RING][:, :, :], hw[s % RING][:, :, :],
                                        ALU.add).then_inc(pc.next(f"add{s // 2}"), 1)

        def back_tensor(pe, l, g, prev):
            pc = bk[l]
            after(pe, prev)
            pe.wait_ge(sc[l].of("yg3"), sc[l].upto(g, "yg3"))
            for b in range(GB):
                key = f"y{b}" if l == 0 else f"g{b}"
                for k in range(RB):
                    r = RB * b + k
                    for c in range(IC):
                        ins = nc.tensor.matmul(side[pc.bank[key]][:, k * D:(k + 1) * D],
                                               dtx[l][:, c, r * P:(r + 1) * P], w_out[l][:, c, :],
                                               start=(c == 0), stop=(c == IC - 1))
                ins.then_inc(pc.next(key), 1)
            yield
            if l == 0:
                for b in range(GB):
                    pe.wait_ge(pc.of(f"yo{b}"), pc.upto(g, f"yo{b}"))
                    for j in range(RB):
                        for k in range(RB):
                            ins = nc.tensor.matmul(side[pc.bank[f"g{b}"]][:, j * D:(j + 1) * D],
                                                   onehot[:, k, j * P:(j + 1) * P], xhat[:, RB * b + k, :],
                                                   start=(k == 0), stop=(k == RB - 1))
                    ins.then_inc(pc.next(f"g{b}"), 1)
            yield

        def back_scalar(act, l, g, prev):
            after(act, prev)
            loads_of_piece(act, "back", l, g, prev)
            if l == 0:
                pc = bk[l]
                for b in range(GB):
                    act.wait_ge(pc.of(f"y{b}"), pc.upto(g, f"y{b}"))
                    nc.scalar.activation(
                        xhat[:, RB * b:RB * (b + 1), :].rearrange("p r d -> p (r d)"),
                        side[pc.bank[f"y{b}"]], ACT.Copy).then_inc(pc.next(f"yo{b}"), 1)
            yield
            yield

        def back_vector(dve, l, g, prev):
            pc = bk[l]
            after(dve, prev)
            yield
            tmp = hT[:, :, :].rearrange("p c (r d) -> p (c r) d", d=D)
            dve.wait_ge(gin[l], 16 * GB * g + 16 * GB)
            for b in range(GB):
                dve.wait_ge(pc.of(f"g{b}"), pc.upto(g, f"g{b}"))
                nc.vector.tensor_tensor(
                    tmp[:, RB * b:RB * (b + 1), :],
                    side[pc.bank[f"g{b}"]].rearrange("p (r d) -> p r d", r=RB),
                    gate[:, b, :].unsqueeze(1).broadcast_to([P, RB, D]), ALU.mult).then_inc(pc.next(f"mul{b}"), 1)
            if l == 0:
                dve.wait_ge(xb_in, 16 * g + 16)
            for b in range(GB):
                dve.wait_ge(pc.of(f"mul{b}"), pc.upto(g, f"mul{b}"))
                rb = slice(RB * b, RB * (b + 1))
                nc.vector.tensor_tensor(x_res[l][:, rb, :], x_res[l][:, rb, :], tmp[:, rb, :], ALU.add).then_inc(pc.next(f"x{b}"), 1)
            yield

        def nothing(eng, l, g, prev):
            yield

        def tail_tensor(pe, pc, n, w, bias, bank_free):
            pe.wait_ge(pc.of("xh2"), pc.upto(n, "xh2"))
            pe.wait_ge(pc.of(bank_free[0]), pc.upto(n, bank_free[0]))
            transpose_rows(pc, "h2")
            yield
            pe.wait_ge(pc.of("hc2"), pc.upto(n, "hc2"))
            pe.wait_ge(pc.of(bank_free[1]), pc.upto(n, bank_free[1]))
            project_rows(pc, "out", w, bias)
            yield

        def transpose_rows(pc, key):
            for c in range(DC):
                for k in range(RB):
                    ins = nc.tensor.transpose(side[pc.bank[key]][:, c * S + k * P:c * S + (k + 1) * P],
                                              xhat[:, k, c * P:(c + 1) * P], ident[:, :])
            ins.then_inc(pc.next(key), 1)

        def project_rows(pc, key, w, bias):
            for k in range(RB):
                dst = side[pc.bank[key]][:, k * D:(k + 1) * D]
                nc.tensor.matmul(dst, *rowb(bias), start=True, stop=False)
                for c in range(DC):
                    ins = nc.tensor.matmul(dst, hT[:, c, k * P:(k + 1) * P], w_att[w][:, c, :],
                                           start=False, stop=(c == DC - 1))
            ins.then_inc(pc.next(key), 1)

        def project_channels(pc, key, w):
            for m in range(DC):
                for c in range(DC):
                    ins = nc.tensor.matmul(side[pc.bank[key]][:, m * S:(m + 1) * S],
                                           w_att[w][:, c, m * P:(m + 1) * P], hT[:, c, 0:S],
                                           start=(c == 0), stop=(c == DC - 1))
            ins.then_inc(pc.next(key), 1)

        def tail_scalar(act, pc, n, b):
            act.wait_ge(pc.of("h2"), pc.upto(n, "h2"))
            for c in range(DC):
                ins = nc.scalar.activation(hT[:, c, 0:S], side[pc.bank["h2"]][:, c * S:(c + 1) * S], ACT.Silu,
                                           bias=cur[:, 1, c, b:b + 1], scale=cur[:, 0, c, b:b + 1])
            ins.then_inc(pc.next("hc2"), 1)

        def attn_tensor(pe, b, g, prev):
            pc, n = at, 2 * g + b
            after(pe, prev)
            yield
            yield
            pe.wait_ge(pc.of("xh"), pc.upto(n, "xh"))
            transpose_rows(pc, "h")
            yield
            pe.wait_ge(pc.of("hc"), pc.upto(n, "hc"))
            project_channels(pc, "q", "a_q")
            project_channels(pc, "k", "a_k")
            yield
            pe.wait_ge(pc.of("hc"), pc.upto(n, "hc"))
            project_rows(pc, "v", "a_v", "a_v_b")
            yield
            for z in range(2):
                for p in range(z * HP, (z + 1) * HP):
                    if p == 0:
                        pe.wait_ge(pc.of("klo"), pc.upto(n, "klo"))
                    pe.wait_ge(pc.of(R_FREE[p]), pc.upto(n, R_FREE[p]))
                    bank = side[pc.bank[f"r{p}"]]
                    for w, src in enumerate((qhl, khl)):
                        for part in range(2):
                            ins = nc.tensor.matmul(bank[:, w * S:(w + 1) * S], stack[:, 2 * w + part, p % 4, :],
                                                   src[:, part, p // 4, :], start=(part == 0), stop=(part == 1))
                    ins.then_inc(pc.next(f"r{p}"), 1)
                    if p % 2:
                        yield
                pe.wait_ge(pc.of(f"rc{(z + 1) * HP - 2}"), pc.upto(n, f"rc{(z + 1) * HP - 2}"))
                pe.wait_ge(pc.of(f"rc{(z + 1) * HP - 1}"), pc.upto(n, f"rc{(z + 1) * HP - 1}"))
                for p in range(z * HP, (z + 1) * HP):
                    banks = [side[pc.bank[f"s{p}{hh}"]] for hh in range(2)]
                    for hh in range(2):
                        j = 2 * p + hh
                        if j - 4 * HP // 2 * z >= 3:
                            pe.wait_ge(pc.of(f"mx{(j - 3) // 2}{(j - 3) % 2}"), pc.upto(n, f"mx{(j - 3) // 2}{(j - 3) % 2}"))
                        nc.tensor.matmul(banks[hh].rearrange("p (h s) -> p h s", h=2),
                                         pick[:, 0:1].broadcast_to([P, P]),
                                         mb[:, :].unsqueeze(1).broadcast_to([P, 2, S]), start=True, stop=False,
                                         skip_group_check=True)
                    for t in range(RB):
                        for hh in range(2):
                            rr = slice(64 * hh, 64 * hh + 64)
                            ins = nc.tensor.matmul(banks[hh][:, t * S:(t + 1) * S],
                                                   qk[rr, p % HP, 0, t * P:(t + 1) * P],
                                                   qk[rr, p % HP, 1, :], start=False, stop=True, skip_group_check=True)
                            if t == RB - 1:
                                ins.then_inc(pc.next(f"s{p}{hh}"), 1)
                    if p % 2:
                        yield
                pe.wait_ge(pc.of(f"mx{(z + 1) * HP - 1}1"), pc.upto(n, f"mx{(z + 1) * HP - 1}1"))
                for t in range(RB):
                    ins = nc.tensor.transpose(side[pc.bank[f"nm{z}"]][0:2 * HP, t * P:(t + 1) * P],
                                              mx[:, t, z * 2 * HP:(z + 1) * 2 * HP], ident[:, :])
                ins.then_inc(pc.next(f"nm{z}"), 1)
                yield
                for p in range(z * HP, (z + 1) * HP + 1):
                    if p < (z + 1) * HP:
                        banks = [side[pc.bank[f"t{p}{hh}"]] for hh in range(2)]
                        for hh in range(2):
                            if p == z * HP and hh == 0:
                                pe.wait_ge(pc.of(f"nmlo{z}"), pc.upto(n, f"nmlo{z}"))
                            if p > z * HP:
                                pe.wait_ge(pc.of(f"x{p - 1}{hh}"), pc.upto(n, f"x{p - 1}{hh}"))
                            c0 = 2 * (p % HP) + hh
                            nc.tensor.matmul(banks[hh].rearrange("p (h s) -> p h s", h=2),
                                             pick[:, c0:c0 + 1].broadcast_to([P, P]),
                                             nm[:, :].unsqueeze(1).broadcast_to([P, 2, S]), start=True, stop=False,
                                             skip_group_check=True)
                        for t in range(RB):
                            for hh in range(2):
                                rr = slice(64 * hh, 64 * hh + 64)
                                ins = nc.tensor.matmul(banks[hh][:, t * S:(t + 1) * S],
                                                       qk[rr, p % HP, 1, t * P:(t + 1) * P], qk[rr, p % HP, 0, :],
                                                       start=False, stop=True, skip_group_check=True)
                                if t == RB - 1:
                                    ins.then_inc(pc.next(f"t{p}{hh}"), 1)
                    if p > z * HP:
                        j, last = (p - 1) // 2, p - 1
                        pe.wait_ge(pc.of(f"x{last}1"), pc.upto(n, f"x{last}1"))
                        if last % 4 == 2:
                            pe.wait_ge(pc.of(f"ye{j - 1}"), pc.upto(n, f"ye{j - 1}"))
                        for hh in range(2):
                            h = 2 * last + hh
                            q0 = 32 * (h % 4)
                            for t in range(RB):
                                ins = nc.tensor.matmul(side[2][q0:q0 + 32, 0:S], va[:, t, h, :],
                                                       pt[h % 4][:, t, :], start=(t == 0), stop=(t == 1))
                        ins.then_inc(pc.next(f"pv{last}"), 1)
                    yield
            for t in range(RB):
                if t == 0:
                    pe.wait_ge(pc.of("ye2"), pc.upto(n, "ye2"))
                    pe.wait_ge(pc.of("ye3"), pc.upto(n, "ye3"))
                for j in range(H // 4):
                    ins = nc.tensor.transpose(side[pc.bank[f"o{t}"]][:, j * P:(j + 1) * P],
                                              yT[:, j, t * P:(t + 1) * P], ident[:, :])
                ins.then_inc(pc.next(f"o{t}"), 1)
            yield
            yield from tail_tensor(pe, pc, n, "a_out", "a_out_b", ("ye3", "yn0"))

        def attn_scalar(act, b, g, prev):
            pc, n = at, 2 * g + b
            after(act, prev, half_of_u=0)
            loads_of_piece(act, "attn", b, g, prev)
            yield
            yield
            act.wait_ge(pc.of("h"), pc.upto(n, "h"))
            for c in range(DC):
                ins = nc.scalar.activation(hT[:, c, 0:S], side[pc.bank["h"]][:, c * S:(c + 1) * S], ACT.Identity,
                                           bias=col("a_norm_b", c), scale=col("a_norm_w", c))
            ins.then_inc(pc.next("hc"), 1)
            yield
            for key, dst, bias in (("q", qhl, "a_q_b"), ("k", khl, "a_k_b")):
                act.wait_ge(pc.of(key), pc.upto(n, key))
                for m in range(DC):
                    ins = nc.scalar.activation(dst[:, 0, m, :], side[pc.bank[key]][:, m * S:(m + 1) * S],
                                               ACT.Identity, bias=col(bias, m))
                ins.then_inc(pc.next(key + "hi"), 1)
            yield
            act.wait_ge(pc.of("v"), pc.upto(n, "v"))
            act.wait_ge(pc.of("mcur"), pc.upto(n, "mcur"))
            for k in range(RB):
                ins = nc.scalar.activation(va[:, k, :, 0:DH],
                                           side[pc.bank["v"]][:, k * D:(k + 1) * D].rearrange("p (h d) -> p h d", h=H),
                                           ACT.Copy, scale=mcur[:, 0, k:k + 1])
            ins.then_inc(pc.next("v_"), 1)
            yield
            for z in range(2):
                for p in range(z * HP, (z + 1) * HP, 2):
                    act.wait_ge(pc.of(f"r{p}"), pc.upto(n, f"r{p}"))
                    nc.scalar.activation(qk[:, p % HP, :, :].rearrange("p w s -> p (w s)"),
                                                   side[pc.bank[f"r{p}"]], ACT.Copy).then_inc(pc.next(f"rc{p}"), 1)
                    yield
                yield
                yield
                act.wait_ge(pc.of(f"nm{z}"), pc.upto(n, f"nm{z}"))
                nc.scalar.activation(nm[0:2 * HP, :], side[pc.bank[f"nm{z}"]][0:2 * HP, 0:S], ACT.Copy,
                                               scale=-1.0).then_inc(pc.next(f"nmhi{z}"), 1)
                yield
                for p in range(z * HP, (z + 1) * HP + 1):
                    if p < (z + 1) * HP:
                        for hh in range(2):
                            act.wait_ge(pc.of(f"t{p}{hh}"), pc.upto(n, f"t{p}{hh}"))
                            if p == 0 and hh == 0:
                                act.wait_ge(pc.of("mbias"), pc.upto(n, "mbias"))
                            for t in range(RB):
                                ins = nc.scalar.activation(pt[(2 * p + hh) % 4][:, t, :],
                                                           side[pc.bank[f"t{p}{hh}"]][:, t * S:(t + 1) * S],
                                                           ACT.Exp, bias=mcur[:, 1, t:t + 1])
                            ins.then_inc(pc.next(f"x{p}{hh}"), 1)
                    if p > z * HP and p % 4 == 0:
                        j = p // 2 - 1
                        act.wait_ge(pc.of(f"pv{2 * j + 1}"), pc.upto(n, f"pv{2 * j + 1}"))
                        nc.scalar.activation(yT[:, j, :], side[2][:, 0:S], ACT.Copy).then_inc(pc.next(f"ye{j}"), 1)
                    yield
            yield
            tail_scalar(act, pc, n, b)
            yield
            yield

        def attn_vector(dve, b, g, prev):
            pc, n = at, 2 * g + b
            after(dve, prev, half_of_u=0)
            src = lambda r: x_b[:, RB * b + r, :]

            def copies():
                copy_coef(pc, "a", g)
                nc.vector.tensor_copy(mcur[:, 0, :],
                                                amask[:, bass.ds(n, 1), :].rearrange("p o k -> p (o k)")).then_inc(pc.next("mcur"), 1)

            ln_stats(dve, pc, n, src, RB, also=copies)
            dve.wait_ge(pc.of("mcur"), pc.upto(n, "mcur"))
            nc.vector.tensor_scalar(mcur[:, 1, :], mcur[:, 0, :], 1.0, 1e6, ALU.subtract, ALU.mult).then_inc(pc.next("mbias"), 1)
            yield
            ln_apply(dve, pc, n, src, RB)
            dve.wait_ge(min_, 16 * n + 16)
            nc.vector.tensor_scalar(mrow[:, :], mrow[:, :], 1.0, 1e6, ALU.subtract, ALU.mult).then_inc(pc.next("mval"), 1)
            dve.wait_ge(pc.of("mval"), pc.upto(n, "mval"))
            nc.vector.tensor_copy(mb[0:1, :], mrow[:, :]).then_inc(pc.next("mhi"), 1)
            dve.wait_ge(pc.of("mhi"), pc.upto(n, "mhi"))
            nc.vector.tensor_tensor(mb[32:33, :], mrow[:, :], mb[0:1, :], ALU.subtract).then_inc(pc.next("mlo"), 1)
            yield
            yield
            for key, dst, bias in (("q", qhl, "a_q_b"), ("k", khl, "a_k_b")):
                dve.wait_ge(pc.of(key + "hi"), pc.upto(n, key + "hi"))
                for m in range(DC):
                    ins = nc.vector.scalar_tensor_tensor(
                        out=dst[:, 1, m, :], in0=side[pc.bank[key]][:, m * S:(m + 1) * S], scalar=col(bias, m),
                        in1=dst[:, 0, m, :], op0=ALU.add, op1=ALU.subtract)
                ins.then_inc(pc.next(key + "lo"), 1)
            yield
            yield
            for z in range(2):
                for p in range(z * HP + 1, (z + 1) * HP, 2):
                    dve.wait_ge(pc.of(f"r{p}"), pc.upto(n, f"r{p}"))
                    nc.vector.tensor_copy(qk[:, p % HP, :, :].rearrange("p w s -> p (w s)"),
                                                    side[pc.bank[f"r{p}"]]).then_inc(pc.next(f"rc{p}"), 1)
                    yield
                for p in range(z * HP, (z + 1) * HP):
                    for hh in range(2):
                        dve.wait_ge(pc.of(f"s{p}{hh}"), pc.upto(n, f"s{p}{hh}"))
                        nc.vector.tensor_reduce(
                            mx[:, :, 2 * p + hh], side[pc.bank[f"s{p}{hh}"]].rearrange("p (t s) -> p t s", t=RB), X,
                            ALU.max).then_inc(pc.next(f"mx{p}{hh}"), 1)
                    if p % 2:
                        yield
                dve.wait_ge(pc.of(f"nmhi{z}"), pc.upto(n, f"nmhi{z}"))
                nc.vector.scalar_tensor_tensor(
                    out=nm[32:32 + 2 * HP, :], in0=side[pc.bank[f"nm{z}"]][0:2 * HP, 0:S], scalar=-1.0,
                    in1=nm[0:2 * HP, :], op0=ALU.mult, op1=ALU.subtract).then_inc(pc.next(f"nmlo{z}"), 1)
                yield
                for p in range(z * HP, (z + 1) * HP + 1):
                    if p > z * HP and p % 4 == 2:
                        j = p // 2 - 1
                        dve.wait_ge(pc.of(f"pv{2 * j + 1}"), pc.upto(n, f"pv{2 * j + 1}"))
                        nc.vector.tensor_copy(yT[:, j, :], side[2][:, 0:S]).then_inc(pc.next(f"ye{j}"), 1)
                    yield
            for t in range(RB):
                bank = side[pc.bank[f"o{t}"]].rearrange("p (h d) -> p h d", h=H)
                dve.wait_ge(pc.of(f"o{t}"), pc.upto(n, f"o{t}"))
                nc.vector.reciprocal(rec[:, 0, t, :], bank[:, :, DH]).then_inc(pc.next(f"rec{t}"), 1)
                dve.wait_ge(pc.of(f"rec{t}"), pc.upto(n, f"rec{t}"))
                nc.vector.tensor_tensor(
                    xhat[:, RB + t, :].rearrange("p (h d) -> p h d", h=H), bank[:, :, 0:DH],
                    rec[:, 0, t, :].unsqueeze(2).broadcast_to([P, H, DH]), ALU.mult).then_inc(pc.next(f"yn{t}"), 1)
            dve.wait_ge(pc.of("yn1"), pc.upto(n, "yn1"))
            ln_stats(dve, pc, n, lambda r: xhat[:, RB + r, :], RB, "2")
            yield
            ln_apply(dve, pc, n, lambda r: xhat[:, RB + r, :], RB, "2")
            yield
            dve.wait_ge(pc.of("out"), pc.upto(n, "out"))
            nc.vector.tensor_tensor(
                x_b[:, RB * b:RB * (b + 1), :], side[pc.bank["out"]].rearrange("p (r d) -> p r d", r=RB),
                x_b[:, RB * b:RB * (b + 1), :], ALU.add).then_inc(pc.next("xo"), 1)
            yield

        def attn_pool(pool, b, g, prev):
            pc, n = at, 2 * g + b
            after(pool, prev)
            yield
            ln_rstd(pool, pc, n, RB)
            for _ in range(ATTN_PH - 4):
                yield
            ln_rstd(pool, pc, n, RB, "2")
            yield

        def lin_tensor(pe, b, g, prev):
            pc, n = li, 2 * g + b
            after(pe, prev)
            yield
            yield
            pe.wait_ge(pc.of("xh"), pc.upto(n, "xh"))
            transpose_rows(pc, "h")
            yield
            pe.wait_ge(pc.of("hc"), pc.upto(n, "hc"))
            project_rows(pc, "q", "l_q", "l_q_b")
            project_channels(pc, "k", "l_k")
            yield
            pe.wait_ge(pc.of("hc"), pc.upto(n, "hc"))
            project_rows(pc, "v", "l_v", "l_v_b")
            yield
            pe.wait_ge(pc.of("qn"), pc.upto(n, "qn"))
            for c in range(DC):
                for k in range(RB):
                    ins = nc.tensor.transpose(side[pc.bank["qt"]][:, c * S + k * P:c * S + (k + 1) * P],
                                              qrow[:, k, c * P:(c + 1) * P], ident[:, :])
            ins.then_inc(pc.next("qt"), 1)
            pe.wait_ge(pc.of("kn1"), pc.upto(n, "kn1"))
            for k in range(RB):
                for c in range(DC):
                    ins = nc.tensor.transpose(side[pc.bank["kt"]][:, k * D + c * P:k * D + (c + 1) * P],
                                              kT[:, c, k * P:(k + 1) * P], ident[:, :])
            ins.then_inc(pc.next("kt"), 1)
            yield
            pe.wait_ge(pc.of("ktc"), pc.upto(n, "ktc"))
            for c in range(DC):
                for k in range(RB):
                    ins = nc.tensor.matmul(side[pc.bank["at"]][:, c * P:(c + 1) * P],
                                           vrow[:, k, c * P:(c + 1) * P], krow[:, k, c * P:(c + 1) * P],
                                           start=(k == 0), stop=(k == RB - 1))
            ins.then_inc(pc.next("at"), 1)
            pe.wait_ge(pc.of("atm"), pc.upto(n, "atm"))
            for k in range(RB):
                for c in range(DC):
                    ins = nc.tensor.matmul(side[pc.bank["y"]][:, k * D + c * P:k * D + (c + 1) * P],
                                           qT[:, c, k * P:(k + 1) * P], attnT[:, c, :], start=True, stop=True)
            ins.then_inc(pc.next("y"), 1)
            yield
            yield from tail_tensor(pe, pc, n, "l_out", "l_out_b", ("ktc", "atm"))

        def lin_scalar(act, b, g, prev):
            pc, n = li, 2 * g + b
            after(act, prev, half_of_u=0)
            loads_of_piece(act, "lin", b, g, prev)
            yield
            yield
            act.wait_ge(pc.of("h"), pc.upto(n, "h"))
            for c in range(DC):
                ins = nc.scalar.activation(hT[:, c, 0:S], side[pc.bank["h"]][:, c * S:(c + 1) * S], ACT.Identity,
                                           bias=col("l_norm_b", c), scale=col("l_norm_w", c))
            ins.then_inc(pc.next("hc"), 1)
            yield
            act.wait_ge(pc.of("qs"), pc.upto(n, "qs"))
            nc.scalar.activation(qrow, qrow, ACT.Exp).then_inc(pc.next("qe"), 1)
            yield
            act.wait_ge(pc.of("v"), pc.upto(n, "v"))
            act.wait_ge(pc.of("nmask"), pc.upto(n, "nmask"))
            for k in range(RB):
                ins = nc.scalar.activation(vrow[:, k, :], side[pc.bank["v"]][:, k * D:(k + 1) * D], ACT.Copy,
                                           scale=mcur[:, 0, k:k + 1])
            ins.then_inc(pc.next("v_"), 1)
            act.wait_ge(pc.of("km"), pc.upto(n, "km"))
            for c in range(DC):
                nc.scalar.activation(kT[:, c, :], kT[:, c, :], ACT.Exp, bias=small[:, c:c + 1],
                                               accum_out=small[:, 2 + c:3 + c]).then_inc(pc.next(f"ke{c}"), 1)
            yield
            act.wait_ge(pc.of("qt"), pc.upto(n, "qt"))
            nc.scalar.activation(qT.rearrange("p c s -> p (c s)"), side[pc.bank["qt"]], ACT.Copy).then_inc(pc.next("qtc"), 1)
            act.wait_ge(pc.of("kt"), pc.upto(n, "kt"))
            nc.scalar.activation(krow.rearrange("p c s -> p (c s)"), side[pc.bank["kt"]], ACT.Copy).then_inc(pc.next("ktc"), 1)
            yield
            yield
            tail_scalar(act, pc, n, b)
            yield
            yield

        def lin_vector(dve, b, g, prev):
            pc, n = li, 2 * g + b
            after(dve, prev, half_of_u=0)
            src = lambda r: x_c[:, RB * b + r, :]

            def copies():
                copy_coef(pc, "l", g)
                nc.vector.tensor_copy(mcur[:, 1, :],
                                                kmask_col[:, bass.ds(n, 1), :].rearrange("p o k -> p (o k)")).then_inc(pc.next("kcur"), 1)

            ln_stats(dve, pc, n, src, RB, also=copies)
            dve.wait_ge(kmin, 16 * n + 16)
            nc.vector.tensor_scalar(kmb, kmrow[:, :], 1.0, -1e30, ALU.is_equal, ALU.mult).then_inc(pc.next("kmask"), 1)
            dve.wait_ge(pc.of("kcur"), pc.upto(n, "kcur"))
            nc.vector.tensor_scalar(mcur[:, 0, :], mcur[:, 1, :], 1.0, -1.0, ALU.is_equal, ALU.mult).then_inc(pc.next("masked"), 1)
            dve.wait_ge(pc.of("masked"), pc.upto(n, "masked"))
            nc.vector.tensor_scalar(mcur[:, 0, :], mcur[:, 0, :], 1.0, None, ALU.add).then_inc(pc.next("nmask"), 1)
            yield
            ln_apply(dve, pc, n, src, RB)
            yield
            yield
            dve.wait_ge(pc.of("q"), pc.upto(n, "q"))
            q3 = side[pc.bank["q"]].rearrange("p (h d) -> p h d", d=DH)
            qm = qmx.rearrange("p r h -> p (r h)")
            qr = qrs.rearrange("p r h -> p (r h)")
            qrow3 = qrow.rearrange("p r (h d) -> p (r h) d", d=DH)
            nc.vector.tensor_reduce(qm, q3, X, ALU.max).then_inc(pc.next("qm"), 1)
            dve.wait_ge(pc.of("qm"), pc.upto(n, "qm"))
            nc.vector.tensor_tensor(qrow3, q3, qm.unsqueeze(2).broadcast_to([P, RB * H, DH]), ALU.subtract).then_inc(pc.next("qs"), 1)
            dve.wait_ge(pc.of("k"), pc.upto(n, "k"))
            dve.wait_ge(pc.of("kmask"), pc.upto(n, "kmask"))
            for c in range(DC):
                nc.vector.scalar_tensor_tensor(
                    out=kT[:, c, :], in0=side[pc.bank["k"]][:, c * S:(c + 1) * S], scalar=col("l_k_b", c),
                    in1=kmb, op0=ALU.add, op1=ALU.add).then_inc(pc.next(f"kb{c}"), 1)
            dve.wait_ge(pc.of("kb1"), pc.upto(n, "kb1"))
            nc.vector.tensor_reduce(small[:, 0:2], kT, X, ALU.max, negate=True).then_inc(pc.next("km"), 1)
            yield
            dve.wait_ge(pc.of("qe"), pc.upto(n, "qe"))
            nc.vector.tensor_reduce(qr, qrow3, X, ALU.add).then_inc(pc.next("qsum"), 1)
            dve.wait_ge(pc.of("qsum"), pc.upto(n, "qsum"))
            nc.vector.reciprocal(qr, qr).then_inc(pc.next("qrec"), 1)
            dve.wait_ge(pc.of("qrec"), pc.upto(n, "qrec"))
            nc.vector.tensor_tensor(qrow3, qrow3, qr.unsqueeze(2).broadcast_to([P, RB * H, DH]), ALU.mult).then_inc(pc.next("qn"), 1)
            dve.wait_ge(pc.of("ke1"), pc.upto(n, "ke1"))
            nc.vector.reciprocal(small[:, 4:6], small[:, 2:4]).then_inc(pc.next("krec"), 1)
            dve.wait_ge(pc.of("krec"), pc.upto(n, "krec"))
            for c in range(DC):
                nc.vector.tensor_scalar(kT[:, c, :], kT[:, c, :], small[:, 4 + c:5 + c], None, ALU.mult).then_inc(pc.next(f"kn{c}"), 1)
            yield
            yield
            dve.wait_ge(pc.of("at"), pc.upto(n, "at"))
            nc.vector.tensor_tensor(
                attnT, side[pc.bank["at"]][:, 0:DC * P].rearrange("p (c e) -> p c e", c=DC),
                blocks[:, :].unsqueeze(1).broadcast_to([P, DC, P]), ALU.mult).then_inc(pc.next("atm"), 1)
            dve.wait_ge(pc.of("y"), pc.upto(n, "y"))
            ysrc = lambda r: side[pc.bank["y"]][:, r * D:(r + 1) * D]
            ln_stats(dve, pc, n, ysrc, RB, "2")
            yield
            ln_apply(dve, pc, n, ysrc, RB, "2")
            yield
            dve.wait_ge(pc.of("out"), pc.upto(n, "out"))
            nc.vector.tensor_tensor(
                x_c[:, RB * b:RB * (b + 1), :], side[pc.bank["out"]].rearrange("p (r d) -> p r d", r=RB),
                x_c[:, RB * b:RB * (b + 1), :], ALU.add).then_inc(pc.next("xo"), 1)
            yield

        def lin_pool(pool, b, g, prev):
            pc, n = li, 2 * g + b
            after(pool, prev)
            yield
            ln_rstd(pool, pc, n, RB)
            for _ in range(LIN_PH - 3):
                yield
            ln_rstd(pool, pc, n, RB, "2")
            yield

        ENG = {
            "pe": dict(front=front_tensor, back=back_tensor, attn=attn_tensor, lin=lin_tensor, scan=scan_tensor),
            "act": dict(front=front_scalar, back=back_scalar, attn=attn_scalar, lin=lin_scalar, scan=scan_scalar),
            "dve": dict(front=front_vector, back=back_vector, attn=attn_vector, lin=lin_vector, scan=scan_vector),
            "pool": dict(front=front_pool, back=nothing, attn=attn_pool, lin=lin_pool, scan=scan_pool),
        }
        END = 10 ** 6
        VARIANT = {"front0": ("front", 0), "front1": ("front", 1), "back0": ("back", 0), "back1": ("back", 1),
                   "attn_a": ("attn", 0), "attn_b": ("attn", 1), "lin_a": ("lin", 0), "lin_b": ("lin", 1)}

        def iteration(eng, e, i):
            for seg in range(2):
                pieces = [(k, name, i + off) for k, (name, off, where) in enumerate(SIDE)
                          if where == seg and alive(i, off)]
                total = sum(sum(WEIGHT[name]) for _, name, _ in pieces)
                scan_name, off = SCAN[seg]
                scanning = alive(i, off)
                busy["scan"] = (scan_name, i + off) if scanning else None
                scan, at_scan = iter(()), END
                if scanning and ENG[e]["scan"]:
                    scan = ENG[e]["scan"](eng, seg, i + off, before_scan(i, seg))
                    at_scan = next(scan)
                done = 0.0
                for k, name, g in pieces:
                    kind, variant = VARIANT[name]
                    run = ENG[e][kind](eng, variant, g, before_side(i, k))
                    for w in WEIGHT[name]:
                        at_side = done / total * STEPS + LAG[e]
                        while at_scan <= at_side:
                            at_scan = next(scan, END)
                        next(run, None)
                        done += w
                    for _ in run:
                        pass
                for _ in scan:
                    pass

        def all_iterations(eng, e):
            for i in range(FIRST_IT, LOOP_FROM):
                iteration(eng, e, i)
            with eng.Fori(LOOP_FROM, LOOP_TO) as i:
                iteration(eng, e, i)
            for i in range(LOOP_TO, LAST_IT + 1):
                iteration(eng, e, i)

        POOL_READY, ACT_READY, DVE_READY = 4, 3, 9
        block = ctx.enter_context(nc.Block())

        @block.sync
        def _(sp):
            n = 0
            loads = [(c_raw, a["c_t"].rearrange("(k p) b -> p k b", p=P)), (cols[:, :], a["cols"]),
                     ] + [(rowb(name)[1], a["rows"][k:k + 1, :]) for k, name in enumerate(ROWS)]
            for k in range(5):
                loads.append((w_mod[k][:, :, :], a["w_mod"][:, k * 512:(k + 1) * 512].rearrange("(k p) n -> p k n", p=P)))
            for k in range(3):
                w = 1024 if k < 2 else 512
                loads.append((mod_bias[k].rearrange("p a b -> p (a b)")[0:B, 0:w],
                              a["b_mod"][:, k * 1024:k * 1024 + w].broadcast_to([B, w])))
            loads.append((idx_i[:, :], a["idx"].broadcast_to([P, S])))
            for l in range(2):
                loads += [(w_in[l][:, :, :], a[f"w_in{l}"].rearrange("(k p) n -> p k n", p=P)),
                          (w_xp[l][:, :, :], a[f"w_xp{l}"].rearrange("(k p) n -> p k n", p=P)),
                          (w_dt[l * DTR:(l + 1) * DTR, :], a[f"w_dt{l}"]),
                          (w_out[l][:, :, :], a[f"w_out{l}"].rearrange("(k p) n -> p k n", p=P))]
            for w in w_att:
                loads.append((w_att[w][:, :, :], a[f"w_{w}"].rearrange("(k p) n -> p k n", p=P)))
            loads += [(amask[:, :, :], a["amask_col"]), (kmask_col[:, :, :], a["kmask_col"])]
            for dst, src in loads:
                sp.dma_start(dst, src).then_inc(loaded, 16)
                n += 16
            total_loads.append(n)
            sp.wait_ge(p_dve, 5)
            for l in range(2):
                src = (mod_rows if l == 0 else mod_rows2)[:, :, :].rearrange("p a b -> p (a b)")
                at0 = GATE_AT[f"m{l}"] - 1024 * l
                sp.dma_start(gates_dram[l], src[0:B, at0:at0 + D]).then_inc(gates_out, 16)
            sp.wait_ge(gates_out, 32)
            sp.wait_ge(stored, 16 * GB * NG)

        @block.gpsimd
        def _(pool):
            k = [0]

            def step(ins):
                k[0] += 1
                ins.then_inc(p_pool, 1)
                pool.wait_ge(p_pool, k[0])

            step(nc.gpsimd.memset(ident[:, :], 0.0))
            step(nc.gpsimd.affine_select(out=ident[:, :], in_=ident[:, :], compare_op=ALU.not_equal, fill=1.0,
                                         base=0, pattern=[[-1, P]], channel_multiplier=1))
            step(nc.gpsimd.memset(pick_f, 0.0))
            for off in (0, 32):
                step(nc.gpsimd.affine_select(out=pick_f, in_=pick_f, compare_op=ALU.not_equal, fill=1.0,
                                             base=-off, pattern=[[-1, 2 * NS]], channel_multiplier=1))
            for v, parts in enumerate(((0, 1), (2, 3), (0, 2), (1, 3))):
                tile = (stack_f if v < 2 else stack_g)[:, (v % 2) * 512:(v % 2) * 512 + 512]
                step(nc.gpsimd.memset(tile, 0.0))
                for part in parts:
                    sub = tile.rearrange("p (a h r l) -> p a h r l", a=4, h=2, r=4)[:, :, :, part, :]
                    step(nc.gpsimd.affine_select(out=sub, in_=sub, compare_op=ALU.not_equal, fill=1.0, base=0,
                                                 pattern=[[-32, 4], [-16, 2], [-1, 16]], channel_multiplier=1))
            step(nc.gpsimd.memset(blocks[:, :], 1.0))
            bl = blocks[:, :].rearrange("p (h d) -> p h d", d=DH)
            step(nc.gpsimd.affine_select(out=bl, in_=bl, compare_op=ALU.is_ge, fill=0.0, base=0,
                                         pattern=[[-DH, P // DH], [0, DH]], channel_multiplier=1))
            step(nc.gpsimd.affine_select(out=bl, in_=bl, compare_op=ALU.is_ge, fill=0.0, base=DH - 1,
                                         pattern=[[DH, P // DH], [0, DH]], channel_multiplier=-1))
            step(nc.gpsimd.iota(iot_i[:, :], [[P, RB]], base=0, channel_multiplier=1))
            step(nc.gpsimd.memset(nhalf[:, :], -0.5))
            step(nc.gpsimd.memset(eps[:, :], EPS))
            step(nc.gpsimd.memset(ones[:, :], 1.0))
            step(nc.gpsimd.memset(one_col[:, :], 1.0))
            step(nc.gpsimd.memset(va[:, :, :, :], 0.0))
            step(nc.gpsimd.memset(va[:, :, :, DH:DH + 1], 1.0))
            pool_steps.append(k[0])
            pool.wait_ge(p_dve, DVE_READY)
            all_iterations(pool, "pool")

        @block.scalar
        def _(act):
            act.wait_ge(loaded, total_loads[0])
            nc.scalar.activation(c_act, c_raw, ACT.Silu).then_inc(p_act, 1)
            for l in range(2):
                nc.scalar.activation(a_neg[:, l, :], col(f"m{l}_A_log", 0, IC * NS), ACT.Exp).then_inc(p_act, 1)
            act.wait_ge(p_dve, DVE_READY)
            act.wait_ge(gates_out, 32)
            all_iterations(act, "act")
            for e, v in li.events.items():
                act.wait_ge(li.sem[e], GB * NG * len(v))
            store_result(act, NG - 1, 1)

        @block.tensor
        def _(pe):
            pe.wait_ge(p_act, 1)
            for k in range(5):
                if k >= 3:
                    pe.wait_ge(p_dve, k - 2)
                for c in range(4):
                    ins = nc.tensor.matmul(side[k % 3][0:B, :], c_act[:, c, :], w_mod[k][:, c, :],
                                           start=(c == 0), stop=(c == 3))
                ins.then_inc(p_pe, 1)
            pe.wait_ge(p_dve, 5)
            pe.wait_ge(p_pool, pool_steps[0])
            for s, site in enumerate(SITES):
                for w, off in enumerate((SCALE_AT[site], SHIFT_AT[site])):
                    for c in range(DC):
                        src = off + c * P
                        tile = (mod_rows, mod_rows2, mod_rows3)[src // 1024][:, :, :].rearrange("p a b -> p (a b)")
                        j = (s * 2 + w) * DC + c
                        ins = nc.tensor.transpose(side[2][:, j * B:(j + 1) * B], tile[0:B, src % 1024:src % 1024 + P],
                                                  ident[0:B, 0:B])
            ins.then_inc(p_pe, 1)
            pe.wait_ge(p_dve, DVE_READY)
            all_iterations(pe, "pe")

        @block.vector
        def _(dve):
            dve.wait_ge(loaded, total_loads[0])
            for k in range(5):
                dve.wait_ge(p_pe, k + 1)
                tile = (mod_rows, mod_rows2, mod_rows3)[k // 2]
                nc.vector.tensor_tensor(tile[0:B, k % 2, :], side[k % 3][0:B, :], mod_bias[k // 2][0:B, k % 2, :],
                                        ALU.add).then_inc(p_dve, 1)
            dve.wait_ge(p_pe, 6)
            nc.vector.tensor_copy(modT, side[2].rearrange("p (k b) -> p k b", b=B)).then_inc(p_dve, 1)
            dve.wait_ge(p_dve, 6)
            for s in range(len(SITES)):
                sc_ = modT[:, 2 * DC * s:2 * DC * s + DC, :]
                ins = nc.vector.tensor_scalar(sc_, sc_, 1.0, None, ALU.add)
            ins.then_inc(p_dve, 1)
            dve.wait_ge(p_dve, 7)
            norm = {"m0": ("m0_ln_g", "m0_ln_b"), "a": ("a_sb_w", "a_sb_b"), "m1": ("m1_ln_g", "m1_ln_b"),
                    "l": ("l_sb_w", "l_sb_b")}
            for s, site in enumerate(SITES):
                for c in range(DC):
                    j = 2 * DC * s + c
                    nc.vector.tensor_scalar(coef[:, j, :], modT[:, j, :], col(norm[site][0], c), None, ALU.mult)
                    nc.vector.scalar_tensor_tensor(out=coef[:, j + DC, :], in0=modT[:, j, :],
                                                   scalar=col(norm[site][1], c), in1=modT[:, j + DC, :],
                                                   op0=ALU.mult, op1=ALU.add)
            dve.wait_ge(p_pool, pool_steps[0])
            dve.wait_ge(p_act, 3)
            nc.vector.tensor_scalar(a_neg[:, :, :], a_neg[:, :, :], -1.0, None, ALU.mult)
            for l in range(2):
                for c in range(IC):
                    nc.vector.tensor_scalar(diag_d[:, l, c, :], ident[:, :], col(f"m{l}_D", c), None, ALU.mult)
            nc.vector.tensor_copy(pick[:, :], pick_f)
            for v in range(4):
                nc.vector.tensor_copy(stack[:, v, :, :].rearrange("p a b -> p (a b)"),
                                      (stack_f if v < 2 else stack_g)[:, (v % 2) * 512:(v % 2) * 512 + 512])
            nc.vector.tensor_copy(idx_f, idx_i[:, :])
            nc.vector.tensor_copy(iot_f[:, :], iot_i[:, :])
            for l in range(2):
                nc.vector.memset(bcr[l][:, :].bitcast(F32), 0.0)
            nc.vector.memset(nm[:, :].bitcast(F32), 0.0)
            nc.vector.memset(mb[:, :].bitcast(F32), 0.0).then_inc(p_dve, 1)
            dve.wait_ge(p_dve, 8)
            for k in range(RB):
                nc.vector.tensor_scalar(onehot[:, k, :], idx_f, iot_f[:, k:k + 1], None, ALU.is_equal)
            for k in range(AHEAD + 1):
                nc.vector.memset(da[k][:, :, :, 0:1], 0.0)
            nc.vector.memset(small[:, :], 0.0).then_inc(p_dve, 1)
            dve.wait_ge(p_dve, DVE_READY)
            all_iterations(dve, "dve")


total_loads, pool_steps = [], []


def kernel(**inputs):
    import concourse.bacc as _bacc
    from concourse.bass_utils import run_bass_kernel_spmd as _run

    v = {k: np.asarray(x) for k, x in inputs.items()}
    c = np.ascontiguousarray

    def chunks(x):
        x = x.reshape(x.shape[0] // P, P, -1)
        return x.transpose(1, 0, 2).reshape(P, -1)

    L = {"m0": "L0_cond_", "m1": "L2_cond_"}
    names = {"m0": dict(conv_w="conv_w", conv_b="conv_b", b_dt="b_dt", D="D_param", A_log="A_log", ln_g="gamma",
                        ln_b="beta"),
             "m1": dict(conv_w="conv_w", conv_b="conv_b", b_dt="dt_proj_b", D="D_param", A_log="A_log", ln_g="ln_g",
                        ln_b="ln_b")}
    vec = {f"{m}_{k}": v[L[m] + s] for m in L for k, s in names[m].items()}
    vec |= {"a_norm_w": v["L1_cond_norm_w"], "a_norm_b": v["L1_cond_norm_b"], "a_q_b": v["L1_cond_q_b"],
            "a_k_b": v["L1_cond_k_b"], "a_sb_w": v["L1_cond_sb_norm_w"], "a_sb_b": v["L1_cond_sb_norm_b"],
            "l_norm_w": v["L3_cond_norm_scale"], "l_norm_b": v["L3_cond_norm_bias"], "l_k_b": v["L3_cond_bk"],
            "l_sb_w": v["L3_cond_film_norm_scale"], "l_sb_b": v["L3_cond_film_norm_bias"]}
    arrays = {
        "x": c(v["x"]),
        "c_t": c(v["cond_2048"].T),
        "idx": c(v["itok_S_0_1023"].reshape(1, S)),
        "amask_row": c(v["mask_BxS_ff1"]),
        "amask_col": c(v["mask_BxS_ff1"].reshape(B, RB, P).transpose(2, 0, 1)),
        "kmask_row": c(v["mask_BxS_ik0"]),
        "kmask_col": c(v["mask_BxS_ik0"].reshape(B, RB, P).transpose(2, 0, 1)),
        "cols": c(np.concatenate([chunks(vec[n]) for n in COLS], axis=1)),
        "rows": c(np.stack([v["L1_cond_v_b"], v["L1_cond_out_b"], v["L3_cond_bq"], v["L3_cond_bv"],
                            v["L3_cond_film_out_b"]])),
        "w_mod": c(np.concatenate([v["L0_cond_W_ada"], v["L1_cond_emb_w"], v["L2_cond_ada_w"].T,
                                   v["L3_cond_film_emb_W"]], axis=1)),
        "b_mod": c(np.concatenate([v["L0_cond_b_ada"], v["L1_cond_emb_b"], v["L2_cond_ada_b"],
                                   v["L3_cond_film_emb_b"]])[None]),
        "w_in0": c(v["L0_cond_W_in"]), "w_in1": c(v["L2_cond_in_proj_w"].T),
        "w_xp0": c(v["L0_cond_W_xp"]), "w_xp1": c(v["L2_cond_x_proj_w"].T),
        "w_dt0": c(v["L0_cond_W_dt"]), "w_dt1": c(v["L2_cond_dt_proj_w"].T),
        "w_out0": c(v["L0_cond_W_out"]), "w_out1": c(v["L2_cond_out_proj_w"].T),
        "w_a_q": c(v["L1_cond_q_w"]), "w_a_k": c(v["L1_cond_k_w"]), "w_a_v": c(v["L1_cond_v_w"]),
        "w_a_out": c(v["L1_cond_out_w"]), "w_l_q": c(v["L3_cond_Wq"]), "w_l_k": c(v["L3_cond_Wk"]),
        "w_l_v": c(v["L3_cond_Wv"]), "w_l_out": c(v["L3_cond_film_out_W"]),
    }
    nc = _bacc.Bacc("TRN2", target_bir_lowering=False, num_devices=1)
    aps = {n: nc.dram_tensor(f"in_{n}", x.shape, mybir.dt.from_np(x.dtype), kind="ExternalInput").ap()
           for n, x in arrays.items()}
    out = nc.dram_tensor("out_0", (B, S, D), F32, kind="ExternalOutput").ap()
    total_loads.clear()
    pool_steps.clear()
    build(nc, aps, out)
    r = _run(nc, [{f"in_{n}": x for n, x in arrays.items()}], core_ids=[0])
    return r.results[0]["out_0"]
```

```python
from contextlib import ExitStack

import numpy as np
import concourse.bass as bass
from concourse import mybir

F32 = mybir.dt.float32
F32R = mybir.dt.float32r
I32 = mybir.dt.int32
ALU = mybir.AluOpType
ACT = mybir.ActivationFunctionType
X = mybir.AxisListType.X

P = 128
B, S, D = 32, 256, 256
GB = 2
NG = B // GB
T = GB * S
R = T // P
RB = S // P
DC = D // P
DI = 512
IC = DI // P
NS = 16
TAPS = 4
DTR = 64
H, DH = 16, 16
EPS = 1e-5
STEPS = 2 * NS
RING = 4
AHEAD = 2
BC_RING = 3
PAIRS = H // 2
HP = PAIRS // 2
EXP_CAP = 1e18

COLS = {}


def _col(name, n):
    COLS[name] = (sum(w for _, w in COLS.values()), n)


for _l in ("m0", "m1"):
    for _n, _w in (("conv_w", IC * TAPS), ("conv_b", IC), ("b_dt", IC), ("D", IC), ("A_log", IC * NS),
                   ("ln_g", DC), ("ln_b", DC)):
        _col(f"{_l}_{_n}", _w)
for _n in ("a_norm_w", "a_norm_b", "a_q_b", "a_k_b", "a_sb_w", "a_sb_b",
           "l_norm_w", "l_norm_b", "l_k_b", "l_sb_w", "l_sb_b"):
    _col(_n, DC)
NCOL = sum(w for _, w in COLS.values())
ROWS = ["a_v_b", "a_out_b", "l_q_b", "l_v_b", "l_out_b"]
SITES = ["m0", "a", "m1", "l"]
MODW = 2560
SCALE_AT = {"m0": 256, "a": 768, "m1": 1280 + 256, "l": 2048}
SHIFT_AT = {"m0": 0, "a": 1024, "m1": 1280, "l": 2304}
GATE_AT = {"m0": 512, "m1": 1280 + 512}


class Piece:

    def __init__(self, sem, name, events, banks=()):
        self.name = name
        self.events = {e: list(v) for e, v in events.items() if v}
        self.sem = {e: sem(f"{name}_{e}") for e in self.events}
        self.where = {n: (e, k + 1) for e, v in self.events.items() for k, n in enumerate(v)}
        self.bank = dict(banks)
        self.made = {e: 0 for e in self.events}

    def of(self, name):
        return self.sem[self.where[name][0]]

    def upto(self, g, name):
        e, k = self.where[name]
        return g * len(self.events[e]) + k

    def next(self, name):
        e, _ = self.where[name]
        assert self.events[e][self.made[e] % len(self.events[e])] == name, (self.name, e, name)
        self.made[e] += 1
        return self.sem[e]


def front_piece(sem, name):
    pe = ["h0", "h1"] + [f"m{m}" for m in range(2 * IC)] + ["xp"] + [f"d{m}" for m in range(IC)]
    act = ["hc0", "hc1"]
    for m in range(IC):
        act.append(f"tap{m}")
        if m:
            act.append(f"u{m - 1}")
    act += [f"u{IC - 1}"] + [f"z{m}" for m in range(IC)] + ["dtr", "bchi"]
    act += ["e0", "e1", "l0", "l1", "e2", "e3", "l2", "l3"]
    dve = ["st", "cur", "mv", "xh"] + [f"cv{m}_{s}" for m in range(IC) for s in (1, 2, 3)] + ["bclo"]
    dve += ["mn0", "mn1", "dt0", "dt1", "mn2", "mn3", "dt2", "dt3"]
    pool = ["var", "rstd"] + [f"dtx{m}" for m in range(IC)]
    uses = [("h0", 0), ("h1", 1)]
    uses += [(f"m{m}", (2 + m) % 3) for m in range(2 * IC)]
    uses += [("xp", 1)] + [(f"d{m}", (2 + m) % 3) for m in range(IC)]
    return Piece(sem, name, {"pe": pe, "act": act, "dve": dve, "pool": pool}, uses)


def back_piece(sem, name, gather):
    if gather:
        ev = {"pe": ["y0", "y1", "g0", "g1"], "act": ["yo0", "yo1"]}
        uses = [("y0", 0), ("y1", 1), ("g0", 2), ("g1", 0)]
    else:
        ev = {"pe": ["g0", "g1"]}
        uses = [("g0", 0), ("g1", 1)]
    return Piece(sem, name, ev | {"dve": ["mul0", "mul1", "x0", "x1"]}, uses)


def attn_piece(sem):
    pe, pool = ["h0", "h1", "q", "k", "v"], ["var", "rstd", "var2", "rstd2"]
    act = ["hc0", "hc1", "qhi", "khi", "v_"]
    dve = ["st", "cur", "mcur", "mv", "mbias", "xh", "mval", "mhi", "mlo", "qlo", "klo"]
    uses = [("h", 0), ("q", 1), ("k", 2), ("v", 0)]
    for z in range(2):
        ps = range(z * HP, (z + 1) * HP)
        pe += [f"r{p}" for p in ps] + [f"s{p}{t}" for p in ps for t in range(2)] + [f"nm{z}"]
        act += [f"rc{p}" for p in ps] + [f"nmhi{z}"]
        dve += [f"mx{p}{t}" for p in ps for t in range(2)] + [f"nmlo{z}"]
        uses += [(f"r{p}", p % 3) for p in ps]
        uses += [(f"s{p}{t}", (2 * p + t) % 3) for p in ps for t in range(2)] + [(f"nm{z}", 0)]
        for p in range(z * HP, (z + 1) * HP + 1):
            if p < (z + 1) * HP:
                pe += [f"t{p}0", f"t{p}1"]
                act += [f"x{p}0", f"x{p}1"]
                uses += [(f"t{p}0", 0), (f"t{p}1", 1)]
                if p % 2:
                    uses += [(f"Y{p // 2}", 2)]
            if p > z * HP:
                pe.append(f"pv{p - 1}")
                if p % 2 == 0:
                    act.append(f"ye{p // 2 - 1}")
    pe += ["o0", "o1", "h20", "h21", "out"]
    dve += ["rec0", "yn0", "rec1", "yn1", "st2", "mv2", "xh2", "xo"]
    act += ["hc20", "hc21"]
    uses += [("o0", 0), ("o1", 1), ("h2", 2), ("out", 0)]
    return Piece(sem, "attn", {"pe": pe, "act": act, "dve": dve, "pool": pool}, uses)


def linattn_piece(sem):
    pe = ["h0", "h1", "q", "k", "v", "qt", "kt", "at", "y", "h20", "h21", "out"]
    act = ["hc0", "hc1", "qe", "v_", "ke0", "ke1", "qtc", "ktc", "hc20", "hc21"]
    dve = ["st", "cur", "kcur", "mv", "kmask", "masked", "nmask", "xh", "qm", "qs", "kb0", "kb1", "km", "qsum", "qrec", "qn", "krec", "kn0", "kn1",
           "atm", "st2", "mv2", "xh2", "xo"]
    pool = ["var", "rstd", "var2", "rstd2"]
    uses = [("h", 0), ("q", 1), ("k", 2), ("v", 0), ("qt", 1),
            ("kt", 2), ("at", 0), ("y", 1), ("h2", 2), ("out", 0)]
    return Piece(sem, "linattn", {"pe": pe, "act": act, "dve": dve, "pool": pool}, uses)


def scan_piece(sem, name):
    pe, act, dve = ["bc0", "bc1", "bc2"], [f"exp{q}" for q in range(AHEAD)], []
    for s in range(STEPS):
        dve += [f"dbx{s}", f"scan{s}", f"hc{s}"]
        if s == NS + 2:
            dve += ["yg0", "yg1"]
        if s:
            pe += [f"bc{k}" for k in (2 * s + 1, 2 * s + 2) if k < 2 * STEPS]
            pe += ["du0"] * (s == 2)
            pe += ["du1"] * (s == NS + 3) + [f"red{(s - 3) // 2}"] * (s % 2 and s >= 3)
        if s + AHEAD < STEPS:
            act.append(f"exp{s + AHEAD}")
    return Piece(sem, name, {"pe": pe + [f"red{STEPS // 2 - 1}"], "act": act, "dve": dve + ["yg2", "yg3"],
                             "pool": [f"add{q}" for q in range(STEPS // 2)]})


FRONT_PH, REST_PH, BACK_PH, ATTN_PH, LIN_PH = 11, 2, 2, 28, 9
WEIGHT = {
          "keep": [1],
          "rest0": [3.52, 0.8],
          "rest1": [2.5, 1.28],
          "front0": [1.6, 1.25, 1, 1, 1, 1, 1, 1, 1, 1, 1],
          "front1": [1, 1, 1, 1, 1, 1, 1, 1.6, 1, 1.25, 1],
          "back0": [1.2, 1.5],
          "back1": [1.25, 1],
          "attn_a": [1, 1, 1, 1, 1, 1, 1, 1, 1, 1, 1, 1, 1, 1, 1, 1, 1, 1, 1, 1, 1, 1, 1, 1, 1, 1, 1, 1],
          "attn_b": [1, 1, 1.25, 1, 1, 1, 1, 1, 0.8, 1, 1, 1, 1, 1, 1, 1, 1, 1, 1, 1, 1, 1, 1, 1, 1, 1, 1,
              1.6],
          "lin_a": [1, 1, 1, 1, 1, 1, 1, 1, 1],
          "lin_b": [1, 1, 1, 1, 1, 1, 1, 1, 1]}
AT = {"spread_c": -0.578, "spread_b": 0.05, "reduce": 0.5, "decay": -0.24, "scan": 0.33, "times_c": 0.67, "add": 1.109}
LAG = {"pe": 0.389, "act": 0.7, "dve": 0.9, "pool": 0.9}

R_FREE = ["v_", "qlo", "klo", "rc0", "x31", "ye1", "x30", "rc4"]
SIDE = [("rest0", 0, 0), ("attn_b", -1, 0), ("back1", -2, 0), ("lin_a", -2, 0), ("front1", -1, 0),
        ("rest1", -1, 1), ("lin_b", -2, 1), ("keep", -1, 1), ("back0", 0, 1), ("attn_a", 0, 1), ("front0", 1, 1)]
SCAN = [("scan0", 0), ("scan1", -1)]
FIRST_IT, LAST_IT, LOOP_FROM, LOOP_TO = -1, NG + 1, 3, NG - 1


def alive(i, off):
    return not isinstance(i, int) or 0 <= i + off < NG


def before_side(i, at):
    while True:
        at -= 1
        if at < 0:
            at, i = len(SIDE) - 1, i - 1
        if isinstance(i, int) and i < FIRST_IT:
            return None
        if alive(i, SIDE[at][1]):
            return SIDE[at][0], i + SIDE[at][1]


def before_scan(i, at):
    while True:
        at -= 1
        if at < 0:
            at, i = 1, i - 1
        if isinstance(i, int) and i < FIRST_IT:
            return None
        if alive(i, SCAN[at][1]):
            return SCAN[at][0], i + SCAN[at][1]


def build(nc, a, out):
    ctx = ExitStack()
    with ctx:
        def sb(name, shape, dt=F32):
            return ctx.enter_context(nc.sbuf_tensor(name, shape, dt))

        def sem(name):
            return ctx.enter_context(nc.semaphore(name))

        w_in = [sb(f"w_in{l}", [P, DC, 2 * DI]) for l in range(2)]
        w_xp = [sb(f"w_xp{l}", [P, IC, DTR + 2 * NS]) for l in range(2)]
        w_dt = sb("w_dt", [2 * DTR, DI])
        w_out = [sb(f"w_out{l}", [P, IC, D]) for l in range(2)]
        w_att = {n: sb(f"w_{n}", [P, DC, D]) for n in ("a_q", "a_k", "a_v", "a_out", "l_q", "l_k", "l_v", "l_out")}
        cols = sb("cols", [P, NCOL])
        rows = sb("rows", [97, 2, D])
        ident = sb("ident", [P, P])
        pick = sb("pick", [P, 2 * NS], F32R)
        onehot = sb("onehot", [P, RB, S])
        stack = sb("stack", [P, 4, 4, P], F32R)
        blocks = sb("blocks", [P, P])
        diag_d = sb("diag_d", [P, 2, IC, P])
        a_neg = sb("a_neg", [P, 2, IC * NS])
        coef = sb("coef", [P, len(SITES) * 2 * DC, B])
        amask = sb("amask", [P, B, RB])
        kmask_col = sb("kmask_col", [P, B, RB], I32)
        ones = sb("ones", [P, P])
        one_col = sb("one_col", [P, 1])
        nhalf = sb("nhalf", [P, R])
        eps = sb("eps", [P, R])
        u = sb("u", [P, IC, T])
        dt_ = [sb(f"dt{l}", [P, IC, T]) for l in range(2)]
        dtx = [sb(f"dtx{l}", [P, IC, T]) for l in range(2)]
        sz = [sb(f"sz{l}", [P, IC, T]) for l in range(2)]
        bcr = [sb(f"bcr{l}", [P, T], F32R) for l in range(2)]
        da = [sb(f"da{k}", [P, 2, GB, S]) for k in range(AHEAD + 1)]
        hw = [sb(f"hw{k}", [P, 2, T]) for k in range(RING)]
        x_b = sb("x_b", [P, R, D])
        x_c = sb("x_c", [P, R, D])
        gate = sb("gate", [P, GB, D])
        xhat = sb("xhat", [P, R, D])
        hT = sb("hT", [P, DC, T])
        stats = sb("stats", [P, R, 6])
        mv = sb("mv", [P, R, 2])
        rstd = sb("rstd", [P, R])
        cur = sb("cur", [P, 2, DC, GB])
        xd = sb("xd", [2 * DTR, T])
        qhl = sb("qhl", [P, 2, DC, S], F32R)
        khl = sb("khl", [P, 2, DC, S], F32R)
        qk = sb("qk", [P, HP, 2, S], F32R)
        va = sb("va", [P, RB, H, 32])
        mx = sb("mx", [P, RB, H])
        nm = sb("nm", [P, S], F32R)
        mb = sb("mb", [P, S], F32R)
        mrow = sb("mrow", [1, S])
        mcur = sb("mcur", [P, 2, RB])
        pt2 = sb("pt2", [P, 2, T])
        pt = [(u if k < 2 else pt2)[:, k % 2, :].rearrange("p (h s) -> p h s", h=2) for k in range(4)]
        yT = sb("yT", [P, H // 4, S])
        rec = sb("rec", [P, 2, RB, H])
        kmrow = sb("kmrow", [P, S], I32)
        kT = yT[:, 0:2, :]
        kmb = yT[:, 2, :]
        qrow = pt[0]
        krow = pt[1]
        vrow = pt[2]
        qT = pt[3]
        attnT = hT[:, :, S:S + P]
        small = sb("small", [P, 8])
        qmx = rec[:, 0, :, :]
        qrs = rec[:, 1, :, :]

        ps = ctx.enter_context(nc.psum_tensor("ps", [P, 8, T], F32))
        yps = ps[:, 0:2, :]
        bc = [ps[:, 2 + k, :] for k in range(BC_RING)]
        side = [ps[:, 2 + BC_RING + k, :] for k in range(3)]

        gates_dram = nc.dram_tensor("gates_scratch", (2, B, D), F32, kind="Internal").ap()

        loaded = sem("loaded")
        gates_out = sem("gates_out")
        xin = sem("xin")
        xb_in = sem("residual_in")
        gin = [sem("gate0_in"), sem("gate1_in")]
        min_ = sem("mask_row_in")
        kmin = sem("key_mask_in")
        stored = sem("stored")
        p_pool, p_act, p_pe, p_dve = (sem(f"prologue_{e}") for e in ("pool", "act", "pe", "dve"))
        fr = [front_piece(sem, "front0"), front_piece(sem, "front1")]
        bk = [back_piece(sem, "back0", True), back_piece(sem, "back1", False)]
        at = attn_piece(sem)
        li = linattn_piece(sem)
        kp = Piece(sem, "keep", {"act": ["xc"]})
        sc = [scan_piece(sem, "scan0"), scan_piece(sem, "scan1")]

        def flat(t, n):
            return t[:].rearrange("p a b -> p (a b)")[:, 0:n]

        w_mod = [dt_[0], dt_[1], dtx[0], dtx[1], sz[0]]
        mod_rows = hw[0]
        mod_rows2 = hw[1]
        mod_rows3 = hw[2]
        c_raw = x_b[:].rearrange("p a b -> p (a b)")[:, 0:4 * B].rearrange("p (k b) -> p k b", b=B)
        c_act = x_c[:].rearrange("p a b -> p (a b)")[:, 0:4 * B].rearrange("p (k b) -> p k b", b=B)
        mod_bias = [da[0][:].rearrange("p a b c -> p a (b c)"), da[1][:].rearrange("p a b c -> p a (b c)"),
                    da[2][:].rearrange("p a b c -> p a (b c)")]
        modT = sz[1][:].rearrange("p a b -> p (a b)")[:, 0:16 * B].rearrange("p (k b) -> p k b", b=B)
        idx_i = kmrow
        idx_f = yT[:, 0, :]
        iot_i = sb("iot_i", [P, RB], I32)
        iot_f = sb("iot_f", [P, RB])
        stack_f = xhat[:].rearrange("p a b -> p (a b)")
        stack_g = hT[:].rearrange("p a b -> p (a b)")
        pick_f = yT[:, 3, 0:2 * NS]

        def col(name, k=0, n=1):
            at0, _ = COLS[name]
            return cols[:, at0 + k:at0 + k + n]

        def rowb(name):
            r = ROWS.index(name)
            return ones[32 * (r % 4):32 * (r % 4) + 1, :], rows[32 * (r % 4):32 * (r % 4) + 1, r // 4, :]

        xv = a["x"].rearrange("b (k p) d -> p (b k) d", p=P)
        ov = out.rearrange("b (k p) d -> p (b k) d", p=P)
        x_src, x_res = [xhat, x_b], [x_b, x_c]
        busy = {}

        def number(name, g):
            return {"keep": (kp, g), "rest0": (fr[0], g), "rest1": (fr[1], g), "front0": (fr[0], g), "front1": (fr[1], g), "back0": (bk[0], g), "back1": (bk[1], g),
                    "attn_a": (at, 2 * g), "attn_b": (at, 2 * g + 1), "lin_a": (li, 2 * g),
                    "lin_b": (li, 2 * g + 1), "scan0": (sc[0], g), "scan1": (sc[1], g)}[name]

        def after(eng, prev):
            if prev is not None:
                kind, n = number(*prev)
                for e, v in kind.events.items():
                    eng.wait_ge(kind.sem[e], (n + 1) * len(v))

        def u_is_free(eng, half):
            if busy["scan"] is not None:
                kind, n = number(*busy["scan"])
                eng.wait_ge(kind.of(f"du{half}"), kind.upto(n, f"du{half}"))

        def loads_of_piece(act, kind, v, g, prev):
            if prev is not None and prev[0] in ("lin_a", "lin_b"):
                store_result(act, prev[1], 0 if prev[0] == "lin_a" else 1)
            if kind == "front" and v == 0:
                act.dma_start(xhat[:, :, :], xv[:, bass.ds(g * R, R), :]).then_inc(xin, 16)
            if kind == "back":
                for b in range(GB):
                    act.dma_start(gate[:, b, :], gates_dram[v, bass.ds(g * GB + b, 1), :].broadcast_to([P, D]))\
                       .then_inc(gin[v], 16)
                if v == 0:
                    act.dma_start(x_b[:, :, :], xv[:, bass.ds(g * R, R), :]).then_inc(xb_in, 16)
            if kind == "attn":
                act.dma_start(mrow[:, :], a["amask_row"][bass.ds(2 * g + v, 1), :]).then_inc(min_, 16)
            if kind == "lin":
                act.dma_start(kmrow[:, :], a["kmask_row"][bass.ds(2 * g + v, 1), :].broadcast_to([P, S]))\
                   .then_inc(kmin, 16)

        def store_result(act, g, b):
            act.dma_start(ov[:, bass.ds((GB * g + b) * RB, RB), :], x_c[:, RB * b:RB * (b + 1), :])\
               .then_inc(stored, 16)

        def ln_stats(dve, pc, n, src, tiles, tag="", also=None):
            for r in range(tiles):
                ins = nc.vector.bn_stats(stats[:, r, :], src(r))
            ins.then_inc(pc.next("st" + tag), 1)
            if also is not None:
                also()
            dve.wait_ge(pc.of("st" + tag), pc.upto(n, "st" + tag))
            nc.vector.tensor_copy(small[:, 7:8], one_col[:, 0:1])
            for r in range(tiles):
                ins = nc.vector.bn_aggr(mv[:, r, :], stats[:, r, :])
            ins.then_inc(pc.next("mv" + tag), 1)

        def ln_rstd(pool, pc, n, tiles, tag=""):
            pool.wait_ge(pc.of("mv" + tag), pc.upto(n, "mv" + tag))
            nc.gpsimd.tensor_tensor(rstd[:, 0:tiles], mv[:, 0:tiles, 1], eps[:, 0:tiles], ALU.add).then_inc(pc.next("var" + tag), 1)
            pool.wait_ge(pc.of("var" + tag), pc.upto(n, "var" + tag))
            nc.gpsimd.tensor_tensor(rstd[:, 0:tiles], rstd[:, 0:tiles], nhalf[:, 0:tiles], ALU.pow).then_inc(pc.next("rstd" + tag), 1)

        def ln_apply(dve, pc, n, src, tiles, tag=""):
            dve.wait_ge(pc.of("rstd" + tag), pc.upto(n, "rstd" + tag))
            for r in range(tiles):
                ins = nc.vector.tensor_scalar(xhat[:, r, :], src(r), mv[:, r, 0:1], rstd[:, r:r + 1],
                                              ALU.subtract, ALU.mult)
            ins.then_inc(pc.next("xh" + tag), 1)

        def front_tensor(pe, l, g, prev):
            pc = fr[l]
            after(pe, prev)
            yield
            yield
            pe.wait_ge(pc.of("xh"), pc.upto(g, "xh"))
            for c in range(DC):
                for b in range(GB):
                    for k in range(RB):
                        if l == 0:
                            ins = nc.tensor.matmul(side[pc.bank[f"h{c}"]][:, b * S:(b + 1) * S],
                                                   xhat[:, RB * b + k, c * P:(c + 1) * P], onehot[:, k, :],
                                                   start=(k == 0), stop=(k == RB - 1))
                        else:
                            ins = nc.tensor.transpose(
                                side[pc.bank[f"h{c}"]][:, b * S + k * P:b * S + (k + 1) * P],
                                xhat[:, RB * b + k, c * P:(c + 1) * P], ident[:, :])
                ins.then_inc(pc.next(f"h{c}"), 1)
            yield
            pe.wait_ge(pc.of("hc1"), pc.upto(g, "hc1"))
            for m in range(2 * IC):
                if m >= 3:
                    free = f"cv{m - 3}_3" if m - 3 < IC else f"z{m - 3 - IC}"
                    pe.wait_ge(pc.of(free), pc.upto(g, free))
                for k in range(DC):
                    ins = nc.tensor.matmul(side[pc.bank[f"m{m}"]], w_in[l][:, k, m * P:(m + 1) * P],
                                           hT[:, k, :], start=(k == 0), stop=(k == DC - 1))
                ins.then_inc(pc.next(f"m{m}"), 1)
                if m % 2:
                    yield
            yield
            pe.wait_ge(pc.of("z1"), pc.upto(g, "z1"))
            for c in range(IC):
                ins = nc.tensor.matmul(side[pc.bank["xp"]][0:DTR + 2 * NS, :], w_xp[l][:, c, :], u[:, c, :],
                                       start=(c == 0), stop=(c == IC - 1))
            ins.then_inc(pc.next("xp"), 1)
            yield
            pe.wait_ge(pc.of("dtr"), pc.upto(g, "dtr"))
            for m in range(2):
                low_rank(l, m)
            yield
            yield

        def low_rank(l, m):
            pc, lr = fr[l], slice(l * DTR, (l + 1) * DTR)
            nc.tensor.matmul(side[pc.bank[f"d{m}"]], w_dt[lr, m * P:(m + 1) * P], xd[lr, :],
                             start=True, stop=True).then_inc(pc.next(f"d{m}"), 1)

        def rest_tensor(pe, l, g, prev):
            pc = fr[l]
            pe.wait_ge(pc.of("bclo"), pc.upto(g, "bclo"))
            low_rank(l, 2)
            pe.wait_ge(pc.of("dt0"), pc.upto(g, "dt0"))
            low_rank(l, 3)
            yield
            yield

        def front_scalar(act, l, g, prev):
            pc = fr[l]
            after(act, prev)
            loads_of_piece(act, "front", l, g, prev)
            yield
            yield
            for c in range(DC):
                act.wait_ge(pc.of(f"h{c}"), pc.upto(g, f"h{c}"))
                if c == 0:
                    act.wait_ge(pc.of("cur"), pc.upto(g, "cur"))
                for b in range(GB):
                    ins = nc.scalar.activation(hT[:, c, b * S:(b + 1) * S],
                                               side[pc.bank[f"h{c}"]][:, b * S:(b + 1) * S], ACT.Identity,
                                               bias=cur[:, 1, c, b:b + 1], scale=cur[:, 0, c, b:b + 1])
                ins.then_inc(pc.next(f"hc{c}"), 1)
            yield

            def silu_u(m):
                act.wait_ge(pc.of(f"cv{m}_3"), pc.upto(g, f"cv{m}_3"))
                nc.scalar.activation(u[:, m, :], u[:, m, :], ACT.Silu).then_inc(pc.next(f"u{m}"), 1)

            for m in range(IC):
                act.wait_ge(pc.of(f"m{m}"), pc.upto(g, f"m{m}"))
                if m == 0:
                    u_is_free(act, 1)
                nc.scalar.activation(u[:, m, :], side[pc.bank[f"m{m}"]], ACT.Identity,
                                               bias=col(f"m{l}_conv_b", m),
                                               scale=col(f"m{l}_conv_w", m * TAPS + TAPS - 1)).then_inc(pc.next(f"tap{m}"), 1)
                if m:
                    silu_u(m - 1)
                if m % 2:
                    yield
            silu_u(IC - 1)
            for m in range(IC):
                act.wait_ge(pc.of(f"m{IC + m}"), pc.upto(g, f"m{IC + m}"))
                nc.scalar.activation(sz[l][:, m, :], side[pc.bank[f"m{IC + m}"]], ACT.Silu).then_inc(pc.next(f"z{m}"), 1)
                if m % 2:
                    yield
            yield
            act.wait_ge(pc.of("xp"), pc.upto(g, "xp"))
            nc.scalar.activation(xd[l * DTR:(l + 1) * DTR, :], side[pc.bank["xp"]][0:DTR, :], ACT.Copy).then_inc(pc.next("dtr"), 1)
            nc.scalar.activation(bcr[l][0:32, :], side[pc.bank["xp"]][DTR:DTR + 32, :], ACT.Copy).then_inc(pc.next("bchi"), 1)
            yield

            for m in range(2):
                exp_dt(act, l, g, m)
            yield
            for m in range(2):
                ln_dt(act, l, g, m)
            yield

        def exp_dt(act, l, g, m):
            pc = fr[l]
            act.wait_ge(pc.of(f"d{m}"), pc.upto(g, f"d{m}"))
            nc.scalar.activation(dt_[l][:, m, :], side[pc.bank[f"d{m}"]], ACT.Exp,
                                 bias=col(f"m{l}_b_dt", m)).then_inc(pc.next(f"e{m}"), 1)

        def ln_dt(act, l, g, m):
            pc = fr[l]
            act.wait_ge(pc.of(f"mn{m}"), pc.upto(g, f"mn{m}"))
            nc.scalar.activation(dt_[l][:, m, :], dt_[l][:, m, :], ACT.Ln, bias=one_col[:, 0:1])\
              .then_inc(pc.next(f"l{m}"), 1)

        def rest_scalar(act, l, g, prev):
            for m in (2, 3):
                exp_dt(act, l, g, m)
            yield
            for m in (2, 3):
                ln_dt(act, l, g, m)
            yield

        def front_vector(dve, l, g, prev):
            pc = fr[l]
            after(dve, prev)
            src = lambda r: x_src[l][:, r, :]
            if l == 0:
                dve.wait_ge(xin, 16 * g + 16)
            ln_stats(dve, pc, g, src, R, also=lambda: copy_coef(pc, "m0" if l == 0 else "m1", g))
            yield
            ln_apply(dve, pc, g, src, R)
            yield
            yield
            for m in range(IC):
                bank = side[pc.bank[f"m{m}"]].rearrange("p (b s) -> p b s", b=GB)
                um = u[:, m, :].rearrange("p (b s) -> p b s", b=GB)
                for s in range(1, TAPS):
                    dve.wait_ge(pc.of(f"cv{m}_{s - 1}" if s > 1 else f"tap{m}"), pc.upto(g, f"cv{m}_{s - 1}" if s > 1 else f"tap{m}"))
                    nc.vector.scalar_tensor_tensor(
                        out=um[:, :, s:], in0=bank[:, :, 0:S - s], scalar=col(f"m{l}_conv_w", m * TAPS + TAPS - 1 - s),
                        in1=um[:, :, s:], op0=ALU.mult, op1=ALU.add).then_inc(pc.next(f"cv{m}_{s}"), 1)
                if m % 2:
                    yield
            yield
            yield
            yield
            dve.wait_ge(pc.of("bchi"), pc.upto(g, "bchi"))
            nc.vector.tensor_tensor(bcr[l][32:64, :], side[pc.bank["xp"]][DTR:DTR + 32, :],
                                              bcr[l][0:32, :], ALU.subtract).then_inc(pc.next("bclo"), 1)
            yield

            for m in range(2):
                cap(dve, l, g, m)
            yield
            for m in range(2):
                step_size(dve, l, g, m)
            yield

        def cap(dve, l, g, m):
            pc = fr[l]
            dve.wait_ge(pc.of(f"e{m}"), pc.upto(g, f"e{m}"))
            nc.vector.tensor_scalar(dt_[l][:, m, :], dt_[l][:, m, :], EXP_CAP, None, ALU.min)\
              .then_inc(pc.next(f"mn{m}"), 1)

        def step_size(dve, l, g, m):
            pc = fr[l]
            dve.wait_ge(pc.of(f"l{m}"), pc.upto(g, f"l{m}"))
            nc.vector.scalar_tensor_tensor(
                out=dt_[l][:, m, :], in0=side[pc.bank[f"d{m}"]], scalar=col(f"m{l}_b_dt", m),
                in1=dt_[l][:, m, :], op0=ALU.add, op1=ALU.max).then_inc(pc.next(f"dt{m}"), 1)

        def rest_vector(dve, l, g, prev):
            for m in (2, 3):
                cap(dve, l, g, m)
            yield
            for m in (2, 3):
                step_size(dve, l, g, m)
            yield

        def front_pool(pool, l, g, prev):
            pc = fr[l]
            after(pool, prev)
            yield
            ln_rstd(pool, pc, g, R)
            for _ in range(FRONT_PH - 2):
                yield
            for m in range(2):
                times_u(pool, l, g, m)
            yield

        def times_u(pool, l, g, m):
            pc = fr[l]
            pool.wait_ge(pc.of(f"dt{m}"), pc.upto(g, f"dt{m}"))
            nc.gpsimd.tensor_tensor(dtx[l][:, m, :], dt_[l][:, m, :], u[:, m, :], ALU.mult)\
              .then_inc(pc.next(f"dtx{m}"), 1)

        def rest_pool(pool, l, g, prev):
            yield
            for m in (2, 3):
                times_u(pool, l, g, m)
            yield

        def copy_coef(pc, site, g):
            c0 = SITES.index(site) * 2 * DC
            nc.vector.tensor_copy(cur[:, :, :, :].rearrange("p a c b -> p (a c) b"),
                                            coef[:, c0:c0 + 2 * DC, bass.ds(g * GB, GB)]).then_inc(pc.next("cur"), 1)

        def reduce(pe, l, g, q):
            pc = sc[l]
            pe.wait_ge(pc.of(f"add{q}"), pc.upto(g, f"add{q}"))
            for cc in range(2):
                ins = nc.tensor.matmul(yps[:, cc, :], ident[:, :], hw[(2 * q + 1) % RING][:, cc, :],
                                       start=False, stop=(2 * q % NS == NS - 2))
            ins.then_inc(pc.next(f"red{q}"), 1)

        def last_pair(pe, l, g):
            reduce(pe, l, g, STEPS // 2 - 1)

        def scan_tensor(pe, l, g, before, follows):
            pc = sc[l]

            def spread(k):
                if k >= BC_RING:
                    used = (f"hc{(k - BC_RING) // 2}" if (k - BC_RING) % 2 else f"dbx{(k - BC_RING) // 2}")
                    pe.wait_ge(pc.of(used), pc.upto(g, used))
                row = k // 2 % NS + NS * (k % 2)
                nc.tensor.matmul(bc[k % BC_RING], pick[:, row:row + 1].broadcast_to([P, P]), bcr[l][:, :],
                                 start=True, stop=True).then_inc(pc.next(f"bc{k}"), 1)

            def skip_term(half):
                for cc in range(2):
                    c = 2 * half + cc
                    ins = nc.tensor.matmul(yps[:, cc, :], diag_d[:, l, c, :], u[:, c, :], start=True, stop=False)
                ins.then_inc(pc.next(f"du{half}"), 1)

            yield 0
            pe.wait_ge(fr[l].of("bchi"), fr[l].upto(g, "bchi"))
            pe.wait_ge(fr[l].of("bclo"), fr[l].upto(g, "bclo"))
            if before is not None:
                kind, n = number(*before)
                pe.wait_ge(kind.of(f"hc{STEPS - 1}"), kind.upto(n, f"hc{STEPS - 1}"))
            for k in range(BC_RING):
                spread(k)
            if follows:
                last_pair(pe, 1 - l, before[1])
            for s in range(1, STEPS):
                yield s + AT["spread_c"]
                spread(2 * s + 1)
                if s + 1 < STEPS:
                    yield s + AT["spread_b"]
                    spread(2 * s + 2)
                if s == 2:
                    if before is not None:
                        pe.wait_ge(kind.of("yg3"), kind.upto(n, "yg3"))
                    skip_term(0)
                if s == NS + 3:
                    pe.wait_ge(pc.of("yg1"), pc.upto(g, "yg1"))
                    skip_term(1)
                if s % 2 and s >= 3:
                    yield s + AT["reduce"]
                    reduce(pe, l, g, (s - 3) // 2)

        def scan_scalar(act, l, g, before, follows):
            pc = sc[l]

            def decay(q):
                if q % NS == 0:
                    last = f"dt{2 * (q // NS) + 1}"
                    act.wait_ge(fr[l].of(last), fr[l].upto(g, last))
                if q > AHEAD:
                    act.wait_ge(pc.of(f"scan{q - AHEAD - 1}"), pc.upto(g, f"scan{q - AHEAD - 1}"))
                for cc in range(2):
                    c = 2 * (q // NS) + cc
                    ins = nc.scalar.activation(
                        da[q % (AHEAD + 1)][:, cc, :, 1:S],
                        dt_[l][:, c, :].rearrange("p (b s) -> p b s", b=GB)[:, :, 1:S],
                        ACT.Exp, scale=a_neg[:, l, c * NS + q % NS:c * NS + q % NS + 1])
                ins.then_inc(pc.next(f"exp{q}"), 1)

            yield 0
            if before is not None:
                kind, n = number(*before)
                act.wait_ge(kind.of(f"scan{STEPS - 1}"), kind.upto(n, f"scan{STEPS - 1}"))
            for q in range(AHEAD):
                decay(q)
            for s in range(STEPS - AHEAD):
                yield s + AT["decay"]
                decay(s + AHEAD)

        def gated(dve, l, g, half):
            pc = sc[l]
            last = f"red{NS // 2 * (half + 1) - 1}"
            dve.wait_ge(pc.of(last), pc.upto(g, last))
            for cc in range(2):
                c = 2 * half + cc
                nc.vector.tensor_tensor(dtx[l][:, c, :], yps[:, cc, :], sz[l][:, c, :], ALU.mult)\
                  .then_inc(pc.next(f"yg{c}"), 1)

        def scan_vector(dve, l, g, before, follows):
            pc = sc[l]
            yield 0
            for s in range(STEPS):
                half, tile = s // NS, hw[s % RING]
                b_n = bc[2 * s % BC_RING].unsqueeze(1).broadcast_to([P, 2, T])
                c_n = bc[(2 * s + 1) % BC_RING].unsqueeze(1).broadcast_to([P, 2, T])
                yield s
                if s % NS == 0:
                    last = f"dtx{2 * half + 1}"
                    dve.wait_ge(fr[l].of(last), fr[l].upto(g, last))
                dve.wait_ge(pc.of(f"bc{2 * s}"), pc.upto(g, f"bc{2 * s}"))
                if s >= RING:
                    used = (f"red{(s - RING) // 2}" if s % 2 else f"add{(s - RING) // 2}")
                    dve.wait_ge(pc.of(used), pc.upto(g, used))
                elif before is not None:
                    kind, k = number(*before)
                    used = (f"red{(STEPS + s - RING) // 2}" if s % 2 else f"add{(STEPS + s - RING) // 2}")
                    dve.wait_ge(kind.of(used), kind.upto(k, used))
                nc.vector.tensor_tensor(tile[:, :, :], dtx[l][:, 2 * half:2 * half + 2, :], b_n, ALU.mult)\
                  .then_inc(pc.next(f"dbx{s}"), 1)
                yield s + AT["scan"]
                dve.wait_ge(pc.of(f"exp{s}"), pc.upto(g, f"exp{s}"))
                dve.wait_ge(pc.of(f"dbx{s}"), pc.upto(g, f"dbx{s}"))
                ht = tile[:, :, :].rearrange("p c t -> p (c t)")
                nc.vector.tensor_tensor_scan(
                    ht, da[s % (AHEAD + 1)][:, :, :, :].rearrange("p c b s -> p (c b s)"), ht, 0.0, ALU.mult, ALU.add)\
                  .then_inc(pc.next(f"scan{s}"), 1)
                yield s + AT["times_c"]
                dve.wait_ge(pc.of(f"bc{2 * s + 1}"), pc.upto(g, f"bc{2 * s + 1}"))
                dve.wait_ge(pc.of(f"scan{s}"), pc.upto(g, f"scan{s}"))
                nc.vector.tensor_tensor(tile[:, :, :], tile[:, :, :], c_n, ALU.mult).then_inc(pc.next(f"hc{s}"), 1)
                if s == 1 and follows:
                    gated(dve, 1 - l, before[1], 1)
                if s == NS + 2:
                    gated(dve, l, g, 0)

        def scan_pool(pool, l, g, before, follows):
            pc = sc[l]
            for s in range(1, STEPS, 2):
                yield s + AT["add"]
                pool.wait_ge(pc.of(f"hc{s}"), pc.upto(g, f"hc{s}"))
                nc.gpsimd.tensor_tensor(hw[s % RING][:, :, :], hw[(s - 1) % RING][:, :, :], hw[s % RING][:, :, :],
                                        ALU.add).then_inc(pc.next(f"add{s // 2}"), 1)

        def back_tensor(pe, l, g, prev):
            pc = bk[l]
            after(pe, prev)
            pe.wait_ge(sc[l].of("yg3"), sc[l].upto(g, "yg3"))
            for b in range(GB):
                key = f"y{b}" if l == 0 else f"g{b}"
                for k in range(RB):
                    r = RB * b + k
                    for c in range(IC):
                        ins = nc.tensor.matmul(side[pc.bank[key]][:, k * D:(k + 1) * D],
                                               dtx[l][:, c, r * P:(r + 1) * P], w_out[l][:, c, :],
                                               start=(c == 0), stop=(c == IC - 1))
                ins.then_inc(pc.next(key), 1)
            yield
            if l == 0:
                for b in range(GB):
                    pe.wait_ge(pc.of(f"yo{b}"), pc.upto(g, f"yo{b}"))
                    for j in range(RB):
                        for k in range(RB):
                            ins = nc.tensor.matmul(side[pc.bank[f"g{b}"]][:, j * D:(j + 1) * D],
                                                   onehot[:, k, j * P:(j + 1) * P], xhat[:, RB * b + k, :],
                                                   start=(k == 0), stop=(k == RB - 1))
                    ins.then_inc(pc.next(f"g{b}"), 1)
            yield

        def back_scalar(act, l, g, prev):
            after(act, prev)
            loads_of_piece(act, "back", l, g, prev)
            if l == 0:
                pc = bk[l]
                for b in range(GB):
                    act.wait_ge(pc.of(f"y{b}"), pc.upto(g, f"y{b}"))
                    nc.scalar.activation(
                        xhat[:, RB * b:RB * (b + 1), :].rearrange("p r d -> p (r d)"),
                        side[pc.bank[f"y{b}"]], ACT.Copy).then_inc(pc.next(f"yo{b}"), 1)
            yield
            yield

        def back_vector(dve, l, g, prev):
            pc = bk[l]
            after(dve, prev)
            yield
            tmp = hT[:, :, :].rearrange("p c (r d) -> p (c r) d", d=D)
            dve.wait_ge(gin[l], 16 * GB * g + 16 * GB)
            for b in range(GB):
                dve.wait_ge(pc.of(f"g{b}"), pc.upto(g, f"g{b}"))
                nc.vector.tensor_tensor(
                    tmp[:, RB * b:RB * (b + 1), :],
                    side[pc.bank[f"g{b}"]].rearrange("p (r d) -> p r d", r=RB),
                    gate[:, b, :].unsqueeze(1).broadcast_to([P, RB, D]), ALU.mult).then_inc(pc.next(f"mul{b}"), 1)
            if l == 0:
                dve.wait_ge(xb_in, 16 * g + 16)
            for b in range(GB):
                dve.wait_ge(pc.of(f"mul{b}"), pc.upto(g, f"mul{b}"))
                rb = slice(RB * b, RB * (b + 1))
                nc.vector.tensor_tensor(x_res[l][:, rb, :], x_res[l][:, rb, :], tmp[:, rb, :], ALU.add).then_inc(pc.next(f"x{b}"), 1)
            yield

        def keep_scalar(act, l, g, prev):
            after(act, prev)
            loads_of_piece(act, "keep", l, g, prev)
            if not (isinstance(g, int) and g == 0):
                act.wait_ge(stored, 16 * GB * g)
            nc.scalar.activation(x_c[:, :, :].rearrange("p r d -> p (r d)"),
                                 x_b[:, :, :].rearrange("p r d -> p (r d)"), ACT.Copy).then_inc(kp.next("xc"), 1)
            yield

        def nothing(eng, l, g, prev):
            yield

        def tail_tensor(pe, pc, n, w, bias, bank_free):
            pe.wait_ge(pc.of("xh2"), pc.upto(n, "xh2"))
            pe.wait_ge(pc.of(bank_free[0]), pc.upto(n, bank_free[0]))
            transpose_rows(pc, "h2")
            yield
            pe.wait_ge(pc.of(bank_free[1]), pc.upto(n, bank_free[1]))
            bias_rows(pc, "out", bias)
            project_rows(pe, pc, n, "out", w, "hc2")
            yield

        def transpose_rows(pc, key):
            for c in range(DC):
                for k in range(RB):
                    ins = nc.tensor.transpose(side[pc.bank[key]][:, c * S + k * P:c * S + (k + 1) * P],
                                              xhat[:, k, c * P:(c + 1) * P], ident[:, :])
                ins.then_inc(pc.next(f"{key}{c}"), 1)

        def bias_rows(pc, key, bias):
            one, row = rowb(bias)
            nc.tensor.matmul(side[pc.bank[key]].rearrange("p (k d) -> p k d", k=RB), one,
                             row.unsqueeze(1).broadcast_to([1, RB, D]), start=True, stop=False,
                             skip_group_check=True)

        def project_rows(pe, pc, n, key, w, of):
            for c in range(DC):
                pe.wait_ge(pc.of(f"{of}{c}"), pc.upto(n, f"{of}{c}"))
                for k in range(RB):
                    ins = nc.tensor.matmul(side[pc.bank[key]][:, k * D:(k + 1) * D], hT[:, c, k * P:(k + 1) * P],
                                           w_att[w][:, c, :], start=False, stop=(c == DC - 1),
                                           skip_group_check=True)
            ins.then_inc(pc.next(key), 1)

        def project_channels(pe, pc, n, key, w):
            pe.wait_ge(pc.of("hc1"), pc.upto(n, "hc1"))
            for m in range(DC):
                for c in range(DC):
                    ins = nc.tensor.matmul(side[pc.bank[key]][:, m * S:(m + 1) * S],
                                           w_att[w][:, c, m * P:(m + 1) * P], hT[:, c, 0:S],
                                           start=(c == 0), stop=(c == DC - 1))
            ins.then_inc(pc.next(key), 1)

        def tail_scalar(act, pc, n, b):
            act.wait_ge(pc.of("h21"), pc.upto(n, "h21"))
            for c in range(DC):
                nc.scalar.activation(hT[:, c, 0:S], side[pc.bank["h2"]][:, c * S:(c + 1) * S], ACT.Silu,
                                     bias=cur[:, 1, c, b:b + 1], scale=cur[:, 0, c, b:b + 1])\
                  .then_inc(pc.next(f"hc2{c}"), 1)

        def attn_tensor(pe, b, g, prev):
            pc, n = at, 2 * g + b
            after(pe, prev)
            yield
            yield
            pe.wait_ge(pc.of("xh"), pc.upto(n, "xh"))
            transpose_rows(pc, "h")
            yield
            project_channels(pe, pc, n, "q", "a_q")
            project_channels(pe, pc, n, "k", "a_k")
            yield
            pe.wait_ge(pc.of("hc1"), pc.upto(n, "hc1"))
            bias_rows(pc, "v", "a_v_b")
            project_rows(pe, pc, n, "v", "a_v", "hc")
            yield
            for z in range(2):
                for p in range(z * HP, (z + 1) * HP):
                    if p == 0:
                        pe.wait_ge(pc.of("klo"), pc.upto(n, "klo"))
                    pe.wait_ge(pc.of(R_FREE[p]), pc.upto(n, R_FREE[p]))
                    bank = side[pc.bank[f"r{p}"]]
                    for w, src in enumerate((qhl, khl)):
                        for part in range(2):
                            ins = nc.tensor.matmul(bank[:, w * S:(w + 1) * S], stack[:, 2 * w + part, p % 4, :],
                                                   src[:, part, p // 4, :], start=(part == 0), stop=(part == 1))
                    ins.then_inc(pc.next(f"r{p}"), 1)
                    if p % 2:
                        yield
                pe.wait_ge(pc.of(f"rc{(z + 1) * HP - 2}"), pc.upto(n, f"rc{(z + 1) * HP - 2}"))
                pe.wait_ge(pc.of(f"rc{(z + 1) * HP - 1}"), pc.upto(n, f"rc{(z + 1) * HP - 1}"))
                for p in range(z * HP, (z + 1) * HP):
                    banks = [side[pc.bank[f"s{p}{hh}"]] for hh in range(2)]
                    for hh in range(2):
                        j = 2 * p + hh
                        if j - 4 * HP // 2 * z >= 3:
                            pe.wait_ge(pc.of(f"mx{(j - 3) // 2}{(j - 3) % 2}"), pc.upto(n, f"mx{(j - 3) // 2}{(j - 3) % 2}"))
                        nc.tensor.matmul(banks[hh].rearrange("p (h s) -> p h s", h=2),
                                         pick[:, 0:1].broadcast_to([P, P]),
                                         mb[:, :].unsqueeze(1).broadcast_to([P, 2, S]), start=True, stop=False,
                                         skip_group_check=True)
                    for t in range(RB):
                        for hh in range(2):
                            rr = slice(64 * hh, 64 * hh + 64)
                            ins = nc.tensor.matmul(banks[hh][:, t * S:(t + 1) * S],
                                                   qk[rr, p % HP, 0, t * P:(t + 1) * P],
                                                   qk[rr, p % HP, 1, :], start=False, stop=True, skip_group_check=True)
                            if t == RB - 1:
                                ins.then_inc(pc.next(f"s{p}{hh}"), 1)
                    if p % 2:
                        yield
                pe.wait_ge(pc.of(f"mx{(z + 1) * HP - 1}1"), pc.upto(n, f"mx{(z + 1) * HP - 1}1"))
                for t in range(RB):
                    ins = nc.tensor.transpose(side[pc.bank[f"nm{z}"]][0:2 * HP, t * P:(t + 1) * P],
                                              mx[:, t, z * 2 * HP:(z + 1) * 2 * HP], ident[:, :])
                ins.then_inc(pc.next(f"nm{z}"), 1)
                yield
                for p in range(z * HP, (z + 1) * HP + 1):
                    if p < (z + 1) * HP:
                        banks = [side[pc.bank[f"t{p}{hh}"]] for hh in range(2)]
                        for hh in range(2):
                            if p == z * HP and hh == 0:
                                pe.wait_ge(pc.of(f"nmlo{z}"), pc.upto(n, f"nmlo{z}"))
                            if p > z * HP:
                                pe.wait_ge(pc.of(f"x{p - 1}{hh}"), pc.upto(n, f"x{p - 1}{hh}"))
                            c0 = 2 * (p % HP) + hh
                            nc.tensor.matmul(banks[hh].rearrange("p (h s) -> p h s", h=2),
                                             pick[:, c0:c0 + 1].broadcast_to([P, P]),
                                             nm[:, :].unsqueeze(1).broadcast_to([P, 2, S]), start=True, stop=False,
                                             skip_group_check=True)
                        for t in range(RB):
                            for hh in range(2):
                                rr = slice(64 * hh, 64 * hh + 64)
                                ins = nc.tensor.matmul(banks[hh][:, t * S:(t + 1) * S],
                                                       qk[rr, p % HP, 1, t * P:(t + 1) * P], qk[rr, p % HP, 0, :],
                                                       start=False, stop=True, skip_group_check=True)
                                if t == RB - 1:
                                    ins.then_inc(pc.next(f"t{p}{hh}"), 1)
                    if p > z * HP:
                        j, last = (p - 1) // 2, p - 1
                        pe.wait_ge(pc.of(f"x{last}1"), pc.upto(n, f"x{last}1"))
                        if last % 4 == 2:
                            pe.wait_ge(pc.of(f"ye{j - 1}"), pc.upto(n, f"ye{j - 1}"))
                        for hh in range(2):
                            h = 2 * last + hh
                            q0 = 32 * (h % 4)
                            for t in range(RB):
                                ins = nc.tensor.matmul(side[2][q0:q0 + 32, 0:S], va[:, t, h, :],
                                                       pt[h % 4][:, t, :], start=(t == 0), stop=(t == 1))
                        ins.then_inc(pc.next(f"pv{last}"), 1)
                    yield
            for t in range(RB):
                if t == 0:
                    pe.wait_ge(pc.of("ye3"), pc.upto(n, "ye3"))
                for j in range(H // 4):
                    ins = nc.tensor.transpose(side[pc.bank[f"o{t}"]][:, j * P:(j + 1) * P],
                                              yT[:, j, t * P:(t + 1) * P], ident[:, :])
                ins.then_inc(pc.next(f"o{t}"), 1)
            yield
            yield from tail_tensor(pe, pc, n, "a_out", "a_out_b", ("ye3", "yn0"))

        def attn_scalar(act, b, g, prev):
            pc, n = at, 2 * g + b
            after(act, prev)
            loads_of_piece(act, "attn", b, g, prev)
            yield
            yield
            act.wait_ge(pc.of("h1"), pc.upto(n, "h1"))
            for c in range(DC):
                nc.scalar.activation(hT[:, c, 0:S], side[pc.bank["h"]][:, c * S:(c + 1) * S], ACT.Identity,
                                     bias=col("a_norm_b", c), scale=col("a_norm_w", c))\
                  .then_inc(pc.next(f"hc{c}"), 1)
            yield
            for key, dst, bias in (("q", qhl, "a_q_b"), ("k", khl, "a_k_b")):
                act.wait_ge(pc.of(key), pc.upto(n, key))
                for m in range(DC):
                    ins = nc.scalar.activation(dst[:, 0, m, :], side[pc.bank[key]][:, m * S:(m + 1) * S],
                                               ACT.Identity, bias=col(bias, m))
                ins.then_inc(pc.next(key + "hi"), 1)
            yield
            act.wait_ge(pc.of("v"), pc.upto(n, "v"))
            act.wait_ge(pc.of("mcur"), pc.upto(n, "mcur"))
            for k in range(RB):
                ins = nc.scalar.activation(va[:, k, :, 0:DH],
                                           side[pc.bank["v"]][:, k * D:(k + 1) * D].rearrange("p (h d) -> p h d", h=H),
                                           ACT.Copy, scale=mcur[:, 0, k:k + 1])
            ins.then_inc(pc.next("v_"), 1)
            yield
            for z in range(2):
                for p in range(z * HP, (z + 1) * HP):
                    act.wait_ge(pc.of(f"r{p}"), pc.upto(n, f"r{p}"))
                    nc.scalar.activation(qk[:, p % HP, :, :].rearrange("p w s -> p (w s)"),
                                         side[pc.bank[f"r{p}"]], ACT.Copy).then_inc(pc.next(f"rc{p}"), 1)
                    if p % 2:
                        yield
                yield
                yield
                act.wait_ge(pc.of(f"nm{z}"), pc.upto(n, f"nm{z}"))
                nc.scalar.activation(nm[0:2 * HP, :], side[pc.bank[f"nm{z}"]][0:2 * HP, 0:S], ACT.Copy,
                                               scale=-1.0).then_inc(pc.next(f"nmhi{z}"), 1)
                yield
                for p in range(z * HP, (z + 1) * HP + 1):
                    if p < (z + 1) * HP:
                        for hh in range(2):
                            act.wait_ge(pc.of(f"t{p}{hh}"), pc.upto(n, f"t{p}{hh}"))
                            if p == 0 and hh == 0:
                                act.wait_ge(pc.of("mbias"), pc.upto(n, "mbias"))
                                u_is_free(act, 0)
                            for t in range(RB):
                                ins = nc.scalar.activation(pt[(2 * p + hh) % 4][:, t, :],
                                                           side[pc.bank[f"t{p}{hh}"]][:, t * S:(t + 1) * S],
                                                           ACT.Exp, bias=mcur[:, 1, t:t + 1])
                            ins.then_inc(pc.next(f"x{p}{hh}"), 1)
                    if p > z * HP and p % 2 == 0:
                        j = p // 2 - 1
                        act.wait_ge(pc.of(f"pv{2 * j + 1}"), pc.upto(n, f"pv{2 * j + 1}"))
                        nc.scalar.activation(yT[:, j, :], side[2][:, 0:S], ACT.Copy).then_inc(pc.next(f"ye{j}"), 1)
                    yield
            yield
            tail_scalar(act, pc, n, b)
            yield
            yield

        def attn_vector(dve, b, g, prev):
            pc, n = at, 2 * g + b
            after(dve, prev)
            src = lambda r: x_b[:, RB * b + r, :]

            def copies():
                copy_coef(pc, "a", g)
                nc.vector.tensor_copy(mcur[:, 0, :],
                                                amask[:, bass.ds(n, 1), :].rearrange("p o k -> p (o k)")).then_inc(pc.next("mcur"), 1)

            ln_stats(dve, pc, n, src, RB, also=copies)
            dve.wait_ge(pc.of("mcur"), pc.upto(n, "mcur"))
            nc.vector.tensor_scalar(mcur[:, 1, :], mcur[:, 0, :], 1.0, 1e6, ALU.subtract, ALU.mult).then_inc(pc.next("mbias"), 1)
            yield
            ln_apply(dve, pc, n, src, RB)
            dve.wait_ge(min_, 16 * n + 16)
            nc.vector.tensor_scalar(mrow[:, :], mrow[:, :], 1.0, 1e6, ALU.subtract, ALU.mult).then_inc(pc.next("mval"), 1)
            dve.wait_ge(pc.of("mval"), pc.upto(n, "mval"))
            nc.vector.tensor_copy(mb[0:1, :], mrow[:, :]).then_inc(pc.next("mhi"), 1)
            dve.wait_ge(pc.of("mhi"), pc.upto(n, "mhi"))
            nc.vector.tensor_tensor(mb[32:33, :], mrow[:, :], mb[0:1, :], ALU.subtract).then_inc(pc.next("mlo"), 1)
            yield
            yield
            for key, dst, bias in (("q", qhl, "a_q_b"), ("k", khl, "a_k_b")):
                dve.wait_ge(pc.of(key + "hi"), pc.upto(n, key + "hi"))
                for m in range(DC):
                    ins = nc.vector.scalar_tensor_tensor(
                        out=dst[:, 1, m, :], in0=side[pc.bank[key]][:, m * S:(m + 1) * S], scalar=col(bias, m),
                        in1=dst[:, 0, m, :], op0=ALU.add, op1=ALU.subtract)
                ins.then_inc(pc.next(key + "lo"), 1)
            yield
            yield
            for z in range(2):
                yield
                yield
                for p in range(z * HP, (z + 1) * HP):
                    for hh in range(2):
                        dve.wait_ge(pc.of(f"s{p}{hh}"), pc.upto(n, f"s{p}{hh}"))
                        nc.vector.tensor_reduce(
                            mx[:, :, 2 * p + hh], side[pc.bank[f"s{p}{hh}"]].rearrange("p (t s) -> p t s", t=RB), X,
                            ALU.max).then_inc(pc.next(f"mx{p}{hh}"), 1)
                    if p % 2:
                        yield
                dve.wait_ge(pc.of(f"nmhi{z}"), pc.upto(n, f"nmhi{z}"))
                nc.vector.scalar_tensor_tensor(
                    out=nm[32:32 + 2 * HP, :], in0=side[pc.bank[f"nm{z}"]][0:2 * HP, 0:S], scalar=-1.0,
                    in1=nm[0:2 * HP, :], op0=ALU.mult, op1=ALU.subtract).then_inc(pc.next(f"nmlo{z}"), 1)
                yield
                for p in range(z * HP, (z + 1) * HP + 1):
                    yield
            for t in range(RB):
                bank = side[pc.bank[f"o{t}"]].rearrange("p (h d) -> p h d", h=H)
                dve.wait_ge(pc.of(f"o{t}"), pc.upto(n, f"o{t}"))
                nc.vector.reciprocal(rec[:, 0, t, :], bank[:, :, DH]).then_inc(pc.next(f"rec{t}"), 1)
                dve.wait_ge(pc.of(f"rec{t}"), pc.upto(n, f"rec{t}"))
                nc.vector.tensor_tensor(
                    xhat[:, RB + t, :].rearrange("p (h d) -> p h d", h=H), bank[:, :, 0:DH],
                    rec[:, 0, t, :].unsqueeze(2).broadcast_to([P, H, DH]), ALU.mult).then_inc(pc.next(f"yn{t}"), 1)
            dve.wait_ge(pc.of("yn1"), pc.upto(n, "yn1"))
            ln_stats(dve, pc, n, lambda r: xhat[:, RB + r, :], RB, "2")
            yield
            ln_apply(dve, pc, n, lambda r: xhat[:, RB + r, :], RB, "2")
            yield
            dve.wait_ge(pc.of("out"), pc.upto(n, "out"))
            nc.vector.tensor_tensor(
                x_b[:, RB * b:RB * (b + 1), :], side[pc.bank["out"]].rearrange("p (r d) -> p r d", r=RB),
                x_b[:, RB * b:RB * (b + 1), :], ALU.add).then_inc(pc.next("xo"), 1)
            yield

        def attn_pool(pool, b, g, prev):
            pc, n = at, 2 * g + b
            after(pool, prev)
            yield
            ln_rstd(pool, pc, n, RB)
            for _ in range(ATTN_PH - 4):
                yield
            ln_rstd(pool, pc, n, RB, "2")
            yield

        def lin_tensor(pe, b, g, prev):
            pc, n = li, 2 * g + b
            after(pe, prev)
            yield
            yield
            pe.wait_ge(pc.of("xh"), pc.upto(n, "xh"))
            transpose_rows(pc, "h")
            yield
            bias_rows(pc, "q", "l_q_b")
            project_rows(pe, pc, n, "q", "l_q", "hc")
            project_channels(pe, pc, n, "k", "l_k")
            yield
            pe.wait_ge(pc.of("hc1"), pc.upto(n, "hc1"))
            bias_rows(pc, "v", "l_v_b")
            project_rows(pe, pc, n, "v", "l_v", "hc")
            yield
            pe.wait_ge(pc.of("qn"), pc.upto(n, "qn"))
            for c in range(DC):
                for k in range(RB):
                    ins = nc.tensor.transpose(side[pc.bank["qt"]][:, c * S + k * P:c * S + (k + 1) * P],
                                              qrow[:, k, c * P:(c + 1) * P], ident[:, :])
            ins.then_inc(pc.next("qt"), 1)
            pe.wait_ge(pc.of("kn1"), pc.upto(n, "kn1"))
            for k in range(RB):
                for c in range(DC):
                    ins = nc.tensor.transpose(side[pc.bank["kt"]][:, k * D + c * P:k * D + (c + 1) * P],
                                              kT[:, c, k * P:(k + 1) * P], ident[:, :])
            ins.then_inc(pc.next("kt"), 1)
            yield
            pe.wait_ge(pc.of("ktc"), pc.upto(n, "ktc"))
            for c in range(DC):
                for k in range(RB):
                    ins = nc.tensor.matmul(side[pc.bank["at"]][:, c * P:(c + 1) * P],
                                           vrow[:, k, c * P:(c + 1) * P], krow[:, k, c * P:(c + 1) * P],
                                           start=(k == 0), stop=(k == RB - 1))
            ins.then_inc(pc.next("at"), 1)
            pe.wait_ge(pc.of("atm"), pc.upto(n, "atm"))
            for k in range(RB):
                for c in range(DC):
                    ins = nc.tensor.matmul(side[pc.bank["y"]][:, k * D + c * P:k * D + (c + 1) * P],
                                           qT[:, c, k * P:(k + 1) * P], attnT[:, c, :], start=True, stop=True)
            ins.then_inc(pc.next("y"), 1)
            yield
            yield from tail_tensor(pe, pc, n, "l_out", "l_out_b", ("ktc", "atm"))

        def lin_scalar(act, b, g, prev):
            pc, n = li, 2 * g + b
            after(act, prev)
            loads_of_piece(act, "lin", b, g, prev)
            yield
            yield
            act.wait_ge(pc.of("h1"), pc.upto(n, "h1"))
            for c in range(DC):
                nc.scalar.activation(hT[:, c, 0:S], side[pc.bank["h"]][:, c * S:(c + 1) * S], ACT.Identity,
                                     bias=col("l_norm_b", c), scale=col("l_norm_w", c))\
                  .then_inc(pc.next(f"hc{c}"), 1)
            yield
            act.wait_ge(pc.of("qs"), pc.upto(n, "qs"))
            nc.scalar.activation(qrow, qrow, ACT.Exp).then_inc(pc.next("qe"), 1)
            yield
            act.wait_ge(pc.of("v"), pc.upto(n, "v"))
            act.wait_ge(pc.of("nmask"), pc.upto(n, "nmask"))
            for k in range(RB):
                ins = nc.scalar.activation(vrow[:, k, :], side[pc.bank["v"]][:, k * D:(k + 1) * D], ACT.Copy,
                                           scale=mcur[:, 0, k:k + 1])
            ins.then_inc(pc.next("v_"), 1)
            act.wait_ge(pc.of("km"), pc.upto(n, "km"))
            for c in range(DC):
                nc.scalar.activation(kT[:, c, :], kT[:, c, :], ACT.Exp, bias=small[:, c:c + 1],
                                               accum_out=small[:, 2 + c:3 + c]).then_inc(pc.next(f"ke{c}"), 1)
            yield
            act.wait_ge(pc.of("qt"), pc.upto(n, "qt"))
            nc.scalar.activation(qT.rearrange("p c s -> p (c s)"), side[pc.bank["qt"]], ACT.Copy).then_inc(pc.next("qtc"), 1)
            act.wait_ge(pc.of("kt"), pc.upto(n, "kt"))
            nc.scalar.activation(krow.rearrange("p c s -> p (c s)"), side[pc.bank["kt"]], ACT.Copy).then_inc(pc.next("ktc"), 1)
            yield
            yield
            tail_scalar(act, pc, n, b)
            yield
            yield

        def lin_vector(dve, b, g, prev):
            pc, n = li, 2 * g + b
            after(dve, prev)
            src = lambda r: x_c[:, RB * b + r, :]

            def copies():
                copy_coef(pc, "l", g)
                nc.vector.tensor_copy(mcur[:, 1, :],
                                                kmask_col[:, bass.ds(n, 1), :].rearrange("p o k -> p (o k)")).then_inc(pc.next("kcur"), 1)

            ln_stats(dve, pc, n, src, RB, also=copies)
            dve.wait_ge(kmin, 16 * n + 16)
            nc.vector.tensor_scalar(kmb, kmrow[:, :], 1.0, -1e30, ALU.is_equal, ALU.mult).then_inc(pc.next("kmask"), 1)
            dve.wait_ge(pc.of("kcur"), pc.upto(n, "kcur"))
            nc.vector.tensor_scalar(mcur[:, 0, :], mcur[:, 1, :], 1.0, -1.0, ALU.is_equal, ALU.mult).then_inc(pc.next("masked"), 1)
            dve.wait_ge(pc.of("masked"), pc.upto(n, "masked"))
            nc.vector.tensor_scalar(mcur[:, 0, :], mcur[:, 0, :], 1.0, None, ALU.add).then_inc(pc.next("nmask"), 1)
            yield
            ln_apply(dve, pc, n, src, RB)
            yield
            yield
            dve.wait_ge(pc.of("q"), pc.upto(n, "q"))
            q3 = side[pc.bank["q"]].rearrange("p (h d) -> p h d", d=DH)
            qm = qmx.rearrange("p r h -> p (r h)")
            qr = qrs.rearrange("p r h -> p (r h)")
            qrow3 = qrow.rearrange("p r (h d) -> p (r h) d", d=DH)
            nc.vector.tensor_reduce(qm, q3, X, ALU.max).then_inc(pc.next("qm"), 1)
            dve.wait_ge(pc.of("qm"), pc.upto(n, "qm"))
            u_is_free(dve, 0)
            nc.vector.tensor_tensor(qrow3, q3, qm.unsqueeze(2).broadcast_to([P, RB * H, DH]), ALU.subtract).then_inc(pc.next("qs"), 1)
            dve.wait_ge(pc.of("k"), pc.upto(n, "k"))
            dve.wait_ge(pc.of("kmask"), pc.upto(n, "kmask"))
            for c in range(DC):
                nc.vector.scalar_tensor_tensor(
                    out=kT[:, c, :], in0=side[pc.bank["k"]][:, c * S:(c + 1) * S], scalar=col("l_k_b", c),
                    in1=kmb, op0=ALU.add, op1=ALU.add).then_inc(pc.next(f"kb{c}"), 1)
            dve.wait_ge(pc.of("kb1"), pc.upto(n, "kb1"))
            nc.vector.tensor_reduce(small[:, 0:2], kT, X, ALU.max, negate=True).then_inc(pc.next("km"), 1)
            yield
            dve.wait_ge(pc.of("qe"), pc.upto(n, "qe"))
            nc.vector.tensor_reduce(qr, qrow3, X, ALU.add).then_inc(pc.next("qsum"), 1)
            dve.wait_ge(pc.of("qsum"), pc.upto(n, "qsum"))
            nc.vector.reciprocal(qr, qr).then_inc(pc.next("qrec"), 1)
            dve.wait_ge(pc.of("qrec"), pc.upto(n, "qrec"))
            nc.vector.tensor_tensor(qrow3, qrow3, qr.unsqueeze(2).broadcast_to([P, RB * H, DH]), ALU.mult).then_inc(pc.next("qn"), 1)
            dve.wait_ge(pc.of("ke1"), pc.upto(n, "ke1"))
            nc.vector.reciprocal(small[:, 4:6], small[:, 2:4]).then_inc(pc.next("krec"), 1)
            dve.wait_ge(pc.of("krec"), pc.upto(n, "krec"))
            for c in range(DC):
                nc.vector.tensor_scalar(kT[:, c, :], kT[:, c, :], small[:, 4 + c:5 + c], None, ALU.mult).then_inc(pc.next(f"kn{c}"), 1)
            yield
            yield
            dve.wait_ge(pc.of("at"), pc.upto(n, "at"))
            nc.vector.tensor_tensor(
                attnT, side[pc.bank["at"]][:, 0:DC * P].rearrange("p (c e) -> p c e", c=DC),
                blocks[:, :].unsqueeze(1).broadcast_to([P, DC, P]), ALU.mult).then_inc(pc.next("atm"), 1)
            dve.wait_ge(pc.of("y"), pc.upto(n, "y"))
            ysrc = lambda r: side[pc.bank["y"]][:, r * D:(r + 1) * D]
            ln_stats(dve, pc, n, ysrc, RB, "2")
            yield
            ln_apply(dve, pc, n, ysrc, RB, "2")
            yield
            dve.wait_ge(pc.of("out"), pc.upto(n, "out"))
            nc.vector.tensor_tensor(
                x_c[:, RB * b:RB * (b + 1), :], side[pc.bank["out"]].rearrange("p (r d) -> p r d", r=RB),
                x_c[:, RB * b:RB * (b + 1), :], ALU.add).then_inc(pc.next("xo"), 1)
            yield

        def lin_pool(pool, b, g, prev):
            pc, n = li, 2 * g + b
            after(pool, prev)
            yield
            ln_rstd(pool, pc, n, RB)
            for _ in range(LIN_PH - 3):
                yield
            ln_rstd(pool, pc, n, RB, "2")
            yield

        ENG = {
            "pe": dict(keep=nothing, rest=rest_tensor, front=front_tensor, back=back_tensor, attn=attn_tensor, lin=lin_tensor, scan=scan_tensor),
            "act": dict(keep=keep_scalar, rest=rest_scalar, front=front_scalar, back=back_scalar, attn=attn_scalar, lin=lin_scalar, scan=scan_scalar),
            "dve": dict(keep=nothing, rest=rest_vector, front=front_vector, back=back_vector, attn=attn_vector, lin=lin_vector, scan=scan_vector),
            "pool": dict(keep=nothing, rest=rest_pool, front=front_pool, back=nothing, attn=attn_pool, lin=lin_pool, scan=scan_pool),
        }
        END = 10 ** 6
        VARIANT = {"keep": ("keep", 0), "rest0": ("rest", 0), "rest1": ("rest", 1), "front0": ("front", 0), "front1": ("front", 1), "back0": ("back", 0), "back1": ("back", 1),
                   "attn_a": ("attn", 0), "attn_b": ("attn", 1), "lin_a": ("lin", 0), "lin_b": ("lin", 1)}

        def iteration(eng, e, i):
            for seg in range(2):
                pieces = [(k, name, i + off) for k, (name, off, where) in enumerate(SIDE)
                          if where == seg]
                total = sum(sum(WEIGHT[name]) for _, name, _ in pieces)
                scan_name, off = SCAN[seg]
                scanning = alive(i, off)
                follows = alive(i, SCAN[0][1]) if seg else not isinstance(i, int) or (i > FIRST_IT and alive(i - 1, SCAN[1][1]))
                busy["scan"] = (scan_name, i + off) if scanning else None
                scan, at_scan = iter(()), END
                if scanning and ENG[e]["scan"]:
                    scan = ENG[e]["scan"](eng, seg, i + off, before_scan(i, seg), follows)
                    at_scan = next(scan)
                elif follows and e == "pe":
                    last_pair(eng, 1 - seg, before_scan(i, seg)[1])
                elif follows and e == "dve":
                    gated(eng, 1 - seg, before_scan(i, seg)[1], 1)
                done = 0.0
                for k, name, g in pieces:
                    if not alive(g, 0):
                        done += sum(WEIGHT[name])
                        continue
                    kind, variant = VARIANT[name]
                    run = ENG[e][kind](eng, variant, g, before_side(i, k))
                    for w in WEIGHT[name]:
                        at_side = done / total * STEPS + LAG[e]
                        while at_scan <= at_side:
                            at_scan = next(scan, END)
                        next(run, None)
                        done += w
                    for _ in run:
                        pass
                for _ in scan:
                    pass

        def all_iterations(eng, e):
            for i in range(FIRST_IT, LOOP_FROM):
                iteration(eng, e, i)
            with eng.Fori(LOOP_FROM, LOOP_TO) as i:
                iteration(eng, e, i)
            for i in range(LOOP_TO, LAST_IT + 1):
                iteration(eng, e, i)

        POOL_READY, ACT_READY, DVE_READY = 4, 3, 9
        block = ctx.enter_context(nc.Block())

        @block.sync
        def _(sp):
            n = 0
            loads = [(c_raw, a["c_t"].rearrange("(k p) b -> p k b", p=P)), (cols[:, :], a["cols"]),
                     ] + [(rowb(name)[1], a["rows"][k:k + 1, :]) for k, name in enumerate(ROWS)]
            for k in range(5):
                loads.append((w_mod[k][:, :, :], a["w_mod"][:, k * 512:(k + 1) * 512].rearrange("(k p) n -> p k n", p=P)))
            for k in range(3):
                w = 1024 if k < 2 else 512
                loads.append((mod_bias[k].rearrange("p a b -> p (a b)")[0:B, 0:w],
                              a["b_mod"][:, k * 1024:k * 1024 + w].broadcast_to([B, w])))
            loads.append((idx_i[:, :], a["idx"].broadcast_to([P, S])))
            for l in range(2):
                loads += [(w_in[l][:, :, :], a[f"w_in{l}"].rearrange("(k p) n -> p k n", p=P)),
                          (w_xp[l][:, :, :], a[f"w_xp{l}"].rearrange("(k p) n -> p k n", p=P)),
                          (w_dt[l * DTR:(l + 1) * DTR, :], a[f"w_dt{l}"]),
                          (w_out[l][:, :, :], a[f"w_out{l}"].rearrange("(k p) n -> p k n", p=P))]
            for w in w_att:
                loads.append((w_att[w][:, :, :], a[f"w_{w}"].rearrange("(k p) n -> p k n", p=P)))
            loads += [(amask[:, :, :], a["amask_col"]), (kmask_col[:, :, :], a["kmask_col"])]
            for dst, src in loads:
                sp.dma_start(dst, src).then_inc(loaded, 16)
                n += 16
            total_loads.append(n)
            sp.wait_ge(p_dve, 5)
            for l in range(2):
                src = (mod_rows if l == 0 else mod_rows2)[:, :, :].rearrange("p a b -> p (a b)")
                at0 = GATE_AT[f"m{l}"] - 1024 * l
                sp.dma_start(gates_dram[l], src[0:B, at0:at0 + D]).then_inc(gates_out, 16)
            sp.wait_ge(gates_out, 32)
            sp.wait_ge(stored, 16 * GB * NG)

        @block.gpsimd
        def _(pool):
            k = [0]

            def step(ins):
                k[0] += 1
                ins.then_inc(p_pool, 1)
                pool.wait_ge(p_pool, k[0])

            step(nc.gpsimd.memset(ident[:, :], 0.0))
            step(nc.gpsimd.affine_select(out=ident[:, :], in_=ident[:, :], compare_op=ALU.not_equal, fill=1.0,
                                         base=0, pattern=[[-1, P]], channel_multiplier=1))
            step(nc.gpsimd.memset(pick_f, 0.0))
            for off in (0, 32):
                step(nc.gpsimd.affine_select(out=pick_f, in_=pick_f, compare_op=ALU.not_equal, fill=1.0,
                                             base=-off, pattern=[[-1, 2 * NS]], channel_multiplier=1))
            for v, parts in enumerate(((0, 1), (2, 3), (0, 2), (1, 3))):
                tile = (stack_f if v < 2 else stack_g)[:, (v % 2) * 512:(v % 2) * 512 + 512]
                step(nc.gpsimd.memset(tile, 0.0))
                for part in parts:
                    sub = tile.rearrange("p (a h r l) -> p a h r l", a=4, h=2, r=4)[:, :, :, part, :]
                    step(nc.gpsimd.affine_select(out=sub, in_=sub, compare_op=ALU.not_equal, fill=1.0, base=0,
                                                 pattern=[[-32, 4], [-16, 2], [-1, 16]], channel_multiplier=1))
            step(nc.gpsimd.memset(blocks[:, :], 1.0))
            bl = blocks[:, :].rearrange("p (h d) -> p h d", d=DH)
            step(nc.gpsimd.affine_select(out=bl, in_=bl, compare_op=ALU.is_ge, fill=0.0, base=0,
                                         pattern=[[-DH, P // DH], [0, DH]], channel_multiplier=1))
            step(nc.gpsimd.affine_select(out=bl, in_=bl, compare_op=ALU.is_ge, fill=0.0, base=DH - 1,
                                         pattern=[[DH, P // DH], [0, DH]], channel_multiplier=-1))
            step(nc.gpsimd.iota(iot_i[:, :], [[P, RB]], base=0, channel_multiplier=1))
            step(nc.gpsimd.memset(nhalf[:, :], -0.5))
            step(nc.gpsimd.memset(eps[:, :], EPS))
            step(nc.gpsimd.memset(ones[:, :], 1.0))
            step(nc.gpsimd.memset(one_col[:, :], 1.0))
            step(nc.gpsimd.memset(va[:, :, :, :], 0.0))
            step(nc.gpsimd.memset(va[:, :, :, DH:DH + 1], 1.0))
            pool_steps.append(k[0])
            pool.wait_ge(p_dve, DVE_READY)
            all_iterations(pool, "pool")

        @block.scalar
        def _(act):
            act.wait_ge(loaded, total_loads[0])
            nc.scalar.activation(c_act, c_raw, ACT.Silu).then_inc(p_act, 1)
            for l in range(2):
                nc.scalar.activation(a_neg[:, l, :], col(f"m{l}_A_log", 0, IC * NS), ACT.Exp).then_inc(p_act, 1)
            act.wait_ge(p_dve, DVE_READY)
            act.wait_ge(gates_out, 32)
            all_iterations(act, "act")
            for e, v in li.events.items():
                act.wait_ge(li.sem[e], GB * NG * len(v))
            store_result(act, NG - 1, 1)

        @block.tensor
        def _(pe):
            pe.wait_ge(p_act, 1)
            for k in range(5):
                if k >= 3:
                    pe.wait_ge(p_dve, k - 2)
                for c in range(4):
                    ins = nc.tensor.matmul(side[k % 3][0:B, :], c_act[:, c, :], w_mod[k][:, c, :],
                                           start=(c == 0), stop=(c == 3))
                ins.then_inc(p_pe, 1)
            pe.wait_ge(p_dve, 5)
            pe.wait_ge(p_pool, pool_steps[0])
            for s, site in enumerate(SITES):
                for w, off in enumerate((SCALE_AT[site], SHIFT_AT[site])):
                    for c in range(DC):
                        src = off + c * P
                        tile = (mod_rows, mod_rows2, mod_rows3)[src // 1024][:, :, :].rearrange("p a b -> p (a b)")
                        j = (s * 2 + w) * DC + c
                        ins = nc.tensor.transpose(side[2][:, j * B:(j + 1) * B], tile[0:B, src % 1024:src % 1024 + P],
                                                  ident[0:B, 0:B])
            ins.then_inc(p_pe, 1)
            pe.wait_ge(p_dve, DVE_READY)
            all_iterations(pe, "pe")

        @block.vector
        def _(dve):
            dve.wait_ge(loaded, total_loads[0])
            for k in range(5):
                dve.wait_ge(p_pe, k + 1)
                tile = (mod_rows, mod_rows2, mod_rows3)[k // 2]
                nc.vector.tensor_tensor(tile[0:B, k % 2, :], side[k % 3][0:B, :], mod_bias[k // 2][0:B, k % 2, :],
                                        ALU.add).then_inc(p_dve, 1)
            dve.wait_ge(p_pe, 6)
            nc.vector.tensor_copy(modT, side[2].rearrange("p (k b) -> p k b", b=B)).then_inc(p_dve, 1)
            dve.wait_ge(p_dve, 6)
            for s in range(len(SITES)):
                sc_ = modT[:, 2 * DC * s:2 * DC * s + DC, :]
                ins = nc.vector.tensor_scalar(sc_, sc_, 1.0, None, ALU.add)
            ins.then_inc(p_dve, 1)
            dve.wait_ge(p_dve, 7)
            norm = {"m0": ("m0_ln_g", "m0_ln_b"), "a": ("a_sb_w", "a_sb_b"), "m1": ("m1_ln_g", "m1_ln_b"),
                    "l": ("l_sb_w", "l_sb_b")}
            for s, site in enumerate(SITES):
                for c in range(DC):
                    j = 2 * DC * s + c
                    nc.vector.tensor_scalar(coef[:, j, :], modT[:, j, :], col(norm[site][0], c), None, ALU.mult)
                    nc.vector.scalar_tensor_tensor(out=coef[:, j + DC, :], in0=modT[:, j, :],
                                                   scalar=col(norm[site][1], c), in1=modT[:, j + DC, :],
                                                   op0=ALU.mult, op1=ALU.add)
            dve.wait_ge(p_pool, pool_steps[0])
            dve.wait_ge(p_act, 3)
            nc.vector.tensor_scalar(a_neg[:, :, :], a_neg[:, :, :], -1.0, None, ALU.mult)
            for l in range(2):
                for c in range(IC):
                    nc.vector.tensor_scalar(diag_d[:, l, c, :], ident[:, :], col(f"m{l}_D", c), None, ALU.mult)
            nc.vector.tensor_copy(pick[:, :], pick_f)
            for v in range(4):
                nc.vector.tensor_copy(stack[:, v, :, :].rearrange("p a b -> p (a b)"),
                                      (stack_f if v < 2 else stack_g)[:, (v % 2) * 512:(v % 2) * 512 + 512])
            nc.vector.tensor_copy(idx_f, idx_i[:, :])
            nc.vector.tensor_copy(iot_f[:, :], iot_i[:, :])
            for l in range(2):
                nc.vector.memset(bcr[l][:, :].bitcast(F32), 0.0)
            nc.vector.memset(nm[:, :].bitcast(F32), 0.0)
            nc.vector.memset(mb[:, :].bitcast(F32), 0.0).then_inc(p_dve, 1)
            dve.wait_ge(p_dve, 8)
            for k in range(RB):
                nc.vector.tensor_scalar(onehot[:, k, :], idx_f, iot_f[:, k:k + 1], None, ALU.is_equal)
            for k in range(AHEAD + 1):
                nc.vector.memset(da[k][:, :, :, 0:1], 0.0)
            nc.vector.memset(small[:, :], 0.0).then_inc(p_dve, 1)
            dve.wait_ge(p_dve, DVE_READY)
            all_iterations(dve, "dve")


total_loads, pool_steps = [], []


def kernel(**inputs):
    import concourse.bacc as _bacc
    from concourse.bass_utils import run_bass_kernel_spmd as _run

    v = {k: np.asarray(x) for k, x in inputs.items()}
    c = np.ascontiguousarray

    def chunks(x):
        x = x.reshape(x.shape[0] // P, P, -1)
        return x.transpose(1, 0, 2).reshape(P, -1)

    L = {"m0": "L0_cond_", "m1": "L2_cond_"}
    names = {"m0": dict(conv_w="conv_w", conv_b="conv_b", b_dt="b_dt", D="D_param", A_log="A_log", ln_g="gamma",
                        ln_b="beta"),
             "m1": dict(conv_w="conv_w", conv_b="conv_b", b_dt="dt_proj_b", D="D_param", A_log="A_log", ln_g="ln_g",
                        ln_b="ln_b")}
    vec = {f"{m}_{k}": v[L[m] + s] for m in L for k, s in names[m].items()}
    vec |= {"a_norm_w": v["L1_cond_norm_w"], "a_norm_b": v["L1_cond_norm_b"], "a_q_b": v["L1_cond_q_b"],
            "a_k_b": v["L1_cond_k_b"], "a_sb_w": v["L1_cond_sb_norm_w"], "a_sb_b": v["L1_cond_sb_norm_b"],
            "l_norm_w": v["L3_cond_norm_scale"], "l_norm_b": v["L3_cond_norm_bias"], "l_k_b": v["L3_cond_bk"],
            "l_sb_w": v["L3_cond_film_norm_scale"], "l_sb_b": v["L3_cond_film_norm_bias"]}
    arrays = {
        "x": c(v["x"]),
        "c_t": c(v["cond_2048"].T),
        "idx": c(v["itok_S_0_1023"].reshape(1, S)),
        "amask_row": c(v["mask_BxS_ff1"]),
        "amask_col": c(v["mask_BxS_ff1"].reshape(B, RB, P).transpose(2, 0, 1)),
        "kmask_row": c(v["mask_BxS_ik0"]),
        "kmask_col": c(v["mask_BxS_ik0"].reshape(B, RB, P).transpose(2, 0, 1)),
        "cols": c(np.concatenate([chunks(vec[n]) for n in COLS], axis=1)),
        "rows": c(np.stack([v["L1_cond_v_b"], v["L1_cond_out_b"], v["L3_cond_bq"], v["L3_cond_bv"],
                            v["L3_cond_film_out_b"]])),
        "w_mod": c(np.concatenate([v["L0_cond_W_ada"], v["L1_cond_emb_w"], v["L2_cond_ada_w"].T,
                                   v["L3_cond_film_emb_W"]], axis=1)),
        "b_mod": c(np.concatenate([v["L0_cond_b_ada"], v["L1_cond_emb_b"], v["L2_cond_ada_b"],
                                   v["L3_cond_film_emb_b"]])[None]),
        "w_in0": c(v["L0_cond_W_in"]), "w_in1": c(v["L2_cond_in_proj_w"].T),
        "w_xp0": c(v["L0_cond_W_xp"]), "w_xp1": c(v["L2_cond_x_proj_w"].T),
        "w_dt0": c(v["L0_cond_W_dt"]), "w_dt1": c(v["L2_cond_dt_proj_w"].T),
        "w_out0": c(v["L0_cond_W_out"]), "w_out1": c(v["L2_cond_out_proj_w"].T),
        "w_a_q": c(v["L1_cond_q_w"]), "w_a_k": c(v["L1_cond_k_w"]), "w_a_v": c(v["L1_cond_v_w"]),
        "w_a_out": c(v["L1_cond_out_w"]), "w_l_q": c(v["L3_cond_Wq"]), "w_l_k": c(v["L3_cond_Wk"]),
        "w_l_v": c(v["L3_cond_Wv"]), "w_l_out": c(v["L3_cond_film_out_W"]),
    }
    nc = _bacc.Bacc("TRN2", target_bir_lowering=False, num_devices=1)
    aps = {n: nc.dram_tensor(f"in_{n}", x.shape, mybir.dt.from_np(x.dtype), kind="ExternalInput").ap()
           for n, x in arrays.items()}
    out = nc.dram_tensor("out_0", (B, S, D), F32, kind="ExternalOutput").ap()
    total_loads.clear()
    pool_steps.clear()
    build(nc, aps, out)
    r = _run(nc, [{f"in_{n}": x for n, x in arrays.items()}], core_ids=[0])
    return r.results[0]["out_0"]
```
